# Optimizing a Trainium2 kernel written in Bass

```python
import numpy as np
import jax
import jax.numpy as jnp

def _softmax(x, axis=-1):
    return jax.nn.softmax(x, axis=axis)

def _gelu(x):
    return jax.nn.gelu(x, approximate=True)

def _silu(x):
    return jax.nn.silu(x)

def _sigmoid(x):
    return jax.nn.sigmoid(x)

def _layernorm(x, axis=-1, eps=1e-05):
    m = jnp.mean(x, axis=axis, keepdims=True)
    v = jnp.var(x, axis=axis, keepdims=True)
    return (x - m) / jnp.sqrt(v + eps)

def _scatter_add(tgt, idx, src, axis=0):
    return tgt.at[idx].add(src)

def _segment_sum(src, seg, n):
    return jax.ops.segment_sum(src, seg, n)
kernel_name = 'mk_xattn_seq_d4_seqx_r4_91bc09'

def setup_inputs(seed: int=0):
    np.random.seed(seed)
    _w = jnp.asarray

    def _rec_inputs():
        import jax
        import jax.numpy as jnp
        _rk = jax.random.key(seed)
        x = -0.0005207 + 1.001 * jax.random.normal(jax.random.fold_in(_rk, 1), (8, 112, 512), jnp.float32)
        _lenS = 112 - jax.random.randint(jax.random.fold_in(_rk, 7), (8,), 0, max(1, 112 // 4) + 1, jnp.int32)
        _lenS2 = 375 - jax.random.randint(jax.random.fold_in(_rk, 8), (8,), 0, max(1, 375 // 4) + 1, jnp.int32)
        _ctx_2048P = jax.random.normal(jax.random.fold_in(_rk, 11), (8, 16, 512), jnp.float32)
        _ctx_2048c = jax.random.dirichlet(jax.random.fold_in(_rk, 511), 0.3 * jnp.ones((16,), jnp.float32), (8, 375))
        _ctx_2048t = jnp.einsum('bsk,bkd->bsd', _ctx_2048c, _ctx_2048P)
        _ctx_2048t = _ctx_2048t * jax.lax.rsqrt(jnp.mean(jnp.square(_ctx_2048t)) + 1e-12) * 0.953939
        ctx_2048 = 2.81802e-05 + 1.00001 * (_ctx_2048t + 0.3 * jax.random.normal(jax.random.fold_in(_rk, 611), (8, 375, 512), jnp.float32))
        _validS = jnp.arange(112)[None, :] < _lenS[:, None]
        _validS2 = jnp.arange(375)[None, :] < _lenS2[:, None]
        _causal = jnp.tril(jnp.ones((112, 112), dtype=bool))
        mask_BxS2_ik0 = jnp.where(jnp.broadcast_to(_validS2[:, :], (8, 375)), 0, 1).astype(jnp.int32)
        mask_Bx1xSxS2_ff0 = jnp.where(jnp.ones((8, 1, 112, 375), dtype=bool), 0.0, -1000000000.0).astype(jnp.float32)
        return (x, ctx_2048, mask_BxS2_ik0, mask_Bx1xSxS2_ff0)
    x, ctx_2048, mask_BxS2_ik0, mask_Bx1xSxS2_ff0 = _rec_inputs()

    def _L0_xattn_setup():
        import jax, jax.numpy as jnp
        import numpy as np
        B, Q, S1, S2 = (4, 64, 512, 512)
        D, H, K, F = (512, 16, 128, 2048)
        LN_EPS = 1e-05

        def _layer_norm(x, scale, offset):
            mu = jnp.mean(x, axis=-1, keepdims=True)
            var = jnp.var(x, axis=-1, keepdims=True)
            return (x - mu) * jax.lax.rsqrt(var + LN_EPS) * scale + offset

        def _cross_attention(q_in, kv_in, wq, bq, wk, bk, wv, bv, wo, bo, bias_k, bias_v):
            b, q_len, _ = q_in.shape
            t = kv_in.shape[1]
            qh = (q_in @ wq + bq).reshape(b, q_len, H, K)
            kh = (kv_in @ wk + bk).reshape(b, t, H, K)
            vh = (kv_in @ wv + bv).reshape(b, t, H, K)
            kh = jnp.concatenate([kh, jnp.broadcast_to(bias_k, (b, 1, H, K))], axis=1)
            vh = jnp.concatenate([vh, jnp.broadcast_to(bias_v, (b, 1, H, K))], axis=1)
            scale = jnp.sqrt(jnp.asarray(K, q_in.dtype))
            logits = jnp.einsum('bqhk,bthk->bhqt', qh, kh) / scale
            weights = jax.nn.softmax(logits, axis=-1)
            ctx = jnp.einsum('bhqt,bthk->bqhk', weights, vh).reshape(b, q_len, H * K)
            return ctx @ wo + bo

        def _forward(x, xf_1, xf_2, ln1_scale, ln1_offset, wq1, bq1, wk1, bk1, wv1, bv1, wo1, bo1, bias_k1, bias_v1, ln2_scale, ln2_offset, wq2, bq2, wk2, bk2, wv2, bv2, wo2, bo2, bias_k2, bias_v2, ln_mlp_scale, ln_mlp_offset, w_fc1, b_fc1, w_fc2, b_fc2):
            res = x
            h = _layer_norm(x, ln1_scale, ln1_offset)
            x = res + _cross_attention(h, xf_1, wq1, bq1, wk1, bk1, wv1, bv1, wo1, bo1, bias_k1, bias_v1)
            res = x
            h = _layer_norm(x, ln2_scale, ln2_offset)
            x = res + _cross_attention(h, xf_2, wq2, bq2, wk2, bk2, wv2, bv2, wo2, bo2, bias_k2, bias_v2)
            h = _layer_norm(x, ln_mlp_scale, ln_mlp_offset)
            h = jax.nn.gelu(h @ w_fc1 + b_fc1, approximate=False) @ w_fc2 + b_fc2
            return x + h
        key = jax.random.key(seed)
        ks = iter(jax.random.split(key, 64))

        def rn(shape, s=0.02):
            return jax.random.normal(next(ks), shape, jnp.float32) * s
        inp = {'x': rn((B, Q, D), 1.0), 'xf_1': rn((B, S1, D), 1.0), 'xf_2': rn((B, S2, D), 1.0)}
        for i in (1, 2):
            inp[f'ln{i}_scale'] = jnp.ones((D,), jnp.float32)
            inp[f'ln{i}_offset'] = jnp.zeros((D,), jnp.float32)
            inp[f'wq{i}'] = rn((D, H * K))
            inp[f'bq{i}'] = jnp.zeros((H * K,), jnp.float32)
            inp[f'wk{i}'] = rn((D, H * K))
            inp[f'bk{i}'] = jnp.zeros((H * K,), jnp.float32)
            inp[f'wv{i}'] = rn((D, H * K))
            inp[f'bv{i}'] = jnp.zeros((H * K,), jnp.float32)
            inp[f'wo{i}'] = rn((H * K, D))
            inp[f'bo{i}'] = jnp.zeros((D,), jnp.float32)
            inp[f'bias_k{i}'] = rn((1, 1, H, K))
            inp[f'bias_v{i}'] = rn((1, 1, H, K))
        inp['ln_mlp_scale'] = jnp.ones((D,), jnp.float32)
        inp['ln_mlp_offset'] = jnp.zeros((D,), jnp.float32)
        inp['w_fc1'] = rn((D, F))
        inp['b_fc1'] = jnp.zeros((F,), jnp.float32)
        inp['w_fc2'] = rn((F, D))
        inp['b_fc2'] = jnp.zeros((D,), jnp.float32)
        return inp
    _L0_xattn_all = _L0_xattn_setup()
    _L0_xattn_in = {k: v for k, v in _L0_xattn_all.items() if k in ('ln1_scale', 'ln1_offset', 'wq1', 'bq1', 'wk1', 'bk1', 'wv1', 'bv1', 'wo1', 'bo1', 'bias_k1', 'bias_v1', 'ln2_scale', 'ln2_offset', 'wq2', 'bq2', 'wk2', 'bk2', 'wv2', 'bv2', 'wo2', 'bo2', 'bias_k2', 'bias_v2', 'ln_mlp_scale', 'ln_mlp_offset', 'w_fc1', 'b_fc1', 'w_fc2', 'b_fc2')}
    del _L0_xattn_all

    def _L1_xattn_setup():
        import jax, jax.numpy as jnp
        import numpy as np
        B, P, K, H, NH = (4, 512, 64, 512, 16)
        DH = H // NH
        EPS = 1e-06

        def rmsnorm(x, w):
            var = jnp.mean(jnp.square(x), axis=-1, keepdims=True)
            return x * jax.lax.rsqrt(var + EPS) * w
        key = jax.random.key(seed)
        ks = jax.random.split(key, 12)
        s = 0.02
        return {'x': jax.random.normal(ks[0], (B, P, H), jnp.float32), 'latents': jax.random.normal(ks[1], (B, K, H), jnp.float32), 'attention_mask': jax.random.randint(ks[2], (B, P), 0, 2, jnp.int32), 'q_w': s * jax.random.normal(ks[3], (H, H), jnp.float32), 'q_b': jnp.zeros((H,), jnp.float32), 'kv_w': s * jax.random.normal(ks[4], (H, 2 * H), jnp.float32), 'kv_b': jnp.zeros((2 * H,), jnp.float32), 'out_w': s * jax.random.normal(ks[5], (H, H), jnp.float32), 'out_b': jnp.zeros((H,), jnp.float32), 'postnorm_w': jnp.ones((H,), jnp.float32), 'mlp_w1': s * jax.random.normal(ks[6], (H, 4 * H), jnp.float32), 'mlp_b1': jnp.zeros((4 * H,), jnp.float32), 'mlp_w2': s * jax.random.normal(ks[7], (4 * H, H), jnp.float32), 'mlp_b2': jnp.zeros((H,), jnp.float32)}
    _L1_xattn_all = _L1_xattn_setup()
    _L1_xattn_in = {k: v for k, v in _L1_xattn_all.items() if k in ('q_w', 'q_b', 'kv_w', 'kv_b', 'out_w', 'out_b', 'postnorm_w', 'mlp_w1', 'mlp_b1', 'mlp_w2', 'mlp_b2')}
    del _L1_xattn_all

    def _L2_xattn_setup():
        import jax, jax.numpy as jnp
        import numpy as np
        H = 512
        NH = 32
        KVH = 8
        HD = H // NH
        GROUPS = NH // KVH
        EPS = 1e-06
        B, L, S = (4, 256, 256)

        def _gqa_forward(hidden_state, encoder_hidden_state, encoder_attention_mask, Wq, bq, Wk, bk, Wv, bv, Wo, bo, gamma, beta):
            b, l, _ = hidden_state.shape
            s = encoder_hidden_state.shape[1]
            q = hidden_state @ Wq + bq
            k = encoder_hidden_state @ Wk + bk
            v = encoder_hidden_state @ Wv + bv
            q = q.reshape(b, l, KVH, GROUPS, HD).transpose(0, 2, 3, 1, 4)
            k = k.reshape(b, s, KVH, HD).transpose(0, 2, 1, 3)
            v = v.reshape(b, s, KVH, HD).transpose(0, 2, 1, 3)
            scale = 1.0 / jnp.sqrt(jnp.asarray(HD, q.dtype))
            scores = jnp.einsum('bkgld,bksd->bkgls', q, k) * scale
            scores = scores + encoder_attention_mask[:, :, None, :, :]
            attn = jax.nn.softmax(scores, axis=-1)
            out = jnp.einsum('bkgls,bksd->bkgld', attn, v)
            out = out.transpose(0, 3, 1, 2, 4).reshape(b, l, H)
            out = out @ Wo + bo
            x = out + hidden_state
            mu = jnp.mean(x, axis=-1, keepdims=True)
            var = jnp.var(x, axis=-1, keepdims=True)
            return (x - mu) * jax.lax.rsqrt(var + EPS) * gamma + beta
        key = jax.random.key(seed)
        ks = jax.random.split(key, 12)
        sd = 0.02
        return {'hidden_state': jax.random.normal(ks[0], (B, L, H), jnp.float32), 'encoder_hidden_state': jax.random.normal(ks[1], (B, S, H), jnp.float32), 'encoder_attention_mask': jnp.zeros((B, 1, L, S), jnp.float32), 'Wq': jax.random.normal(ks[2], (H, H), jnp.float32) * sd, 'bq': jnp.zeros((H,), jnp.float32), 'Wk': jax.random.normal(ks[3], (H, KVH * HD), jnp.float32) * sd, 'bk': jnp.zeros((KVH * HD,), jnp.float32), 'Wv': jax.random.normal(ks[4], (H, KVH * HD), jnp.float32) * sd, 'bv': jnp.zeros((KVH * HD,), jnp.float32), 'Wo': jax.random.normal(ks[5], (H, H), jnp.float32) * sd, 'bo': jnp.zeros((H,), jnp.float32), 'gamma': jnp.ones((H,), jnp.float32), 'beta': jnp.zeros((H,), jnp.float32)}
    _L2_xattn_all = _L2_xattn_setup()
    _L2_xattn_in = {k: v for k, v in _L2_xattn_all.items() if k in ('Wq', 'bq', 'Wk', 'bk', 'Wv', 'bv', 'Wo', 'bo', 'gamma', 'beta')}
    del _L2_xattn_all

    def _L3_xattn_setup():
        import jax, jax.numpy as jnp
        import numpy as np
        H = 512
        B, L, S = (4, 1024, 10)
        key = jax.random.key(seed)
        k1, k2, k3, k4, k5, k6 = jax.random.split(key, 6)
        scale = 1.0 / np.sqrt(H)
        return {'h_english': jax.random.normal(k1, (B, L, H), dtype=jnp.float32), 'h_lojban': jax.random.normal(k2, (B, S, H), dtype=jnp.float32), 'w_q': jax.random.normal(k3, (H, H), dtype=jnp.float32) * scale, 'w_k': jax.random.normal(k4, (H, H), dtype=jnp.float32) * scale, 'w_v': jax.random.normal(k5, (H, H), dtype=jnp.float32) * scale, 'w_o': jax.random.normal(k6, (H, H), dtype=jnp.float32) * scale, 'alpha': jnp.float32(0.1)}
    _L3_xattn_all = _L3_xattn_setup()
    _L3_xattn_in = {k: v for k, v in _L3_xattn_all.items() if k in ('w_q', 'w_k', 'w_v', 'w_o', 'alpha')}
    del _L3_xattn_all
    return {'x': x, 'ctx_2048': ctx_2048, 'mask_BxS2_ik0': mask_BxS2_ik0, 'mask_Bx1xSxS2_ff0': mask_Bx1xSxS2_ff0, 'L0_xattn_ln1_scale': _L0_xattn_in['ln1_scale'], 'L0_xattn_ln1_offset': _L0_xattn_in['ln1_offset'], 'L0_xattn_wq1': _L0_xattn_in['wq1'], 'L0_xattn_bq1': _L0_xattn_in['bq1'], 'L0_xattn_wk1': _L0_xattn_in['wk1'], 'L0_xattn_bk1': _L0_xattn_in['bk1'], 'L0_xattn_wv1': _L0_xattn_in['wv1'], 'L0_xattn_bv1': _L0_xattn_in['bv1'], 'L0_xattn_wo1': _L0_xattn_in['wo1'], 'L0_xattn_bo1': _L0_xattn_in['bo1'], 'L0_xattn_bias_k1': _L0_xattn_in['bias_k1'], 'L0_xattn_bias_v1': _L0_xattn_in['bias_v1'], 'L0_xattn_ln2_scale': _L0_xattn_in['ln2_scale'], 'L0_xattn_ln2_offset': _L0_xattn_in['ln2_offset'], 'L0_xattn_wq2': _L0_xattn_in['wq2'], 'L0_xattn_bq2': _L0_xattn_in['bq2'], 'L0_xattn_wk2': _L0_xattn_in['wk2'], 'L0_xattn_bk2': _L0_xattn_in['bk2'], 'L0_xattn_wv2': _L0_xattn_in['wv2'], 'L0_xattn_bv2': _L0_xattn_in['bv2'], 'L0_xattn_wo2': _L0_xattn_in['wo2'], 'L0_xattn_bo2': _L0_xattn_in['bo2'], 'L0_xattn_bias_k2': _L0_xattn_in['bias_k2'], 'L0_xattn_bias_v2': _L0_xattn_in['bias_v2'], 'L0_xattn_ln_mlp_scale': _L0_xattn_in['ln_mlp_scale'], 'L0_xattn_ln_mlp_offset': _L0_xattn_in['ln_mlp_offset'], 'L0_xattn_w_fc1': _L0_xattn_in['w_fc1'], 'L0_xattn_b_fc1': _L0_xattn_in['b_fc1'], 'L0_xattn_w_fc2': _L0_xattn_in['w_fc2'], 'L0_xattn_b_fc2': _L0_xattn_in['b_fc2'], 'L1_xattn_q_w': _L1_xattn_in['q_w'], 'L1_xattn_q_b': _L1_xattn_in['q_b'], 'L1_xattn_kv_w': _L1_xattn_in['kv_w'], 'L1_xattn_kv_b': _L1_xattn_in['kv_b'], 'L1_xattn_out_w': _L1_xattn_in['out_w'], 'L1_xattn_out_b': _L1_xattn_in['out_b'], 'L1_xattn_postnorm_w': _L1_xattn_in['postnorm_w'], 'L1_xattn_mlp_w1': _L1_xattn_in['mlp_w1'], 'L1_xattn_mlp_b1': _L1_xattn_in['mlp_b1'], 'L1_xattn_mlp_w2': _L1_xattn_in['mlp_w2'], 'L1_xattn_mlp_b2': _L1_xattn_in['mlp_b2'], 'L2_xattn_Wq': _L2_xattn_in['Wq'], 'L2_xattn_bq': _L2_xattn_in['bq'], 'L2_xattn_Wk': _L2_xattn_in['Wk'], 'L2_xattn_bk': _L2_xattn_in['bk'], 'L2_xattn_Wv': _L2_xattn_in['Wv'], 'L2_xattn_bv': _L2_xattn_in['bv'], 'L2_xattn_Wo': _L2_xattn_in['Wo'], 'L2_xattn_bo': _L2_xattn_in['bo'], 'L2_xattn_gamma': _L2_xattn_in['gamma'], 'L2_xattn_beta': _L2_xattn_in['beta'], 'L3_xattn_w_q': _L3_xattn_in['w_q'], 'L3_xattn_w_k': _L3_xattn_in['w_k'], 'L3_xattn_w_v': _L3_xattn_in['w_v'], 'L3_xattn_w_o': _L3_xattn_in['w_o'], 'L3_xattn_alpha': _L3_xattn_in['alpha']}

def reference(x, ctx_2048, mask_BxS2_ik0, mask_Bx1xSxS2_ff0, L0_xattn_ln1_scale, L0_xattn_ln1_offset, L0_xattn_wq1, L0_xattn_bq1, L0_xattn_wk1, L0_xattn_bk1, L0_xattn_wv1, L0_xattn_bv1, L0_xattn_wo1, L0_xattn_bo1, L0_xattn_bias_k1, L0_xattn_bias_v1, L0_xattn_ln2_scale, L0_xattn_ln2_offset, L0_xattn_wq2, L0_xattn_bq2, L0_xattn_wk2, L0_xattn_bk2, L0_xattn_wv2, L0_xattn_bv2, L0_xattn_wo2, L0_xattn_bo2, L0_xattn_bias_k2, L0_xattn_bias_v2, L0_xattn_ln_mlp_scale, L0_xattn_ln_mlp_offset, L0_xattn_w_fc1, L0_xattn_b_fc1, L0_xattn_w_fc2, L0_xattn_b_fc2, L1_xattn_q_w, L1_xattn_q_b, L1_xattn_kv_w, L1_xattn_kv_b, L1_xattn_out_w, L1_xattn_out_b, L1_xattn_postnorm_w, L1_xattn_mlp_w1, L1_xattn_mlp_b1, L1_xattn_mlp_w2, L1_xattn_mlp_b2, L2_xattn_Wq, L2_xattn_bq, L2_xattn_Wk, L2_xattn_bk, L2_xattn_Wv, L2_xattn_bv, L2_xattn_Wo, L2_xattn_bo, L2_xattn_gamma, L2_xattn_beta, L3_xattn_w_q, L3_xattn_w_k, L3_xattn_w_v, L3_xattn_w_o, L3_xattn_alpha):
    import jax
    import jax.numpy as jnp

    def _L0_xattn_ref(x, xf_1, xf_2, ln1_scale, ln1_offset, wq1, bq1, wk1, bk1, wv1, bv1, wo1, bo1, bias_k1, bias_v1, ln2_scale, ln2_offset, wq2, bq2, wk2, bk2, wv2, bv2, wo2, bo2, bias_k2, bias_v2, ln_mlp_scale, ln_mlp_offset, w_fc1, b_fc1, w_fc2, b_fc2):
        import jax, jax.numpy as jnp
        import numpy as np
        B, Q, S1, S2 = (4, 64, 512, 512)
        D, H, K, F = (512, 16, 128, 2048)
        LN_EPS = 1e-05

        def _layer_norm(x, scale, offset):
            mu = jnp.mean(x, axis=-1, keepdims=True)
            var = jnp.var(x, axis=-1, keepdims=True)
            return (x - mu) * jax.lax.rsqrt(var + LN_EPS) * scale + offset

        def _cross_attention(q_in, kv_in, wq, bq, wk, bk, wv, bv, wo, bo, bias_k, bias_v):
            b, q_len, _ = q_in.shape
            t = kv_in.shape[1]
            qh = (q_in @ wq + bq).reshape(b, q_len, H, K)
            kh = (kv_in @ wk + bk).reshape(b, t, H, K)
            vh = (kv_in @ wv + bv).reshape(b, t, H, K)
            kh = jnp.concatenate([kh, jnp.broadcast_to(bias_k, (b, 1, H, K))], axis=1)
            vh = jnp.concatenate([vh, jnp.broadcast_to(bias_v, (b, 1, H, K))], axis=1)
            scale = jnp.sqrt(jnp.asarray(K, q_in.dtype))
            logits = jnp.einsum('bqhk,bthk->bhqt', qh, kh) / scale
            weights = jax.nn.softmax(logits, axis=-1)
            ctx = jnp.einsum('bhqt,bthk->bqhk', weights, vh).reshape(b, q_len, H * K)
            return ctx @ wo + bo

        def _forward(x, xf_1, xf_2, ln1_scale, ln1_offset, wq1, bq1, wk1, bk1, wv1, bv1, wo1, bo1, bias_k1, bias_v1, ln2_scale, ln2_offset, wq2, bq2, wk2, bk2, wv2, bv2, wo2, bo2, bias_k2, bias_v2, ln_mlp_scale, ln_mlp_offset, w_fc1, b_fc1, w_fc2, b_fc2):
            res = x
            h = _layer_norm(x, ln1_scale, ln1_offset)
            x = res + _cross_attention(h, xf_1, wq1, bq1, wk1, bk1, wv1, bv1, wo1, bo1, bias_k1, bias_v1)
            res = x
            h = _layer_norm(x, ln2_scale, ln2_offset)
            x = res + _cross_attention(h, xf_2, wq2, bq2, wk2, bk2, wv2, bv2, wo2, bo2, bias_k2, bias_v2)
            h = _layer_norm(x, ln_mlp_scale, ln_mlp_offset)
            h = jax.nn.gelu(h @ w_fc1 + b_fc1, approximate=False) @ w_fc2 + b_fc2
            return x + h
        return _forward(x, xf_1, xf_2, ln1_scale, ln1_offset, wq1, bq1, wk1, bk1, wv1, bv1, wo1, bo1, bias_k1, bias_v1, ln2_scale, ln2_offset, wq2, bq2, wk2, bk2, wv2, bv2, wo2, bo2, bias_k2, bias_v2, ln_mlp_scale, ln_mlp_offset, w_fc1, b_fc1, w_fc2, b_fc2)

    def _L1_xattn_ref(x, latents, attention_mask, q_w, q_b, kv_w, kv_b, out_w, out_b, postnorm_w, mlp_w1, mlp_b1, mlp_w2, mlp_b2):
        import jax, jax.numpy as jnp
        import numpy as np
        B, P, K, H, NH = (4, 512, 64, 512, 16)
        DH = H // NH
        EPS = 1e-06

        def rmsnorm(x, w):
            var = jnp.mean(jnp.square(x), axis=-1, keepdims=True)
            return x * jax.lax.rsqrt(var + EPS) * w
        b, p, _ = x.shape
        k_len = latents.shape[1]
        residual = latents
        h = jnp.concatenate([x, latents], axis=1)
        q = (latents @ q_w + q_b).reshape(b, k_len, NH, DH)
        kv = (h @ kv_w + kv_b).reshape(b, p + k_len, NH, DH, 2)
        kmat, v = (kv[..., 0], kv[..., 1])
        attn = jnp.einsum('bkhd,bnhd->bhkn', q, kmat) / DH
        full_mask = jnp.concatenate([attention_mask.astype(bool), jnp.ones((b, k_len), bool)], axis=-1)
        attn = jnp.where(full_mask[:, None, None, :], attn, -jnp.inf)
        attn = jax.nn.softmax(attn.astype(jnp.float32), axis=-1).astype(q.dtype)
        attn_out = jnp.einsum('bhkn,bnhd->bkhd', attn, v).reshape(b, k_len, H)
        attn_out = attn_out @ out_w + out_b + residual
        out = rmsnorm(attn_out, postnorm_w)
        out = jax.nn.gelu(out @ mlp_w1 + mlp_b1) @ mlp_w2 + mlp_b2
        return out + residual

    def _L2_xattn_ref(hidden_state, encoder_hidden_state, encoder_attention_mask, Wq, bq, Wk, bk, Wv, bv, Wo, bo, gamma, beta):
        import jax, jax.numpy as jnp
        import numpy as np
        H = 512
        NH = 32
        KVH = 8
        HD = H // NH
        GROUPS = NH // KVH
        EPS = 1e-06
        B, L, S = (4, 256, 256)

        def _gqa_forward(hidden_state, encoder_hidden_state, encoder_attention_mask, Wq, bq, Wk, bk, Wv, bv, Wo, bo, gamma, beta):
            b, l, _ = hidden_state.shape
            s = encoder_hidden_state.shape[1]
            q = hidden_state @ Wq + bq
            k = encoder_hidden_state @ Wk + bk
            v = encoder_hidden_state @ Wv + bv
            q = q.reshape(b, l, KVH, GROUPS, HD).transpose(0, 2, 3, 1, 4)
            k = k.reshape(b, s, KVH, HD).transpose(0, 2, 1, 3)
            v = v.reshape(b, s, KVH, HD).transpose(0, 2, 1, 3)
            scale = 1.0 / jnp.sqrt(jnp.asarray(HD, q.dtype))
            scores = jnp.einsum('bkgld,bksd->bkgls', q, k) * scale
            scores = scores + encoder_attention_mask[:, :, None, :, :]
            attn = jax.nn.softmax(scores, axis=-1)
            out = jnp.einsum('bkgls,bksd->bkgld', attn, v)
            out = out.transpose(0, 3, 1, 2, 4).reshape(b, l, H)
            out = out @ Wo + bo
            x = out + hidden_state
            mu = jnp.mean(x, axis=-1, keepdims=True)
            var = jnp.var(x, axis=-1, keepdims=True)
            return (x - mu) * jax.lax.rsqrt(var + EPS) * gamma + beta
        return _gqa_forward(hidden_state, encoder_hidden_state, encoder_attention_mask, Wq, bq, Wk, bk, Wv, bv, Wo, bo, gamma, beta)

    def _L3_xattn_ref(h_english, h_lojban, w_q, w_k, w_v, w_o, alpha):
        import jax, jax.numpy as jnp
        import numpy as np
        H = 512
        B, L, S = (4, 1024, 10)
        h = h_english.shape[-1]
        q = jnp.einsum('blh,oh->blo', h_english, w_q)
        k = jnp.einsum('bsh,oh->bso', h_lojban, w_k)
        v = jnp.einsum('bsh,oh->bso', h_lojban, w_v)
        scores = jnp.einsum('blh,bsh->bls', q, k) / jnp.sqrt(jnp.float32(h))
        probs = jax.nn.softmax(scores, axis=-1)
        context = jnp.einsum('bls,bsh->blh', probs, v)
        delta = jnp.einsum('blh,oh->blo', context, w_o)
        return h_english + alpha * delta
    x = _L0_xattn_ref(x, ctx_2048, ctx_2048, L0_xattn_ln1_scale, L0_xattn_ln1_offset, L0_xattn_wq1, L0_xattn_bq1, L0_xattn_wk1, L0_xattn_bk1, L0_xattn_wv1, L0_xattn_bv1, L0_xattn_wo1, L0_xattn_bo1, L0_xattn_bias_k1, L0_xattn_bias_v1, L0_xattn_ln2_scale, L0_xattn_ln2_offset, L0_xattn_wq2, L0_xattn_bq2, L0_xattn_wk2, L0_xattn_bk2, L0_xattn_wv2, L0_xattn_bv2, L0_xattn_wo2, L0_xattn_bo2, L0_xattn_bias_k2, L0_xattn_bias_v2, L0_xattn_ln_mlp_scale, L0_xattn_ln_mlp_offset, L0_xattn_w_fc1, L0_xattn_b_fc1, L0_xattn_w_fc2, L0_xattn_b_fc2)
    x = _L1_xattn_ref(ctx_2048, x, mask_BxS2_ik0, L1_xattn_q_w, L1_xattn_q_b, L1_xattn_kv_w, L1_xattn_kv_b, L1_xattn_out_w, L1_xattn_out_b, L1_xattn_postnorm_w, L1_xattn_mlp_w1, L1_xattn_mlp_b1, L1_xattn_mlp_w2, L1_xattn_mlp_b2)
    x = _L2_xattn_ref(x, ctx_2048, mask_Bx1xSxS2_ff0, L2_xattn_Wq, L2_xattn_bq, L2_xattn_Wk, L2_xattn_bk, L2_xattn_Wv, L2_xattn_bv, L2_xattn_Wo, L2_xattn_bo, L2_xattn_gamma, L2_xattn_beta)
    x = _L3_xattn_ref(x, ctx_2048, L3_xattn_w_q, L3_xattn_w_k, L3_xattn_w_v, L3_xattn_w_o, L3_xattn_alpha)
    return x

_drawn_inputs = setup_inputs


def setup_inputs(seed=0):
    import zlib

    import numpy as np

    out = dict(_drawn_inputs(seed))
    spreads = {'L0_xattn_ln1_scale': (1.0, 0.6),
     'L0_xattn_ln1_offset': (0.0, 0.8),
     'L0_xattn_bq1': (0.0, 0.8),
     'L0_xattn_bk1': (0.0, 2.0),
     'L0_xattn_bv1': (0.0, 0.1),
     'L0_xattn_bo1': (0.0, 0.1),
     'L0_xattn_ln2_scale': (1.0, 0.6),
     'L0_xattn_ln2_offset': (0.0, 0.8),
     'L0_xattn_bq2': (0.0, 0.8),
     'L0_xattn_bk2': (0.0, 2.0),
     'L0_xattn_bv2': (0.0, 0.1),
     'L0_xattn_bo2': (0.0, 0.1),
     'L0_xattn_ln_mlp_scale': (1.0, 0.2),
     'L0_xattn_ln_mlp_offset': (0.0, 0.353),
     'L0_xattn_b_fc1': (0.0, 0.1),
     'L0_xattn_b_fc2': (0.0, 0.1),
     'L1_xattn_q_b': (0.0, 2.0),
     'L1_xattn_kv_b': (0.0, 0.8),
     'L1_xattn_out_b': (0.0, 0.416),
     'L1_xattn_postnorm_w': (1.0, 0.2),
     'L1_xattn_mlp_b1': (0.0, 0.1),
     'L1_xattn_mlp_b2': (0.0, 0.1),
     'L2_xattn_bq': (0.0, 0.8),
     'L2_xattn_bk': (0.0, 2.0),
     'L2_xattn_bv': (0.0, 0.1),
     'L2_xattn_bo': (0.0, 0.1),
     'L2_xattn_gamma': (1.0, 0.2),
     'L2_xattn_beta': (0.0, 0.1)}
    factors = {'L0_xattn_wq1': 3.841,
     'L0_xattn_wk1': 3.749,
     'L0_xattn_bias_k1': 64.0,
     'L0_xattn_bias_v1': 64.0,
     'L0_xattn_wq2': 3.961,
     'L0_xattn_wk2': 3.891,
     'L0_xattn_bias_k2': 64.0,
     'L0_xattn_bias_v2': 64.0,
     'L1_xattn_q_w': 8.0,
     'L1_xattn_kv_w': 4.42,
     'L1_xattn_out_w': 3.656,
     'L2_xattn_Wq': 7.571,
     'L2_xattn_Wk': 7.405,
     'L3_xattn_w_q': 2.718,
     'L3_xattn_w_k': 2.814}
    for name, (base, spread) in spreads.items():
        noise = np.random.default_rng([zlib.crc32(name.encode()), seed]).standard_normal(out[name].shape)
        drawn = base * np.exp(spread * noise) if base else spread * noise
        out[name] = jnp.asarray(drawn.astype(out[name].dtype))
    for name, factor in factors.items():
        out[name] = (out[name] * factor).astype(out[name].dtype)
    return out
```

```python
from contextlib import ExitStack

import concourse.bass as bass
from concourse import mybir

F32 = mybir.dt.float32
I32 = mybir.dt.int32
ALU = mybir.AluOpType
ACT = mybir.ActivationFunctionType
AX = mybir.AxisListType

P = 128
B = 8
SQ = 112
NT = B * SQ
HALF = NT // 2
SK = 375
KT = 3
KW = 126
SKP = KT * KW
SKB = SK + 1
D = 512
C = D // P
H0 = 16
HG = 2
NG = H0 // HG
GW = HG * P
F = 2048
FG = 4
NFG = F // (FG * P)
WROW = 16 * P * HG
MASKED = -1.0e30

COLS = {}


def _layout():
    at = 0
    names = []
    for a in ("1", "2"):
        names += [("ln_s" + a, C), ("ln_o" + a, C), ("bq" + a, H0), ("bk" + a, H0), ("bv" + a, H0),
                  ("bias_k" + a, H0), ("bo" + a, C)]
    names += [("ln_sm", C), ("ln_om", C), ("fc1", F // P), ("fc2", C)]
    names += [("l1_q", C), ("l1_k", C), ("l1_v", C), ("l1_o", C), ("l1_post", C), ("l1_m1", F // P), ("l1_m2", C)]
    names += [("l2_q", C), ("l2_k", 1), ("l2_v", C), ("l2_o", C), ("gamma", C), ("beta", C)]
    names += [("alpha", 1), ("even", 1), ("odd", 1), ("one", 1), ("eps5", 1), ("eps6", 1)]
    for n, w in names:
        COLS[n] = (at, w)
        at += w
    return at


NCOL = _layout()


class Machine:
    pass


class Mark:

    def __init__(self, sem):
        self.sem, self.base = sem, 0


def col(m, name, i=0, n=1):
    at = COLS[name][0] + i
    return m.cols[:, at:at + n]


def wait_loop(eng, sem, value):
    eng.wait_ge(sem, value)
    eng.nop(nofuse=True)


def load_group(sp, m, pack, g, buf, sem):
    sp.dma_start(m.wbuf[:, buf, :], pack[g]).then_inc(sem, 16)


def phase_load(nc, m, ctx, d, preload):
    ident_zero = ctx.enter_context(nc.semaphore("ident_zero"))
    constants_made = ctx.enter_context(nc.semaphore("constants_made"))
    inputs_loaded = ctx.enter_context(nc.semaphore("inputs_loaded"))
    with nc.Block() as block:
        @block.sync
        def _(sp):
            sp.dma_start(m.xT[:, :, :], d["x"]).then_inc(inputs_loaded, 16)
            sp.dma_start(m.cols[:, :], d["cols"]).then_inc(inputs_loaded, 16)
            preload(sp)
            sp.wait_ge(inputs_loaded, 32)

        @block.gpsimd
        def _(pool):
            nc.gpsimd.memset(m.ident[:, :], 0.0).then_inc(ident_zero, 1)
            nc.gpsimd.memset(m.mean_of[:, :], 1.0 / D).then_inc(constants_made, 1)
            pool.wait_ge(ident_zero, 1)
            nc.gpsimd.affine_select(out=m.ident[:, :], in_=m.ident[:, :], compare_op=ALU.not_equal, fill=1.0,
                                    base=0, pattern=[[-1, P]], channel_multiplier=1).then_inc(constants_made, 1)
            pool.wait_ge(constants_made, 2)


def phase_norm(nc, m, ctx, tag, src, dst, eps, scale, offset, centred=True, after_bias=None, preload=None,
               store=None):
    mean_done, centre_done, square_done, var_done, deviation_done, rstd_done, scaled, affine_done, bias_added = (
        m.norm_marks)
    with ExitStack() as own:
        sq = own.enter_context(nc.sbuf_tensor(f"sq_{tag}", [P, 2, C, HALF], F32))
        rstd = own.enter_context(nc.sbuf_tensor(f"rstd_{tag}", [P, 2, HALF], F32))
        ps = [own.enter_context(nc.psum_tensor(f"norm{i}_{tag}", [P, 512], F32)) for i in range(4)]
        block = own.enter_context(nc.Block())
        h = lambda t, s: t[:, :, s * HALF:(s + 1) * HALF]
        spread = lambda t: t.unsqueeze(1).broadcast_to((P, C, HALF))

        @block.tensor
        def _(pe):
            for s in range(2):
                if centred:
                    for c in range(C):
                        mm = pe.matmul(ps[s][:, 0:HALF], m.mean_of[:, :], src[:, c, s * HALF:(s + 1) * HALF],
                                       start=(c == 0), stop=(c == C - 1))
                    mm.then_inc(mean_done.sem, 1)
            for s in range(2):
                pe.wait_ge(square_done.sem, square_done.base + s + 1)
                for c in range(C):
                    mm = pe.matmul(ps[2 + s][:, 0:HALF], m.mean_of[:, :], sq[:, s, c, :],
                                   start=(c == 0), stop=(c == C - 1))
                mm.then_inc(var_done.sem, 1)

        @block.scalar
        def _(act):
            for s in range(2):
                if centred:
                    act.wait_ge(centre_done.sem, centre_done.base + s + 1)
                nc.scalar.activation(sq[:, s, :, :], h(dst if centred else src, s), ACT.Square
                                     ).then_inc(square_done.sem, 1)
            for s in range(2):
                act.wait_ge(var_done.sem, var_done.base + s + 1)
                nc.scalar.activation(rstd[:, s, :], ps[2 + s][:, 0:HALF], ACT.Sqrt, bias=col(m, eps)
                                     ).then_inc(deviation_done.sem, 1)
            for s in range(2):
                act.wait_ge(scaled.sem, scaled.base + s + 1)
                for c in range(C):
                    part = dst[:, c, s * HALF:(s + 1) * HALF]
                    if offset is None:
                        i = nc.scalar.activation(part, part, ACT.Identity, scale=col(m, scale, c))
                    else:
                        i = nc.scalar.activation(part, part, ACT.Identity, bias=col(m, offset, c),
                                                 scale=col(m, scale, c))
                    i.then_inc(affine_done.sem, 1)

        @block.vector
        def _(dve):
            if centred:
                for s in range(2):
                    dve.wait_ge(mean_done.sem, mean_done.base + s + 1)
                    nc.vector.tensor_tensor(h(dst, s), h(src, s), spread(ps[s][:, 0:HALF]), ALU.subtract
                                            ).then_inc(centre_done.sem, 1)
            for s in range(2):
                dve.wait_ge(deviation_done.sem, deviation_done.base + s + 1)
                nc.vector.reciprocal(rstd[:, s, :], rstd[:, s, :]).then_inc(rstd_done.sem, 1)
                dve.wait_ge(rstd_done.sem, rstd_done.base + s + 1)
                nc.vector.tensor_tensor(h(dst, s), h(dst if centred else src, s), spread(rstd[:, s, :]), ALU.mult
                                        ).then_inc(scaled.sem, 1)

        @block.gpsimd
        def _(pool):
            if after_bias is not None:
                pool.wait_ge(centre_done.sem, centre_done.base + 2)
                for c in range(C):
                    nc.gpsimd.tensor_scalar(src[:, c, :], src[:, c, :], col(m, after_bias, c), None, ALU.add
                                            ).then_inc(bias_added.sem, 1)

        @block.sync
        def _(sp):
            if preload is not None:
                preload(sp)
    for mark in (square_done, var_done, deviation_done, rstd_done, scaled) + (
            (mean_done, centre_done) if centred else ()):
        mark.base += 2


def phase_attn0(nc, m, ctx, tag, pack, rows, loaded):
    a = tag
    sem = lambda n: ctx.enter_context(nc.semaphore(f"{n}_a{tag}"))
    bq_scaled, kq_done, v_done, s_done, t_done, o_done = (sem(n) for n in ("bqs", "kq", "v", "s", "t", "o"))
    kq_out, exp_done, v_out, max_done, t_out, o_out = (sem(n) for n in ("kqe", "exp", "ve", "mx", "te", "oe"))
    vb_made, v_fixed, p_normed, pads_zero, recip_done = (sem(n) for n in ("vb", "vf", "pn", "pz", "rc"))
    scale = float(P) ** -0.5
    ITS = NG // 2
    KQ, VO, KQ_OUT, SMX, O_OUT = 4 + HG * B, 2 * B + 2 * C, 4 + 2 * HG * B, HG * B, HG * B
    with ExitStack() as own:
        sb = lambda n, s: own.enter_context(nc.sbuf_tensor(f"{n}_a{tag}", s, F32))
        q = sb("q", [P, HG, NT])
        ot = sb("ot", [P, HG, NT])
        kT = sb("kT", [P, 2, HG, SKB])
        v = sb("v", [KW, 2, KT, GW])
        p = sb("p", [SQ, 2, HG, SKP])
        pt = sb("pt", [KW, HG, KT, SQ])
        nmx = sb("nmx", [SQ, 2, HG])
        rsum, rinv = sb("rsum", [SQ, 2, HG]), sb("rinv", [SQ, 2, HG])
        bqs = sb("bqs", [P, H0])
        vb = sb("vb", [1, 2, GW])
        ps = lambda n: own.enter_context(nc.psum_tensor(f"{n}_a{tag}", [P, 512], F32))
        kbank, vbank, sbank = [ps("k0"), ps("k1")], [ps("v0"), ps("v1")], [ps("s0"), ps("s1")]
        tbank, obank = ps("t"), ps("o")
        wq = lambda g, k, j: m.wbuf[:, g, k * GW + j * P:k * GW + (j + 1) * P]
        wk = lambda g, k, j: m.wbuf[:, g, (C + k) * GW + j * P:(C + k) * GW + (j + 1) * P]
        wv = lambda g, k: m.wbuf[:, g, (2 * C + k) * GW:(2 * C + k + 1) * GW]
        wo = lambda g, j, c: m.wbuf[:, g, 3 * C * GW + j * D + c * P:3 * C * GW + j * D + (c + 1) * P]
        block = own.enter_context(nc.Block())

        @block.sync
        def _(sp):
            with sp.Fori(0, ITS - 1) as it:
                for g in range(2):
                    wait_loop(sp, v_out, it * (2 * VO) + ((g + 1) * VO + 1))
                    wait_loop(sp, v_fixed, it * (2 * B) + (g + 1) * B)
                    sp.dma_start(m.wbuf[:, g, :], pack[bass.ds(it * 2 + (2 + g), 1), :, :].rearrange("a p w -> p (a w)")
                                 ).then_inc(loaded[g], 16)
                    sp.dma_start(m.rowbuf[:, g, :], rows[bass.ds(it * 2 + (2 + g), 1), :]).then_inc(loaded[g], 16)

        @block.tensor
        def _(pe):
            with pe.Fori(0, ITS) as it:
                for g in range(2):
                    kq_freed = [0, 0]
                    outs = g * KQ_OUT
                    done = {"kq": 0, "v": 0}

                    def kq_bank(evacuations):
                        n = done["kq"]
                        pe.wait_ge(kq_out, it * (2 * KQ_OUT) + (1 + kq_freed[n % 2] if n >= 2 else 1 + outs))
                        done["kq"] += 1
                        total = done.get("kq_total", outs) + evacuations
                        done["kq_total"] = kq_freed[n % 2] = total
                        return kbank[n % 2]

                    def v_bank():
                        n = done["v"]
                        pe.wait_ge(v_out, it * (2 * VO) + (1 + g * VO + max(n - 1, 0)))
                        done["v"] += 1
                        return vbank[n % 2]

                    def q_proj(j, s):
                        bank = kq_bank(1)
                        for k in range(C):
                            mm = pe.matmul(bank[:, 0:HALF], wq(g, k, j), m.hT[:, k, s * HALF:(s + 1) * HALF],
                                           start=(k == 0), stop=(k == C - 1))
                        mm.then_inc(kq_done, 1)

                    def k_proj(b, j):
                        bank = kq_bank(2)
                        for k in range(C):
                            mm = pe.matmul(bank[:, 0:SKB], wk(g, k, j), m.ctxT[:, k, b * SKP:b * SKP + SKB],
                                           start=(k == 0), stop=(k == C - 1))
                        mm.then_inc(kq_done, 1)

                    def v_proj(b, tiles):
                        bank = v_bank()
                        for i, t in enumerate(tiles):
                            for k in range(C):
                                at = b * SKP + t * KW
                                mm = pe.matmul(bank[0:KW, i * GW:(i + 1) * GW], m.ctxT[:, k, at:at + KW], wv(g, k),
                                               start=(k == 0), stop=(k == C - 1))
                        mm.then_inc(v_done, 1)

                    def scores(b, j):
                        n = g * SMX + HG * b + j
                        pe.wait_ge(kq_out, it * (2 * KQ_OUT) + (1 + g * KQ_OUT + 4 + 2 * (HG * b + j + 1)))
                        pe.wait_ge(exp_done, it * (2 * SMX) + (1 + max(n - 1, 0)))
                        pe.matmul(sbank[j][0:SQ, 0:SKB], q[:, j, b * SQ:(b + 1) * SQ], kT[:, b % 2, j, :],
                                  start=True, stop=True).then_inc(s_done, 1)

                    def turn(b, j):
                        n = g * SMX + HG * b + j
                        pe.wait_ge(p_normed, it * (2 * SMX) + (n + 1))
                        pe.wait_ge(t_out, it * (2 * SMX) + (1 + n))
                        for t in range(KT):
                            mm = pe.transpose(tbank[0:KW, t * SQ:(t + 1) * SQ], p[:, b % 2, j, t * KW:(t + 1) * KW],
                                              m.ident[0:SQ, 0:SQ])
                        mm.then_inc(t_done, 1)

                    def weigh(b, j):
                        n = g * SMX + HG * b + j
                        pe.wait_ge(t_out, it * (2 * SMX) + (2 + n))
                        if j == 0:
                            pe.wait_ge(v_fixed, it * (2 * B) + (g * B + b + 1))
                            pe.wait_ge(v_out, it * (2 * VO) + (1 + g * VO + 2 * (b + 1)))
                            pe.wait_ge(o_out, it * (2 * O_OUT) + (1 + g * O_OUT + HG * b))
                        for t in range(KT):
                            mm = pe.matmul(obank[:, j * SQ:(j + 1) * SQ], v[:, b % 2, t, j * P:(j + 1) * P],
                                           pt[:, j, t, :], start=(t == 0), stop=(t == KT - 1))
                        if j == HG - 1:
                            mm.then_inc(o_done, 1)

                    def o_proj(s):
                        pe.wait_ge(o_out, it * (2 * O_OUT) + (1 + g * O_OUT + HG * (B // 2) * (s + 1)))
                        for c in range(C):
                            bank = v_bank()
                            for j in range(HG):
                                mm = pe.matmul(bank[:, 0:HALF], wo(g, j, c), ot[:, j, s * HALF:(s + 1) * HALF],
                                               start=(j == 0), stop=(j == HG - 1))
                            mm.then_inc(v_done, 1)

                    pe.wait_ge(loaded[g], it * 32 + 32)
                    for j in range(HG):
                        for s in range(2):
                            q_proj(j, s)
                    for b in range(B):
                        k_proj(b, 0)
                        k_proj(b, 1)
                        if b:
                            turn(b - 1, 0)
                        v_proj(b, [0, 1])
                        if b:
                            weigh(b - 1, 0)
                            turn(b - 1, 1)
                        v_proj(b, [2])
                        if b:
                            weigh(b - 1, 1)
                        scores(b, 0)
                        scores(b, 1)
                    o_proj(0)
                    for j in range(HG):
                        turn(B - 1, j)
                        weigh(B - 1, j)
                    o_proj(1)

        @block.scalar
        def _(act):
            act.sem_inc(kq_out, 1)
            act.sem_inc(exp_done, 1)
            act.wait_ge(bq_scaled, 1)
            with act.Fori(0, ITS) as it:
                for g in range(2):
                    head = it * (2 * HG) + g * HG

                    def column(t, at, j):
                        return t[:, bass.ds(head + (at + j), 1)]

                    for j in range(HG):
                        for s in range(2):
                            wait_loop(act, kq_done, it * (2 * KQ) + (g * KQ + 2 * j + s + 1))
                            nc.scalar.activation(q[:, j, s * HALF:(s + 1) * HALF],
                                                 kbank[s][:, 0:HALF], ACT.Identity,
                                                 bias=column(bqs, 0, j),
                                                 scale=scale).then_inc(kq_out, 1)
                    for b in range(B):
                        for j in range(HG):
                            wait_loop(act, kq_done, it * (2 * KQ) + (g * KQ + 4 + HG * b + j + 1))
                            nc.scalar.activation(kT[:, b % 2, j, 1:SKB], kbank[j][:, 1:SKB], ACT.Identity,
                                                 bias=column(m.cols, COLS["bk" + a][0], j)).then_inc(kq_out, 1)
                            nc.scalar.activation(kT[:, b % 2, j, 0:1], column(m.cols, COLS["bias_k" + a][0], j),
                                                 ACT.Identity).then_inc(kq_out, 1)
                        for j in range(HG):
                            n = g * SMX + HG * b + j
                            wait_loop(act, max_done, it * (2 * SMX) + (n + 1))
                            if g == 0 and b < 2:
                                act.wait_ge(pads_zero, 1)
                            nc.scalar.activation(p[:, b % 2, j, 0:SKB], sbank[j][0:SQ, 0:SKB], ACT.Exp,
                                                 bias=nmx[:, b % 2, j:j + 1],
                                                 accum_out=rsum[:, b % 2, j:j + 1]).then_inc(exp_done, 1)

        @block.vector
        def _(dve):
            dve.sem_inc(v_out, 1)
            dve.sem_inc(t_out, 1)
            dve.sem_inc(o_out, 1)
            nc.vector.tensor_scalar(bqs[:, :], col(m, "bq" + a, 0, H0), scale, None, ALU.mult).then_inc(bq_scaled, 1)
            with dve.Fori(0, ITS) as it:
                for g in range(2):
                    head = it * (2 * HG) + g * HG

                    def v_evacuate(b, n):
                        dve.wait_ge(v_done, it * (2 * VO) + (g * VO + 2 * b + n + 1))
                        w = 2 * GW if n == 0 else GW
                        nc.vector.tensor_copy(v[:, b % 2, 2 * n:2 * n + w // GW, :],
                                              vbank[n][0:KW, 0:w].rearrange("p (t w) -> p t w", w=GW)
                                              ).then_inc(v_out, 1)

                    def t_evacuate(b, j):
                        dve.wait_ge(t_done, it * (2 * SMX) + (g * SMX + HG * b + j + 1))
                        nc.vector.tensor_copy(pt[:, j, :, :],
                                              tbank[0:KW, 0:KT * SQ].rearrange("p (t q) -> p t q", q=SQ)
                                              ).then_inc(t_out, 1)

                    def o_evacuate(b):
                        dve.wait_ge(o_done, it * (2 * B) + (g * B + b + 1))
                        for j in range(HG):
                            at = COLS["bv" + a][0] + j
                            nc.vector.tensor_scalar(ot[:, j, b * SQ:(b + 1) * SQ], obank[:, j * SQ:(j + 1) * SQ],
                                                    m.cols[:, bass.ds(head + at, 1)], None, ALU.add
                                                    ).then_inc(o_out, 1)

                    def row_max(b, j):
                        dve.wait_ge(s_done, it * (2 * SMX) + (g * SMX + HG * b + j + 1))
                        nc.vector.tensor_reduce(nmx[:, b % 2, j:j + 1], sbank[j][0:SQ, 0:SKB], AX.X, ALU.max,
                                                negate=True).then_inc(max_done, 1)

                    def add_to_x(s):
                        for c in range(C):
                            dve.wait_ge(v_done, it * (2 * VO) + (g * VO + 2 * B + C * s + c + 1))
                            part = m.xT[:, c, s * HALF:(s + 1) * HALF]
                            nc.vector.tensor_tensor(part, part, vbank[c % 2][:, 0:HALF], ALU.add).then_inc(v_out, 1)

                    for b in range(B):
                        if b:
                            t_evacuate(b - 1, 0)
                        v_evacuate(b, 0)
                        if b:
                            t_evacuate(b - 1, 1)
                        v_evacuate(b, 1)
                        if b:
                            o_evacuate(b - 1)
                        row_max(b, 0)
                        row_max(b, 1)
                        dve.wait_ge(exp_done, it * (2 * SMX) + (1 + g * SMX + HG * (b + 1)))
                        nc.vector.reciprocal(rinv[:, b % 2, :], rsum[:, b % 2, :]).then_inc(recip_done, 1)
                    add_to_x(0)
                    t_evacuate(B - 1, 0)
                    t_evacuate(B - 1, 1)
                    o_evacuate(B - 1)
                    add_to_x(1)

        @block.gpsimd
        def _(pool):
            nc.gpsimd.memset(p[:, :, :, SKB:SKP], 0.0).then_inc(pads_zero, 1)
            with pool.Fori(0, ITS) as it:
                for g in range(2):
                    wait_loop(pool, loaded[g], it * 32 + 32)
                    nc.gpsimd.tensor_tensor(vb[:, g, :], m.rowbuf[:, g, 0:GW], m.rowbuf[:, g, GW:2 * GW], ALU.subtract
                                            ).then_inc(vb_made, 1)
                    wait_loop(pool, vb_made, it * 2 + (g + 1))
                    for b in range(B):
                        wait_loop(pool, v_out, it * (2 * VO) + (1 + g * VO + 2 * b + 1))
                        nc.gpsimd.tensor_copy(v[0:1, b % 2, 0, :], vb[:, g, :]).then_inc(v_fixed, 1)
                        for j in range(HG):
                            if j == 0:
                                wait_loop(pool, recip_done, it * (2 * B) + (g * B + b + 1))
                            nc.gpsimd.tensor_scalar(p[:, b % 2, j, 0:SKB], p[:, b % 2, j, 0:SKB],
                                                    rinv[:, b % 2, j:j + 1], None, ALU.mult).then_inc(p_normed, 1)


def phase_mlp(nc, m, ctx, tag, pack, loaded, func, b1, b2):
    sem = lambda n: ctx.enter_context(nc.semaphore(f"{n}_{tag}"))
    up_done, act_done, down_done, added, bias_added = (sem(n) for n in ("up", "gelu", "down", "add", "b2"))
    ITS = NFG // 2
    UP, DOWN = 2 * FG, 2 * C
    with ExitStack() as own:
        g = own.enter_context(nc.sbuf_tensor(f"g_{tag}", [P, 2, FG, HALF], F32))
        ps = lambda n: own.enter_context(nc.psum_tensor(f"{n}_{tag}", [P, 512], F32))
        up, down = [ps(f"up{i}") for i in range(4)], [ps(f"down{i}") for i in range(4)]
        w1 = lambda i, k, f: m.wbuf[:, i, (k * FG + f) * P:(k * FG + f + 1) * P]
        w2 = lambda i, f, c: m.wbuf[:, i, C * FG * P + f * D + c * P:C * FG * P + f * D + (c + 1) * P]
        block = own.enter_context(nc.Block())

        @block.sync
        def _(sp):
            with sp.Fori(0, ITS - 1) as it:
                for i in range(2):
                    wait_loop(sp, added, it * (2 * DOWN) + (1 + (i + 1) * DOWN))
                    sp.dma_start(m.wbuf[:, i, :], pack[bass.ds(it * 2 + (2 + i), 1), :, :].rearrange("a p w -> p (a w)")
                                 ).then_inc(loaded[i], 16)

        @block.tensor
        def _(pe):
            with pe.Fori(0, ITS) as it:
                for i in range(2):
                    pe.wait_ge(loaded[i], it * 16 + 16)
                    for s in range(2):
                        for f in range(FG):
                            n = i * UP + s * FG + f
                            pe.wait_ge(act_done, it * (2 * UP) + (1 + max(n - 3, 0)))
                            for k in range(C):
                                mm = pe.matmul(up[f][:, 0:HALF], w1(i, k, f), m.hT[:, k, s * HALF:(s + 1) * HALF],
                                               start=(k == 0), stop=(k == C - 1))
                            mm.then_inc(up_done, 1)
                    for s in range(2):
                        pe.wait_ge(act_done, it * (2 * UP) + (1 + i * UP + (s + 1) * FG))
                        for c in range(C):
                            n = i * DOWN + s * C + c
                            pe.wait_ge(added, it * (2 * DOWN) + (1 + max(n - 3, 0)))
                            for f in range(FG):
                                mm = pe.matmul(down[c][:, 0:HALF], w2(i, f, c), g[:, s, f, :],
                                               start=(f == 0), stop=(f == FG - 1))
                            mm.then_inc(down_done, 1)

        @block.scalar
        def _(act):
            act.sem_inc(act_done, 1)
            with act.Fori(0, ITS) as it:
                for i in range(2):
                    for s in range(2):
                        for f in range(FG):
                            wait_loop(act, up_done, it * (2 * UP) + (i * UP + s * FG + f + 1))
                            at = COLS[b1][0] + i * FG + f
                            nc.scalar.activation(g[:, s, f, :], up[f][:, 0:HALF], func,
                                                 bias=m.cols[:, bass.ds(it * (2 * FG) + at, 1)]).then_inc(act_done, 1)

        @block.vector
        def _(dve):
            dve.sem_inc(added, 1)
            dve.wait_ge(bias_added, C)
            with dve.Fori(0, ITS) as it:
                for i in range(2):
                    for s in range(2):
                        for c in range(C):
                            dve.wait_ge(down_done, it * (2 * DOWN) + (i * DOWN + s * C + c + 1))
                            part = m.xT[:, c, s * HALF:(s + 1) * HALF]
                            nc.vector.tensor_tensor(part, part, down[c][:, 0:HALF], ALU.add).then_inc(added, 1)

        @block.gpsimd
        def _(pool):
            for c in range(C):
                nc.gpsimd.tensor_scalar(m.xT[:, c, :], m.xT[:, c, :], col(m, b2, c), None, ALU.add
                                        ).then_inc(bias_added, 1)


def phase_dense(nc, m, ctx, tag, w, src, dst, evacuate, preload=None):
    w_loaded, product_done, stored = m.dense_marks
    with ExitStack() as own:
        wt = own.enter_context(nc.sbuf_tensor(f"w_{tag}", [P, C, D], F32))
        bank = [own.enter_context(nc.psum_tensor(f"b{i}_{tag}", [P, 512], F32)) for i in range(4)]
        block = own.enter_context(nc.Block())

        @block.sync
        def _(sp):
            sp.dma_start(wt[:, :, :], w).then_inc(w_loaded.sem, 16)
            if preload is not None:
                preload(sp)

        @block.tensor
        def _(pe):
            pe.wait_ge(w_loaded.sem, w_loaded.base + 16)
            for s in range(2):
                for c in range(C):
                    n = s * C + c
                    if n >= 4:
                        pe.wait_ge(stored.sem, stored.base + n - 3)
                    for k in range(C):
                        mm = pe.matmul(bank[n % 4][:, 0:HALF], wt[:, k, c * P:(c + 1) * P],
                                       src[:, k, s * HALF:(s + 1) * HALF], start=(k == 0), stop=(k == C - 1))
                    mm.then_inc(product_done.sem, 1)

        @block.vector
        def _(dve):
            for s in range(2):
                for c in range(C):
                    n = s * C + c
                    dve.wait_ge(product_done.sem, product_done.base + n + 1)
                    evacuate(dst[:, c, s * HALF:(s + 1) * HALF], bank[n % 4][:, 0:HALF], c,
                             slice(s * HALF, (s + 1) * HALF)).then_inc(stored.sem, 1)
    for mark, n in ((w_loaded, 16), (product_done, 2 * C), (stored, 2 * C)):
        mark.base += n


class Small:

    def __init__(self, heads, width, k_chunks, latent, scale):
        self.heads, self.width, self.k_chunks, self.latent, self.scale = heads, width, k_chunks, latent, scale
        self.keys = SKP + (SQ if latent else 0)
        self.tiles = KT + (1 if latent else 0)
        self.v_width = k_chunks * P


def phase_small(nc, m, ctx, tag, cfg, d, mask, q_of, head_of, bias):
    sem = lambda n: ctx.enter_context(nc.semaphore(f"{n}_{tag}"))
    w_loaded, staged = sem("w"), [sem(f"staged{i}") for i in range(2)]
    unit_done, s_done, t_done, o_done = sem("unit"), sem("s"), sem("t"), sem("o")
    unit_act, unit_dve, sm_done, exp_done, o_out = sem("ua"), sem("ud"), sem("sm"), sem("exp"), sem("oo")
    t_out = [sem(f"te{i}") for i in range(2)]
    recip_done, mask_made, setup_done, pad_done = sem("rc"), sem("mk"), sem("su"), sem("pd")
    NH, NC, NTL, KEYS, VW, HW = cfg.heads, cfg.k_chunks, cfg.tiles, cfg.keys, cfg.v_width, cfg.width
    ITS = B // 2
    tiles = [(i * KW, KW) for i in range(KT)] + ([(SKP, SQ)] if cfg.latent else [])
    per_bank = 512 // VW
    v_units = [list(range(i, min(i + per_bank, NTL))) for i in range(0, NTL, per_bank)]
    plan = {-1: [("q", 0, 0), ("k", 0, 0)] + ([("k", 0, 1)] if NC > 1 else [])}
    vs = [("v", 0, u) for u in range(len(v_units))]
    for i, u in enumerate(vs):
        plan.setdefault(min(i // 2, 1) if len(vs) > 1 else 0, []).append(u)
    for c in range(2, NC):
        plan.setdefault(NH // NC * (c - 1), []).append(("k", 0, c))
    nxt = [("q", 1, 0)] + [("k", 1, c) for c in range(NC)] + [("v", 1, u) for u in range(len(v_units))]
    at = NH - len(nxt)
    for i, u in enumerate(nxt):
        plan.setdefault(at + i, []).append(u)
    LAG_T, LAG_O, LAG_N = 2, 3, 5
    STEPS = 2 * NH
    for b in range(2):
        plan.setdefault((b + 1) * NH - 1 + LAG_N, []).append(("ot", b, 0))
    order = [u for s in sorted(plan) for u in plan[s]]
    number = {u: n for n, u in enumerate(order)}
    owner = {u: ("act" if u[0] in "qk" and u[0] != "ot" else "dve") for u in order}
    incs = {}
    for u in order:
        incs[u] = {"q": len(q_of["parts"]), "k": 1, "v": 2 if 3 in v_units[u[2]] and len(v_units[u[2]]) > 1 else 1,
                   "ot": 1}[u[0]]
    after = {}
    total = {"act": 0, "dve": 0}
    for u in order:
        total[owner[u]] += incs[u]
        after[u] = total[owner[u]]
    with ExitStack() as own:
        sb = lambda n, s, dt=F32: own.enter_context(nc.sbuf_tensor(f"{n}_{tag}", s, dt))
        wq, wk, wv = sb("wq", [P, C, D]), sb("wk", [P, C, NC * P]), sb("wv", [P, C, VW])
        cb = sb("cb", [P, 2, C, SKP])
        xb = sb("xb", [P, 2, C, SQ])
        NQ = q_of["versions"]
        qb = sb("qb", [P, 2, NQ, C, SQ])
        kb = sb("kb", [P, 2, NC, KEYS])
        vb = sb("vb", [KW, 2, NTL, VW])
        mraw = sb("mraw", [SQ, 2, SKP], mask["dtype"])
        mk = sb("mk", [SQ, 2, KEYS]) if mask["convert"] else mraw
        sm = sb("sm", [SQ, 3, KEYS])
        p = sb("p", [SQ, 3, KEYS])
        pt = sb("pt", [KW, 2, NTL, SQ])
        nmx, rsum, rinv = sb("nmx", [SQ, 4]), sb("rsum", [SQ, 2, NH]), sb("rinv", [SQ, 2, NH])
        on = sb("on", [SQ, D])
        qcols = sb("qcols", [P, 2 * (C + 1)])
        ps = lambda n: own.enter_context(nc.psum_tensor(f"{n}_{tag}", [P, 512], F32))
        ubank, sbank, tbank, obank = [ps("u0"), ps("u1")], [ps(f"s{i}") for i in range(3)], [ps("t0"), ps("t1")], ps("o")
        block = own.enter_context(nc.Block())
        SM, TE = 2 * NH, NH

        @block.sync
        def _(sp):
            for dst, name in ((wq, "wq"), (wk, "wk"), (wv, "wv")):
                sp.dma_start(dst[:, :, :], d[name]).then_inc(w_loaded, 16)

            def stage(b, i):
                sp.dma_start(cb[:, i, :, :], d["ctx"][bass.ds(b, 1), :, :, :].rearrange("a p c w -> p (a c) w")
                             ).then_inc(staged[i], 16)
                sp.dma_start(xb[:, i, :, :], m.xT[:, :, bass.ds(b * SQ, SQ)]).then_inc(staged[i], 16)
                sp.dma_start(mraw[:, i, :], mask["source"](b)).then_inc(staged[i], 16)

            for i in range(2):
                stage(i, i)
            with sp.Fori(0, ITS - 1) as it:
                for i in range(2):
                    wait_loop(sp, unit_dve, it * total["dve"] + (1 + after["ot", i, 0]))
                    stage(it * 2 + (2 + i), i)

        @block.tensor
        def _(pe):
            pe.wait_ge(w_loaded, 48)
            with pe.Fori(0, ITS) as it:
                def unit(u):
                    kind, b, i = u
                    n = number[u]
                    before = order[n - 2] if n >= 2 else None
                    for who, s in (("act", unit_act), ("dve", unit_dve)):
                        if before is None or owner[before] == who:
                            pe.wait_ge(s, it * total[who] + (1 + (after[before] if before else 0)))
                    bank = ubank[n % 2]
                    if kind == "q":
                        pe.wait_ge(staged[b], it * 48 + 48)
                        for c in range(C):
                            for k in range(C):
                                mm = pe.matmul(bank[:, c * SQ:(c + 1) * SQ], wq[:, k, c * P:(c + 1) * P], xb[:, b, k, :],
                                               start=(k == 0), stop=(k == C - 1))
                    elif kind == "k":
                        for k in range(C):
                            mm = pe.matmul(bank[:, 0:SKP], wk[:, k, i * P:(i + 1) * P], cb[:, b, k, :],
                                           start=(k == 0), stop=(k == C - 1))
                        if cfg.latent:
                            for k in range(C):
                                mm = pe.matmul(bank[:, SKP:KEYS], wk[:, k, i * P:(i + 1) * P], xb[:, b, k, :],
                                               start=(k == 0), stop=(k == C - 1))
                    elif kind == "v":
                        for e, t in enumerate(v_units[i]):
                            lo, w = tiles[t]
                            for k in range(C):
                                lhs = cb[:, b, k, lo:lo + w] if t < KT else xb[:, b, k, :]
                                mm = pe.matmul(bank[0:w, e * VW:(e + 1) * VW], lhs, wv[:, k, :],
                                               start=(k == 0), stop=(k == C - 1))
                    else:
                        pe.wait_ge(o_out, it * 2 + (2 + b))
                        for c in range(C):
                            mm = pe.transpose(bank[:, c * SQ:(c + 1) * SQ], on[:, c * P:(c + 1) * P], m.ident[0:SQ, 0:SQ])
                    mm.then_inc(unit_done, 1)

                def scores(n):
                    b, h = divmod(n, NH)
                    row, chunk, version, qc = head_of(h)
                    if h == 0:
                        pe.wait_ge(unit_act, it * total["act"] + (1 + after["q", b, 0]))
                    if h % (NH // NC) == 0:
                        pe.wait_ge(unit_act, it * total["act"] + (1 + after["k", b, chunk]))
                    pe.wait_ge(sm_done, it * SM + (1 + max(n - 2, 0)))
                    pe.matmul(sbank[n % 3][0:SQ, 0:KEYS], qb[row:row + 32, b, version, qc, :],
                              kb[row:row + 32, b, chunk, :], start=True, stop=True).then_inc(s_done, 1)

                def turn(n):
                    pe.wait_ge(exp_done, it * SM + (2 + n))
                    pe.wait_ge(t_out[n % 2], it * TE + (1 + n // 2))
                    for t, (lo, w) in enumerate(tiles):
                        mm = pe.transpose(tbank[n % 2][0:w, t * SQ:(t + 1) * SQ], p[:, n % 3, lo:lo + w],
                                          m.ident[0:SQ, 0:SQ])
                    mm.then_inc(t_done, 1)

                def weigh(n):
                    b, h = divmod(n, NH)
                    pe.wait_ge(t_out[n % 2], it * TE + (2 + n // 2))
                    if h == 0:
                        pe.wait_ge(unit_dve, it * total["dve"] + (1 + after["v", b, len(v_units) - 1]))
                        pe.wait_ge(o_out, it * 2 + (1 + b))
                    lo = bias["value_column"](h)
                    for t, (_, w) in enumerate(tiles):
                        mm = pe.matmul(obank[0:SQ, h * HW:(h + 1) * HW], pt[0:w, n % 2, t, :],
                                       vb[0:w, b, t, lo:lo + HW], start=(t == 0), stop=(t == NTL - 1))
                    if h == NH - 1:
                        mm.then_inc(o_done, 1)

                for u in plan[-1]:
                    unit(u)
                for s in range(STEPS + LAG_N):
                    if s < STEPS:
                        scores(s)
                    if 0 <= s - LAG_T < STEPS:
                        turn(s - LAG_T)
                    for u in plan.get(s, []):
                        unit(u)
                    if 0 <= s - LAG_O < STEPS:
                        weigh(s - LAG_O)

        def turned(eng, copy, it, n):
            wait_loop(eng, t_done, it * SM + (n + 1))
            src = tbank[n % 2][:, 0:NTL * SQ].rearrange("p (t q) -> p t q", q=SQ)
            i = copy(pt[:, n % 2, 0:KT, :], src[0:KW, 0:KT, :])
            if cfg.latent:
                i = copy(pt[0:SQ, n % 2, KT, :], src[0:SQ, KT, :])
            i.then_inc(t_out[n % 2], 1)

        @block.scalar
        def _(act):
            act.sem_inc(unit_act, 1)
            act.sem_inc(exp_done, 1)
            act.sem_inc(t_out[1], 1)
            act.wait_ge(setup_done, 2 * NQ)
            with act.Fori(0, ITS) as it:
                def unit(u):
                    kind, b, i = u
                    if owner[u] != "act":
                        return
                    wait_loop(act, unit_done, it * len(order) + (number[u] + 1))
                    bank = ubank[number[u] % 2]
                    if kind == "q":
                        for version, c, sc, bi in q_of["parts"]:
                            nc.scalar.activation(qb[:, b, version, c, :], bank[:, c * SQ:(c + 1) * SQ], ACT.Identity,
                                                 scale=qcols[:, sc:sc + 1], bias=qcols[:, bi:bi + 1]
                                                 ).then_inc(unit_act, 1)
                    else:
                        nc.scalar.activation(kb[:, b, i, :], bank[:, 0:KEYS], ACT.Identity,
                                             bias=col(m, bias["k"], i)).then_inc(unit_act, 1)

                def exponential(n):
                    b, h = divmod(n, NH)
                    wait_loop(act, sm_done, it * SM + (2 + n))
                    nc.scalar.activation(p[:, n % 3, :], sm[:, n % 3, :], ACT.Exp, scale=-1.0,
                                         bias=nmx[:, n % 4:n % 4 + 1],
                                         accum_out=rsum[:, b, h:h + 1]).then_inc(exp_done, 1)

                for u in plan[-1]:
                    unit(u)
                for s in range(STEPS + LAG_N):
                    if s < STEPS:
                        exponential(s)
                    if 0 <= s - LAG_T < STEPS and (s - LAG_T) % 2 == 1:
                        turned(act, nc.scalar.copy, it, s - LAG_T)
                    for u in plan.get(s, []):
                        unit(u)

        @block.vector
        def _(dve):
            dve.sem_inc(unit_dve, 1)
            dve.sem_inc(sm_done, 1)
            dve.sem_inc(t_out[0], 1)
            dve.sem_inc(o_out, 1)
            for ver in range(NQ):
                lo = ver * (C + 1)
                keep = col(m, q_of["keep"][ver])
                nc.vector.tensor_scalar(qcols[:, lo:lo + 1], keep, cfg.scale, None, ALU.mult).then_inc(setup_done, 1)
                nc.vector.tensor_scalar(qcols[:, lo + 1:lo + 1 + C], col(m, bias["q"], 0, C), keep, cfg.scale,
                                        ALU.mult, ALU.mult).then_inc(setup_done, 1)
            if cfg.latent:
                nc.vector.memset(mk[:, :, SKP:KEYS], 0.0).then_inc(pad_done, 1)
                dve.wait_ge(pad_done, 1)
            with dve.Fori(0, ITS) as it:
                def make_mask(b):
                    dve.wait_ge(staged[b], it * 48 + 48)
                    if mask["convert"]:
                        nc.vector.tensor_scalar(mk[:, b, 0:SKP], mraw[:, b, :], 0, MASKED, ALU.is_equal, ALU.mult
                                                ).then_inc(mask_made, 1)
                        dve.wait_ge(mask_made, it * 2 + (b + 1))

                def unit(u):
                    kind, b, i = u
                    if owner[u] != "dve":
                        return
                    dve.wait_ge(unit_done, it * len(order) + (number[u] + 1))
                    bank = ubank[number[u] % 2]
                    if kind == "v":
                        own_tiles = v_units[i]
                        ctx_tiles = [t for t in own_tiles if t < KT]
                        if ctx_tiles:
                            n = len(ctx_tiles)
                            nc.vector.tensor_copy(vb[:, b, ctx_tiles[0]:ctx_tiles[0] + n, :],
                                                  bank[0:KW, 0:n * VW].rearrange("p (t w) -> p t w", w=VW)
                                                  ).then_inc(unit_dve, 1)
                        if KT in own_tiles:
                            e = own_tiles.index(KT)
                            nc.vector.tensor_copy(vb[0:SQ, b, KT, :], bank[0:SQ, e * VW:(e + 1) * VW]
                                                  ).then_inc(unit_dve, 1)
                    else:
                        spread = col(m, bias["v"], 0, C).unsqueeze(2).broadcast_to((P, C, SQ))
                        nc.vector.tensor_tensor(m.hT[:, :, bass.ds((it * 2 + b) * SQ, SQ)],
                                                bank[:, 0:C * SQ].rearrange("p (c q) -> p c q", q=SQ), spread, ALU.add
                                                ).then_inc(unit_dve, 1)

                def mask_max(n):
                    b = n // NH
                    wait_loop(dve, s_done, it * SM + (n + 1))
                    if n >= 3:
                        wait_loop(dve, exp_done, it * SM + (2 + n - 3))
                    nc.vector.tensor_tensor_reduce(sm[:, n % 3, :], sbank[n % 3][0:SQ, 0:KEYS], mk[:, b, :], -1.0, 3.0e38,
                                                   ALU.add, ALU.min, nmx[:, n % 4:n % 4 + 1]).then_inc(sm_done, 1)

                def normalise(b):
                    dve.wait_ge(exp_done, it * SM + (1 + (b + 1) * NH))
                    nc.vector.reciprocal(rinv[:, b, :], rsum[:, b, :]).then_inc(recip_done, 1)
                    dve.wait_ge(recip_done, it * 2 + (b + 1))
                    dve.wait_ge(o_done, it * 2 + (b + 1))
                    view = lambda t: t.rearrange("p (h w) -> p h w", w=HW)
                    nc.vector.tensor_tensor(view(on[:, :]), view(obank[0:SQ, :]),
                                            rinv[:, b, :].unsqueeze(2).broadcast_to((SQ, NH, HW)), ALU.mult
                                            ).then_inc(o_out, 1)

                make_mask(0)
                for u in plan[-1]:
                    unit(u)
                for s in range(STEPS + LAG_N):
                    if s == NH:
                        make_mask(1)
                    if s < STEPS:
                        mask_max(s)
                    if 0 <= s - LAG_T < STEPS and (s - LAG_T) % 2 == 0:
                        turned(dve, nc.vector.tensor_copy, it, s - LAG_T)
                    for u in plan.get(s, []):
                        if u[0] != "ot":
                            unit(u)
                    if s in (NH - 1 + LAG_O, 2 * NH - 1 + LAG_O):
                        normalise(0 if s < 2 * NH else 1)
                    for u in plan.get(s, []):
                        if u[0] == "ot":
                            unit(u)


def phase_attn3(nc, m, ctx, tag, ctx_rows):
    sem = lambda n: ctx.enter_context(nc.semaphore(f"{n}_{tag}"))
    rows_loaded, s_done, t_done, c_done, ot_done = sem("rows"), sem("s"), sem("t"), sem("c"), sem("ot")
    max_done, exp_done, t_out, recip_done, c_out, ot_out, pads = (
        sem(n) for n in ("mx", "exp", "te", "rc", "ce", "oe", "pz"))
    with ExitStack() as own:
        sb = lambda n, s: own.enter_context(nc.sbuf_tensor(f"{n}_{tag}", s, F32))
        rows = sb("rows", [KW, B, KT, D])
        p, pt, on = sb("p", [SQ, 2, SKP]), sb("pt", [KW, 2, KT, SQ]), sb("on", [SQ, 2, D])
        nmx, rsum, rinv = sb("nmx", [SQ, B]), sb("rsum", [SQ, B]), sb("rinv", [SQ, B])
        bank = lambda n: [own.enter_context(nc.psum_tensor(f"{n}{i}_{tag}", [P, 512], F32)) for i in range(2)]
        sbank, tbank, cbank, obank = bank("s"), bank("t"), bank("c"), bank("o")
        block = own.enter_context(nc.Block())

        @block.sync
        def _(sp):
            sp.dma_start(rows[:, :, :, :], ctx_rows).then_inc(rows_loaded, 16)

        @block.tensor
        def _(pe):
            def scores(b):
                if b >= 2:
                    pe.wait_ge(exp_done, b - 1)
                for c in range(C):
                    at = b * SKP + 1
                    mm = pe.matmul(sbank[b % 2][0:SQ, 0:SK], m.aT[:, c, b * SQ:(b + 1) * SQ], m.ctxT[:, c, at:at + SK],
                                   start=(c == 0), stop=(c == C - 1))
                mm.then_inc(s_done, 1)

            def turn(b):
                pe.wait_ge(exp_done, b + 1)
                if b >= 2:
                    pe.wait_ge(t_out, b - 1)
                for t in range(KT):
                    mm = pe.transpose(tbank[b % 2][0:KW, t * SQ:(t + 1) * SQ], p[:, b % 2, t * KW:(t + 1) * KW],
                                      m.ident[0:SQ, 0:SQ])
                mm.then_inc(t_done, 1)

            def weigh(b):
                pe.wait_ge(t_out, b + 1)
                if b == 0:
                    pe.wait_ge(rows_loaded, 16)
                if b >= 2:
                    pe.wait_ge(c_out, b - 1)
                for t in range(KT):
                    mm = pe.matmul(cbank[b % 2][0:SQ, :], pt[:, b % 2, t, :], rows[:, b, t, :],
                                   start=(t == 0), stop=(t == KT - 1))
                mm.then_inc(c_done, 1)

            def turn_out(b):
                pe.wait_ge(c_out, b + 1)
                if b >= 2:
                    pe.wait_ge(ot_out, b - 1)
                for c in range(C):
                    mm = pe.transpose(obank[b % 2][:, c * SQ:(c + 1) * SQ], on[:, b % 2, c * P:(c + 1) * P],
                                      m.ident[0:SQ, 0:SQ])
                mm.then_inc(ot_done, 1)

            for b in range(B + 3):
                if b < B:
                    scores(b)
                for stage, lag in ((turn, 1), (weigh, 2), (turn_out, 3)):
                    if 0 <= b - lag < B:
                        stage(b - lag)

        @block.scalar
        def _(act):
            act.wait_ge(pads, 1)
            for b in range(B + 3):
                if b < B:
                    act.wait_ge(max_done, b + 1)
                    if b >= 2:
                        act.wait_ge(t_done, b - 1)
                    nc.scalar.activation(p[:, b % 2, 1:1 + SK], sbank[b % 2][0:SQ, 0:SK], ACT.Exp,
                                         bias=nmx[:, b:b + 1], accum_out=rsum[:, b:b + 1]).then_inc(exp_done, 1)
                if b >= 3:
                    act.wait_ge(ot_done, b - 2)
                    nc.scalar.copy(m.hT[:, :, (b - 3) * SQ:(b - 2) * SQ],
                                   obank[(b - 3) % 2][:, 0:C * SQ].rearrange("p (c q) -> p c q", q=SQ)
                                   ).then_inc(ot_out, 1)

        @block.vector
        def _(dve):
            for b in range(B + 2):
                if b < B:
                    dve.wait_ge(s_done, b + 1)
                    nc.vector.tensor_reduce(nmx[:, b:b + 1], sbank[b % 2][0:SQ, 0:SK], AX.X, ALU.max, negate=True
                                            ).then_inc(max_done, 1)
                if 0 <= b - 1 < B:
                    n = b - 1
                    dve.wait_ge(t_done, n + 1)
                    dve.wait_ge(exp_done, n + 1)
                    nc.vector.tensor_copy(pt[:, n % 2, :, :], tbank[n % 2][0:KW, 0:KT * SQ].rearrange(
                        "p (t q) -> p t q", q=SQ)).then_inc(t_out, 1)
                    nc.vector.reciprocal(rinv[:, n:n + 1], rsum[:, n:n + 1]).then_inc(recip_done, 1)
                if 0 <= b - 2 < B:
                    n = b - 2
                    dve.wait_ge(c_done, n + 1)
                    dve.wait_ge(recip_done, n + 1)
                    nc.vector.tensor_scalar(on[:, n % 2, :], cbank[n % 2][0:SQ, :], rinv[:, n:n + 1], None, ALU.mult
                                            ).then_inc(c_out, 1)

        @block.gpsimd
        def _(pool):
            nc.gpsimd.memset(p[:, :, :], 0.0).then_inc(pads, 1)


def phase_store(nc, m, ctx, out):
    stored = ctx.enter_context(nc.semaphore("stored"))
    with nc.Block() as block:
        @block.sync
        def _(sp):
            sp.dma_start(out, m.xT[:, :, :]).then_inc(stored, 16)
            sp.wait_ge(stored, 16)


def program(nc, d, out, until=99):
    m = Machine()
    with ExitStack() as ctx:
        sb = lambda n, s: ctx.enter_context(nc.sbuf_tensor(n, s, F32))
        m.cols, m.ident, m.mean_of = sb("cols", [P, NCOL]), sb("ident", [P, P]), sb("mean_of", [P, P])
        m.xT, m.hT = sb("xT", [P, C, NT]), sb("hT", [P, C, NT])
        sem = lambda n: ctx.enter_context(nc.semaphore(n))
        loaded = {n: [sem(f"loaded_{n}{i}") for i in range(2)] for n in ("a1", "a2", "m0", "m1")}
        ctx_loaded = sem("ctx_loaded")
        m.norm_marks = [Mark(sem("norm_" + n)) for n in
                        ("mean", "centre", "square", "var", "deviation", "rstd", "scaled", "affine", "bias")]
        m.dense_marks = [Mark(sem("dense_" + n)) for n in ("w", "product", "stored")]

        with ExitStack() as early:
            m.ctxT = early.enter_context(nc.sbuf_tensor("ctxT", [P, C, B * SKP], F32))
            m.wbuf = early.enter_context(nc.sbuf_tensor("wbuf", [P, 2, WROW], F32))
            m.rowbuf = early.enter_context(nc.sbuf_tensor("rowbuf", [1, 2, 2 * GW], F32))

            def first_groups(name, pack, rows=None):
                def load(sp):
                    for i in range(2):
                        load_group(sp, m, pack, i, i, loaded[name][i])
                        if rows is not None:
                            sp.dma_start(m.rowbuf[:, i, :], rows[i:i + 1, :]).then_inc(loaded[name][i], 16)
                return load

            def first_loads(sp):
                load_group(sp, m, d["w_a1"], 0, 0, loaded["a1"][0])
                sp.dma_start(m.rowbuf[:, 0, :], d["rows1"][0:1, :]).then_inc(loaded["a1"][0], 16)
                sp.dma_start(m.ctxT[:, :, :], d["ctxT"]).then_inc(ctx_loaded, 16)
                load_group(sp, m, d["w_a1"], 1, 1, loaded["a1"][1])
                sp.dma_start(m.rowbuf[:, 1, :], d["rows1"][1:2, :]).then_inc(loaded["a1"][1], 16)

            phase_load(nc, m, ctx, d, first_loads)
            phase_norm(nc, m, ctx, "n1", m.xT, m.hT, "eps5", "ln_s1", "ln_o1", after_bias="bo1",
                       preload=lambda sp: sp.wait_ge(ctx_loaded, 16))
            if until >= 1:
                phase_attn0(nc, m, ctx, "1", d["w_a1"], d["rows1"], loaded["a1"])
            if until >= 2:
                phase_norm(nc, m, ctx, "n2", m.xT, m.hT, "eps5", "ln_s2", "ln_o2", after_bias="bo2",
                           preload=first_groups("a2", d["w_a2"], d["rows2"]))
                phase_attn0(nc, m, ctx, "2", d["w_a2"], d["rows2"], loaded["a2"])
            if until >= 3:
                phase_norm(nc, m, ctx, "nm", m.xT, m.hT, "eps5", "ln_sm", "ln_om", preload=first_groups("m0", d["w_m0"]))
                phase_mlp(nc, m, ctx, "m0", d["w_m0"], loaded["m0"], ACT.Gelu, "fc1", "fc2")
        m.aT = sb("aT", [P, C, NT])

        def with_residual(bias_name):
            def evacuate(dst, bank, c, half):
                return nc.vector.scalar_tensor_tensor(dst, bank, col(m, bias_name, c), m.xT[:, c, half], ALU.add, ALU.add)
            return evacuate

        if until >= 4:
            phase_small(nc, m, ctx, "l1", Small(16, 32, C, True, 1.0 / 32),
                        {"wq": d["l1_wq"], "wk": d["l1_wk"], "wv": d["l1_wv"], "ctx": d["ctxB"]},
                        {"dtype": I32, "convert": True,
                         "source": lambda b: d["mask1"][bass.ds(b, 1), :].broadcast_to((SQ, SKP))},
                        {"versions": 1, "keep": ("one",), "parts": [(0, c, 0, 1 + c) for c in range(C)]},
                        lambda h: (32 * (h % 4), h // 4, 0, h // 4),
                        {"q": "l1_q", "k": "l1_k", "v": "l1_v", "value_column": lambda h: h * 32})
            phase_dense(nc, m, ctx, "l1o", d["l1_wo"], m.hT, m.aT, with_residual("l1_o"))
            with nc.sbuf_tensor("wbuf1", [P, 2, WROW], F32) as m.wbuf:
                phase_norm(nc, m, ctx, "l1n", m.aT, m.hT, "eps6", "l1_post", None, centred=False,
                           preload=first_groups("m1", d["w_m1"]))
                phase_mlp(nc, m, ctx, "m1", d["w_m1"], loaded["m1"], ACT.Gelu_apprx_tanh, "l1_m1", "l1_m2")
        if until >= 5:
            phase_small(nc, m, ctx, "l2", Small(32, 16, 1, False, 0.25),
                        {"wq": d["l2_wq"], "wk": d["l2_wk"], "wv": d["l2_wv"], "ctx": d["ctxB"]},
                        {"dtype": F32, "convert": False,
                         "source": lambda b: d["mask2"][bass.ds(b, 1), :, :].rearrange("a q k -> q (a k)")},
                        {"versions": 2, "keep": ("even", "odd"),
                         "parts": [(v, c, v * (C + 1), v * (C + 1) + 1 + c) for c in range(C) for v in range(2)]},
                        lambda h: (32 * (h // 8), 0, (h // 4) % 2, h % 4),
                        {"q": "l2_q", "k": "l2_k", "v": "l2_v", "value_column": lambda h: (h // 4) * 16})
            phase_dense(nc, m, ctx, "l2o", d["l2_wo"], m.hT, m.aT, with_residual("l2_o"))
            phase_norm(nc, m, ctx, "l2n", m.aT, m.xT, "eps6", "gamma", "beta")
        if until >= 6:
            m.ctxT = sb("ctxT3", [P, C, B * SKP])
            scale = float(D) ** -0.5
            phase_dense(nc, m, ctx, "l3q", d["l3_wq"], m.xT, m.hT,
                        lambda dst, bank, c, half: nc.vector.tensor_scalar(dst, bank, scale, None, ALU.mult),
                        preload=lambda sp: (sp.dma_start(m.ctxT[:, :, :], d["ctxT"]).then_inc(ctx_loaded, 16),
                                            sp.wait_ge(ctx_loaded, 32)))
            plain = lambda dst, bank, c, half: nc.vector.tensor_copy(dst, bank)
            phase_dense(nc, m, ctx, "l3k", d["l3_wk"], m.hT, m.aT, plain)
            phase_attn3(nc, m, ctx, "l3", d["ctxR"])
            phase_dense(nc, m, ctx, "l3v", d["l3_wv"], m.hT, m.aT, plain)
            phase_dense(nc, m, ctx, "l3o", d["l3_wo"], m.aT, m.xT,
                        lambda dst, bank, c, half: nc.vector.scalar_tensor_tensor(dst, bank, col(m, "alpha"), dst,
                                                                                  ALU.mult, ALU.add))
        phase_store(nc, m, ctx, out)


def _columns(vectors):
    import numpy as np
    return np.concatenate([np.asarray(v).reshape(-1, P).T for v in vectors], axis=1)


def _features_first(a, np):
    return np.ascontiguousarray(a.reshape(-1, P, a.shape[-1]).transpose(1, 0, 2))


def _pack_attention(wq, wk, wv, wo, np):
    per_group = lambda w: w.reshape(C, P, NG, GW).transpose(2, 1, 0, 3).reshape(NG, P, C * GW)
    out = wo.reshape(NG, HG, P, D).transpose(0, 2, 1, 3).reshape(NG, P, HG * D)
    return np.ascontiguousarray(np.concatenate([per_group(wq), per_group(wk), per_group(wv), out], axis=2))


def _pack_mlp(w1, w2, np):
    up = w1.reshape(C, P, NFG, FG * P).transpose(2, 1, 0, 3).reshape(NFG, P, C * FG * P)
    down = w2.reshape(NFG, FG, P, D).transpose(0, 2, 1, 3).reshape(NFG, P, FG * D)
    return np.ascontiguousarray(np.concatenate([up, down], axis=2))


def _layout_inputs(i):
    import numpy as np
    f = lambda n: np.asarray(i[n])
    x, ctx = f("x"), f("ctx_2048")
    a = {}
    a["x"] = _features_first(x.reshape(NT, D).T, np)
    padded = np.zeros((B, SKP, D), x.dtype)
    padded[:, 1:1 + SK] = ctx
    a["ctxT"] = _features_first(padded.reshape(B * SKP, D).T, np)
    a["ctxB"] = np.ascontiguousarray(a["ctxT"].reshape(P, C, B, SKP).transpose(2, 0, 1, 3))
    a["ctxR"] = np.ascontiguousarray(padded.reshape(B, KT, KW, D).transpose(2, 0, 1, 3))
    mask1 = np.zeros((B, SKP), f("mask_BxS2_ik0").dtype)
    mask1[:, 1:1 + SK] = f("mask_BxS2_ik0")
    a["mask1"] = mask1
    mask2 = np.full((B, SQ, SKP), MASKED, x.dtype)
    mask2[:, :, 1:1 + SK] = f("mask_Bx1xSxS2_ff0")[:, 0]
    a["mask2"] = mask2
    vectors = []
    for n in ("1", "2"):
        g = lambda k: f("L0_xattn_" + k + n)
        a["w_a" + n] = _pack_attention(g("wq"), g("wk"), g("wv"), g("wo"), np)
        a["rows" + n] = np.ascontiguousarray(
            np.concatenate([g("bias_v").reshape(NG, GW), g("bv").reshape(NG, GW)], axis=1))
        vectors += [f(f"L0_xattn_ln{n}_scale"), f(f"L0_xattn_ln{n}_offset"), g("bq"), g("bk"), g("bv"), g("bias_k"),
                    g("bo")]
    vectors += [f("L0_xattn_ln_mlp_scale"), f("L0_xattn_ln_mlp_offset"), f("L0_xattn_b_fc1"), f("L0_xattn_b_fc2")]
    a["w_m0"] = _pack_mlp(f("L0_xattn_w_fc1"), f("L0_xattn_w_fc2"), np)
    a["w_m1"] = _pack_mlp(f("L1_xattn_mlp_w1"), f("L1_xattn_mlp_w2"), np)
    kv, kvb = f("L1_xattn_kv_w").reshape(D, D, 2), f("L1_xattn_kv_b").reshape(D, 2)
    a["l1_wq"] = _features_first(f("L1_xattn_q_w"), np)
    a["l1_wk"] = _features_first(kv[:, :, 0], np)
    a["l1_wv"] = _features_first(kv[:, :, 1], np)
    a["l1_wo"] = _features_first(f("L1_xattn_out_w"), np)
    vectors += [f("L1_xattn_q_b"), kvb[:, 0], kvb[:, 1], f("L1_xattn_out_b"), f("L1_xattn_postnorm_w"),
                f("L1_xattn_mlp_b1"), f("L1_xattn_mlp_b2")]
    order = lambda w: w.reshape(-1, 8, 4, 16).transpose(0, 2, 1, 3).reshape(-1, D)
    a["l2_wq"] = _features_first(order(f("L2_xattn_Wq")), np)
    a["l2_wk"] = _features_first(f("L2_xattn_Wk"), np)
    a["l2_wv"] = _features_first(f("L2_xattn_Wv"), np)
    a["l2_wo"] = _features_first(f("L2_xattn_Wo"), np)
    bv = np.broadcast_to(f("L2_xattn_bv").reshape(8, 1, 16), (8, 4, 16)).reshape(D)
    vectors += [order(f("L2_xattn_bq").reshape(1, D)).reshape(D), f("L2_xattn_bk"), bv, f("L2_xattn_bo"),
                f("L2_xattn_gamma"), f("L2_xattn_beta")]
    a["l3_wq"] = _features_first(f("L3_xattn_w_q").T, np)
    a["l3_wk"] = _features_first(f("L3_xattn_w_k"), np)
    a["l3_wv"] = _features_first(f("L3_xattn_w_v").T, np)
    a["l3_wo"] = _features_first(f("L3_xattn_w_o").T, np)
    even = np.zeros((P,), x.dtype)
    even.reshape(4, 2, 16)[:, 0] = 1
    odd = np.zeros((P,), x.dtype)
    odd.reshape(4, 2, 16)[:, 1] = 1
    vectors += [np.full((P,), f("L3_xattn_alpha"), x.dtype), even, odd, np.ones((P,), x.dtype),
                np.full((P,), 1e-5, x.dtype), np.full((P,), 1e-6, x.dtype)]
    a["cols"] = np.ascontiguousarray(_columns(vectors))
    return a


UNTIL = 99


def kernel(**inputs):
    import concourse.bacc as _bacc
    import numpy as _np
    from concourse.bass_utils import run_bass_kernel_spmd as _run

    nc = _bacc.Bacc("TRN2", target_bir_lowering=False, num_devices=1)
    arrays = _layout_inputs(inputs)
    dram = {n: nc.dram_tensor(f"in_{n}", a.shape, mybir.dt.from_np(a.dtype), kind="ExternalInput").ap()
            for n, a in arrays.items()}
    out = nc.dram_tensor("out", (P, C, NT), F32, kind="ExternalOutput").ap()
    program(nc, dram, out, UNTIL)
    r = _run(nc, [{f"in_{n}": a for n, a in arrays.items()}], core_ids=[0])
    y = r.results[0]["out"]
    return _np.ascontiguousarray(y.transpose(1, 0, 2).reshape(D, NT).T.reshape(B, SQ, D))
```

```python
from contextlib import ExitStack

import concourse.bass as bass
from concourse import mybir

F32 = mybir.dt.float32
F32R = mybir.dt.float32r
I32 = mybir.dt.int32
ALU = mybir.AluOpType
ACT = mybir.ActivationFunctionType
AX = mybir.AxisListType

P = 128
B = 8
SQ = 112
NT = B * SQ
HALF = NT // 2
SK = 375
KT = 3
KW = 126
SKP = KT * KW
SKB = SK + 1
D = 512
C = D // P
H0 = 16
HG = 2
NG = H0 // HG
GW = HG * P
F = 2048
FG = 4
NFG = F // (FG * P)
WROW = 16 * P * HG
MASKED = -1.0e30

COLS = {}


def _layout():
    at = 0
    names = []
    for a in ("1", "2"):
        names += [("ln_s" + a, C), ("ln_o" + a, C), ("bq" + a, H0), ("bk" + a, H0), ("bv" + a, H0),
                  ("bias_k" + a, H0), ("bo" + a, C)]
    names += [("ln_sm", C), ("ln_om", C), ("fc1", F // P), ("fc2", C)]
    names += [("l1_q", C), ("l1_k", C), ("l1_v", C), ("l1_o", C), ("l1_post", C), ("l1_m1", F // P), ("l1_m2", C)]
    names += [("l2_q", C), ("l2_k", 1), ("l2_v", C), ("l2_o", C), ("gamma", C), ("beta", C)]
    names += [("alpha", 1), ("even", 1), ("odd", 1), ("one", 1), ("eps5", 1), ("eps6", 1)]
    for n, w in names:
        COLS[n] = (at, w)
        at += w
    return at


NCOL = _layout()


class Machine:
    pass


class Mark:

    def __init__(self, sem):
        self.sem, self.base = sem, 0


def col(m, name, i=0, n=1):
    at = COLS[name][0] + i
    return m.cols[:, at:at + n]


def wait_loop(eng, sem, value):
    eng.wait_ge(sem, value)
    eng.nop(nofuse=True)


def load_group(sp, m, pack, g, buf, sem):
    sp.dma_start(m.wbuf[:, buf, :], pack[g]).then_inc(sem, 16)


def phase_load(nc, m, ctx, d):
    ident_zero = ctx.enter_context(nc.semaphore("ident_zero"))
    constants_made = ctx.enter_context(nc.semaphore("constants_made"))
    inputs_loaded = ctx.enter_context(nc.semaphore("inputs_loaded"))
    with nc.Block() as block:
        @block.sync
        def _(sp):
            sp.dma_start(m.xT[:, :, :], d["x"]).then_inc(inputs_loaded, 16)
            sp.dma_start(m.cols[:, :], d["cols"]).then_inc(inputs_loaded, 16)
            sp.wait_ge(inputs_loaded, 32)

        @block.gpsimd
        def _(pool):
            nc.gpsimd.memset(m.ident[:, :], 0.0).then_inc(ident_zero, 1)
            nc.gpsimd.memset(m.mean_of[:, :], 1.0 / D).then_inc(constants_made, 1)
            pool.wait_ge(ident_zero, 1)
            nc.gpsimd.affine_select(out=m.ident[:, :], in_=m.ident[:, :], compare_op=ALU.not_equal, fill=1.0,
                                    base=0, pattern=[[-1, P]], channel_multiplier=1).then_inc(constants_made, 1)
            pool.wait_ge(constants_made, 2)


def phase_norm(nc, m, ctx, tag, src, dst, eps, scale, offset, centred=True, after_bias=None, preload=None,
               store=None):
    mean_done, centre_done, square_done, var_done, deviation_done, rstd_done, scaled, affine_done, bias_added = (
        m.norm_marks)
    with ExitStack() as own:
        sq = own.enter_context(nc.sbuf_tensor(f"sq_{tag}", [P, 2, C, HALF], F32))
        rstd = own.enter_context(nc.sbuf_tensor(f"rstd_{tag}", [P, 2, HALF], F32))
        ps = [own.enter_context(nc.psum_tensor(f"norm{i}_{tag}", [P, 512], F32)) for i in range(4)]
        block = own.enter_context(nc.Block())
        h = lambda t, s: t[:, :, s * HALF:(s + 1) * HALF]
        spread = lambda t: t.unsqueeze(1).broadcast_to((P, C, HALF))

        @block.tensor
        def _(pe):
            for s in range(2):
                if centred:
                    for c in range(C):
                        mm = pe.matmul(ps[s][:, 0:HALF], m.mean_of[:, :], src[:, c, s * HALF:(s + 1) * HALF],
                                       start=(c == 0), stop=(c == C - 1))
                    mm.then_inc(mean_done.sem, 1)
            for s in range(2):
                pe.wait_ge(square_done.sem, square_done.base + s + 1)
                for c in range(C):
                    mm = pe.matmul(ps[2 + s][:, 0:HALF], m.mean_of[:, :], sq[:, s, c, :],
                                   start=(c == 0), stop=(c == C - 1))
                mm.then_inc(var_done.sem, 1)

        @block.scalar
        def _(act):
            for s in range(2):
                if centred:
                    act.wait_ge(centre_done.sem, centre_done.base + s + 1)
                nc.scalar.activation(sq[:, s, :, :], h(dst if centred else src, s), ACT.Square
                                     ).then_inc(square_done.sem, 1)
            for s in range(2):
                act.wait_ge(var_done.sem, var_done.base + s + 1)
                nc.scalar.activation(rstd[:, s, :], ps[2 + s][:, 0:HALF], ACT.Sqrt, bias=col(m, eps)
                                     ).then_inc(deviation_done.sem, 1)
            for s in range(2):
                act.wait_ge(scaled.sem, scaled.base + s + 1)
                for c in range(C):
                    part = dst[:, c, s * HALF:(s + 1) * HALF]
                    if offset is None:
                        i = nc.scalar.activation(part, part, ACT.Identity, scale=col(m, scale, c))
                    else:
                        i = nc.scalar.activation(part, part, ACT.Identity, bias=col(m, offset, c),
                                                 scale=col(m, scale, c))
                    i.then_inc(affine_done.sem, 1)

        @block.vector
        def _(dve):
            if centred:
                for s in range(2):
                    dve.wait_ge(mean_done.sem, mean_done.base + s + 1)
                    nc.vector.tensor_tensor(h(dst, s), h(src, s), spread(ps[s][:, 0:HALF]), ALU.subtract
                                            ).then_inc(centre_done.sem, 1)
            for s in range(2):
                dve.wait_ge(deviation_done.sem, deviation_done.base + s + 1)
                nc.vector.reciprocal(rstd[:, s, :], rstd[:, s, :]).then_inc(rstd_done.sem, 1)
                dve.wait_ge(rstd_done.sem, rstd_done.base + s + 1)
                nc.vector.tensor_tensor(h(dst, s), h(dst if centred else src, s), spread(rstd[:, s, :]), ALU.mult
                                        ).then_inc(scaled.sem, 1)

        @block.gpsimd
        def _(pool):
            if after_bias is not None:
                pool.wait_ge(centre_done.sem, centre_done.base + 2)
                for c in range(C):
                    nc.gpsimd.tensor_scalar(src[:, c, :], src[:, c, :], col(m, after_bias, c), None, ALU.add
                                            ).then_inc(bias_added.sem, 1)

        @block.sync
        def _(sp):
            if preload is not None:
                preload(sp)
    for mark in (square_done, var_done, deviation_done, rstd_done, scaled) + (
            (mean_done, centre_done) if centred else ()):
        mark.base += 2


class Split:

    def __init__(self, make, name, shape):
        self.high, self.low = make(name + "_high", shape, F32R), make(name + "_low", shape, F32R)

    def at(self, *index):
        return self.high[index], self.low[index]


def products(pe, out, stationary, moving, first, last):
    (sh, sl), (mh, ml) = stationary, moving
    pe.matmul(out, sh, mh, start=first, stop=False)
    pe.matmul(out, sh, ml, start=False, stop=False)
    return pe.matmul(out, sl, mh, start=False, stop=last)


def phase_attn0(nc, m, ctx, tag, pack, rows, ctx_batches):
    a = tag
    sem = lambda n: ctx.enter_context(nc.semaphore(f"{n}_a{tag}"))
    c_loaded = [sem("craw0"), sem("craw1")]
    qkv_loaded, wo_loaded, row_loaded = sem("rqkv"), sem("rwo"), sem("rrow")
    w_high, w_split, h_high, h_split, c_high, c_split = (sem(n) for n in ("wh", "ws", "hh", "hs", "ch", "cs"))
    kq_done, v_done, s_done, t_done, o_done = (sem(n) for n in ("kq", "v", "s", "t", "o"))
    kq_high, v_high, t_high, o_high, exp_done = (sem(n) for n in ("kqh", "vh", "th", "oh", "exp"))
    kq_out, v_out, t_out, o_out = (sem(n) for n in ("kqe", "ve", "te", "oe"))
    max_done, nmx_done, recip_done = (sem(n) for n in ("mx", "nmx", "rc"))
    vb_step, row_used, v_fixed, p_normed, pads_zero = (sem(n) for n in ("vb", "ru", "vf", "pn", "pz"))
    scale = float(P) ** -0.5
    NB = B // 2
    KQ, VO, N2, OO = HG * NB + HG + 2, 2 * NB + 2, HG * NB, HG * NB
    with ExitStack() as own:
        sb = lambda n, s, dt=F32: own.enter_context(nc.sbuf_tensor(f"{n}_a{tag}", s, dt))
        c, w = Split(sb, "c", [P, C, NB * SKP]), Split(sb, "w", [P, WROW])
        craw, raw_qkv, raw_wo = sb("craw", [P, 2, C, SKP]), sb("raw_qkv", [P, 3 * C * GW]), sb("raw_wo", [P, HG * D])
        h, q, ot = Split(sb, "h", [P, C, HALF]), Split(sb, "q", [P, HG, HALF]), Split(sb, "ot", [P, HG, HALF])
        kT, v, pt = Split(sb, "kT", [P, HG, SKB]), Split(sb, "v", [KW, 2, KT, GW]), Split(sb, "pt", [KW, HG, KT, SQ])
        p = sb("p", [SQ, HG, SKP])
        mx, nmx = sb("mx", [SQ, 2, HG]), sb("nmx", [SQ, 2, HG])
        rsum, rinv = sb("rsum", [SQ, 2, HG]), sb("rinv", [SQ, 2, HG])
        row, vrow, vrow_split = sb("row", [1, 2 * GW]), sb("vrow", [1, GW]), Split(sb, "vrs", [1, GW])
        ps = lambda n: own.enter_context(nc.psum_tensor(f"{n}_a{tag}", [P, 512], F32))
        kbank, vbank, sbank = [ps("k0"), ps("k1")], [ps("v0"), ps("v1")], [ps("s0"), ps("s1")]
        tbank, obank = ps("t"), ps("o")
        KIND = C * GW
        part = lambda lo, n=P: w.at(slice(None), slice(lo, lo + n))
        wq = lambda k, j: part(k * GW + j * P)
        wk = lambda k, j: part(KIND + k * GW + j * P)
        wv = lambda k: part(2 * KIND + k * GW, GW)
        wo = lambda j, o: part(3 * KIND + j * D + o * P)
        block = own.enter_context(nc.Block())

        @block.sync
        def _(sp):
            def load_next(g, n, wo_too=True):
                wait_loop(sp, w_split, n * 4 + 3)
                sp.dma_start(raw_qkv[:, :], pack[g, :, 0:3 * KIND].rearrange("a p w -> p (a w)")
                             ).then_inc(qkv_loaded, 16)
                if wo_too:
                    wait_loop(sp, w_split, n * 4 + 4)
                    sp.dma_start(raw_wo[:, :], pack[g, :, 3 * KIND:WROW].rearrange("a p w -> p (a w)")
                                 ).then_inc(wo_loaded, 16)
                    wait_loop(sp, row_used, n + 1)
                    sp.dma_start(row[:, :], rows[g, :]).then_inc(row_loaded, 16)

            first = bass.ds(0, 1)
            sp.dma_start(raw_qkv[:, :], pack[first, :, 0:3 * KIND].rearrange("a p w -> p (a w)")
                         ).then_inc(qkv_loaded, 16)
            for half in range(2):
                for b in range(NB):
                    n = half * NB + b
                    if n >= 2:
                        sp.wait_ge(c_split, n - 1)
                    sp.dma_start(craw[:, b % 2, :, :], ctx_batches[n]).then_inc(c_loaded[b % 2], 16)
                if half == 0:
                    sp.dma_start(raw_wo[:, :], pack[first, :, 3 * KIND:WROW].rearrange("a p w -> p (a w)")
                                 ).then_inc(wo_loaded, 16)
                    sp.dma_start(row[:, :], rows[0:1, :]).then_inc(row_loaded, 16)
                with sp.Fori(0, NG - 1) as it:
                    load_next(bass.ds(it + 1, 1), it + NG * half)
                load_next(first, NG * (half + 1) - 1, wo_too=(half == 0))

        @block.tensor
        def _(pe):
            for half in range(2):
                KQ0, Q0 = half * (HG + NG * KQ), HG
                kq0, v0, n0, oo0, g0 = KQ0 + Q0, half * NG * VO, half * NG * N2, half * NG * OO, half * NG

                def q_proj(j, at, unit):
                    pe.wait_ge(kq_out, at + (1 + unit - 1))
                    bank = kbank[unit % 2]
                    for k in range(C):
                        mm = products(pe, bank[:, 0:HALF], wq(k, j), h.at(slice(None), k), k == 0, k == C - 1)
                    mm.then_inc(kq_done, 1)

                pe.wait_ge(h_split, half + 1)
                pe.wait_ge(w_split, g0 * 4 + 1)
                for j in range(HG):
                    q_proj(j, 0, KQ0 + j)
                with pe.Fori(0, NG) as it:
                    def bank_of_kq(u):
                        pe.wait_ge(kq_out, it * KQ + (1 + kq0 + u - 1))
                        return kbank[u % 2]

                    def bank_of_v(u):
                        pe.wait_ge(v_out, it * VO + (1 + v0 + u - 1))
                        return vbank[u % 2]

                    def k_proj(b, j):
                        bank = bank_of_kq(HG * b + j)
                        for k in range(C):
                            mm = products(pe, bank[:, 0:SKB], wk(k, j),
                                          c.at(slice(None), k, slice(b * SKP, b * SKP + SKB)), k == 0, k == C - 1)
                        mm.then_inc(kq_done, 1)

                    def v_proj(b, n):
                        bank = bank_of_v(2 * b + n)
                        for i, t in enumerate(([0, 1], [2])[n]):
                            for k in range(C):
                                at = b * SKP + t * KW
                                mm = products(pe, bank[0:KW, i * GW:(i + 1) * GW],
                                              c.at(slice(None), k, slice(at, at + KW)), wv(k), k == 0, k == C - 1)
                        mm.then_inc(v_done, 1)

                    def scores(b, j):
                        n = HG * b + j
                        pe.wait_ge(kq_out, it * KQ + (1 + kq0 + n + 1))
                        pe.wait_ge(exp_done, it * N2 + (1 + n0 + max(n - 1, 0)))
                        products(pe, sbank[j][0:SQ, 0:SKB], q.at(slice(None), j, slice(b * SQ, (b + 1) * SQ)),
                                 kT.at(slice(None), j), True, True).then_inc(s_done, 1)

                    def turn(b, j):
                        n = HG * b + j
                        pe.wait_ge(p_normed, it * N2 + (n0 + n + 1))
                        pe.wait_ge(t_out, it * N2 + (1 + n0 + n))
                        for t in range(KT):
                            mm = pe.transpose(tbank[0:KW, t * SQ:(t + 1) * SQ], p[:, j, t * KW:(t + 1) * KW],
                                              m.ident[0:SQ, 0:SQ])
                        mm.then_inc(t_done, 1)

                    def weigh(b, j):
                        n = HG * b + j
                        pe.wait_ge(t_out, it * N2 + (2 + n0 + n))
                        if j == 0:
                            pe.wait_ge(v_fixed, it * NB + (half * NG * NB + b + 1))
                            pe.wait_ge(v_out, it * VO + (1 + v0 + 2 * (b + 1)))
                            pe.wait_ge(o_out, it * OO + (1 + oo0 + HG * b))
                        for t in range(KT):
                            mm = products(pe, obank[:, j * SQ:(j + 1) * SQ],
                                          v.at(slice(None), b % 2, t, slice(j * P, (j + 1) * P)),
                                          pt.at(slice(None), j, t), t == 0, t == KT - 1)
                        if j == HG - 1:
                            mm.then_inc(o_done, 1)

                    def o_proj(o, lo, hi):
                        bank = (vbank if o < 2 else kbank)[o % 2]
                        if lo == 0:
                            (bank_of_v if o < 2 else bank_of_kq)(2 * NB + o if o < 2 else HG * NB + HG + o - 2)
                        pe.wait_ge(o_out, it * OO + (1 + oo0 + HG * hi))
                        cols = slice(lo * SQ, hi * SQ)
                        for j in range(HG):
                            mm = products(pe, bank[:, cols], wo(j, o), ot.at(slice(None), j, cols), j == 0, j == HG - 1)
                        if hi == NB:
                            mm.then_inc(v_done if o < 2 else kq_done, 1)

                    pe.wait_ge(w_split, it * 4 + (g0 * 4 + 3))
                    for b in range(NB):
                        pe.wait_ge(c_split, half * NB + b + 1)
                        k_proj(b, 0)
                        v_proj(b, 0)
                        if b:
                            turn(b - 1, 0)
                        k_proj(b, 1)
                        if b:
                            weigh(b - 1, 0)
                            turn(b - 1, 1)
                        v_proj(b, 1)
                        scores(b, 0)
                        if b:
                            weigh(b - 1, 1)
                        scores(b, 1)
                    last = NB - 1
                    pe.wait_ge(w_split, it * 4 + (g0 * 4 + 5))
                    q_proj(0, it * KQ, kq0 + HG * NB)
                    o_proj(0, 0, last)
                    o_proj(1, 0, last)
                    turn(last, 0)
                    q_proj(1, it * KQ, kq0 + HG * NB + 1)
                    weigh(last, 0)
                    turn(last, 1)
                    o_proj(2, 0, last)
                    weigh(last, 1)
                    o_proj(3, 0, last)
                    for o in (2, 3, 0, 1):
                        o_proj(o, last, NB)

        def split_units(eng, half, do):
            if half == 0:
                for kind in range(3):
                    do.weight(0, kind, True)
            do.hidden(half)
            do.context(half, 0)
            for j in range(HG):
                do.query(None, j)
            for b in range(1, NB):
                do.context(half, b)
            with eng.Fori(0, NG) as it:
                last = NB - 1
                for b in range(NB):
                    do.key(it, b, 0)
                    do.value(it, b, 0)
                    if b:
                        do.turned(it, b - 1, 0)
                    do.key(it, b, 1)
                    if b:
                        do.turned(it, b - 1, 1)
                    do.value(it, b, 1)
                    do.maximum(it, b, 0)
                    if b:
                        do.attended(it, b - 1)
                    do.maximum(it, b, 1)
                    do.softmax(it, b)
                    if b == 1:
                        do.weight(it, 3)
                    if b == 2:
                        do.weight(it, 0)
                do.weight(it, 1)
                do.query(it, 0)
                do.turned(it, last, 0)
                do.query(it, 1)
                do.turned(it, last, 1)
                do.attended(it, last)
                do.weight(it, 2)
                do.output(it)

        class Work:

            def __init__(self, half):
                self.half, self.g0 = half, half * NG
                self.kq0, self.v0, self.n0 = half * (HG + NG * KQ) + HG, half * NG * VO, half * NG * N2

            def kq(self, it, b, j):
                return (self.kq0 - HG + j + 1) if it is None else it * KQ + (self.kq0 + HG * b + j + 1)

            def v(self, it, b, n):
                return it * VO + (self.v0 + 2 * b + n + 1)

            def n(self, it, b, j):
                return it * N2 + (self.n0 + HG * b + j + 1)

            def o(self, it, b):
                return it * NB + (self.half * NG * NB + b + 1)

            def w(self, it, kind, first=False):
                return kind if first else it * 4 + (self.g0 * 4 + (3 if kind == 3 else 4 + kind))

            def column(self, it, name, j):
                at = COLS[name + a][0] + j
                return m.cols[:, at:at + 1] if it is None else m.cols[:, bass.ds(it * HG + at, 1)]

            def query_column(self, it, j):
                at = COLS["bq" + a][0] + j
                return m.cols[:, at:at + 1] if it is None else m.cols[:, bass.ds(it * HG + (at + HG), 1)]

            @staticmethod
            def weights(kind):
                if kind == 3:
                    return slice(3 * KIND, WROW), raw_wo[:, :]
                return slice(kind * KIND, (kind + 1) * KIND), raw_qkv[:, kind * KIND:(kind + 1) * KIND]

        @block.scalar
        def _(act):
            class High(Work):
                def weight(self, it, kind, first=False):
                    if kind == 3:
                        wait_loop(act, wo_loaded, it * 16 + (self.g0 + 1) * 16)
                    elif kind == 0 and first:
                        act.wait_ge(qkv_loaded, 16)
                    elif kind == 0:
                        wait_loop(act, qkv_loaded, it * 16 + (self.g0 + 2) * 16)
                    to, src = self.weights(kind)
                    nc.scalar.copy(w.high[:, to], src).then_inc(w_high, 1)

                def hidden(self, half):
                    nc.scalar.copy(h.high[:, :, :], m.hT[:, :, half * HALF:(half + 1) * HALF]).then_inc(h_high, 1)

                def context(self, half, b):
                    act.wait_ge(c_loaded[b % 2], 16 * (half * NB // 2 + b // 2 + 1))
                    nc.scalar.copy(c.high[:, :, b * SKP:(b + 1) * SKP], craw[:, b % 2, :, :]).then_inc(c_high, 1)

                def query(self, it, j):
                    wait_loop(act, kq_done, self.kq(it, NB, j))
                    nc.scalar.activation(q.high[:, j, :], kbank[j][:, 0:HALF], ACT.Identity,
                                         bias=self.query_column(it, j)).then_inc(kq_high, 1)

                def key(self, it, b, j):
                    wait_loop(act, kq_done, self.kq(it, b, j))
                    if b == 0:
                        nc.scalar.activation(kT.high[:, j, 0:1], self.column(it, "bias_k", j), ACT.Identity
                                             ).then_inc(kq_high, 1)
                    nc.scalar.activation(kT.high[:, j, 1:SKB], kbank[j][:, 1:SKB], ACT.Identity,
                                         bias=self.column(it, "bk", j)).then_inc(kq_high, 1)

                def value(self, it, b, n):
                    wait_loop(act, v_done, self.v(it, b, n))
                    wide = (2 - n) * GW
                    nc.scalar.copy(v.high[:, b % 2, 2 * n:2 * n + 2 - n, :],
                                   vbank[n][0:KW, 0:wide].rearrange("p (t w) -> p t w", w=GW)).then_inc(v_high, 1)

                def turned(self, it, b, j):
                    wait_loop(act, t_done, self.n(it, b, j))
                    nc.scalar.copy(pt.high[:, j, :, :], tbank[0:KW, 0:KT * SQ].rearrange("p (t q) -> p t q", q=SQ)
                                   ).then_inc(t_high, 1)

                def attended(self, it, b):
                    wait_loop(act, o_done, self.o(it, b))
                    for j in range(HG):
                        nc.scalar.activation(ot.high[:, j, b * SQ:(b + 1) * SQ], obank[:, j * SQ:(j + 1) * SQ],
                                             ACT.Identity, bias=self.column(it, "bv", j)).then_inc(o_high, 1)

                def softmax(self, it, b):
                    wait_loop(act, nmx_done, self.o(it, b))
                    for j in range(HG):
                        nc.scalar.activation(p[:, j, 0:SKB], sbank[j][0:SQ, 0:SKB], ACT.Exp, scale=scale,
                                             bias=nmx[:, b % 2, j:j + 1],
                                             accum_out=rsum[:, b % 2, j:j + 1]).then_inc(exp_done, 1)

                def maximum(self, it, b, j):
                    pass

                def output(self, it):
                    pass

            act.sem_inc(exp_done, 1)
            act.wait_ge(pads_zero, 1)
            for half in range(2):
                split_units(act, half, High(half))

        @block.vector
        def _(dve):
            def rest(out, bank, bias, high):
                if bias is None:
                    return nc.vector.tensor_tensor(out, bank, high, ALU.subtract)
                return nc.vector.scalar_tensor_tensor(out, bank, bias, high, ALU.add, ALU.subtract)

            class Low(Work):
                def keys_high(self, it, b, j):
                    per = HG * NB + HG + HG
                    base = self.half * (HG + NG * per) + HG
                    if it is None:
                        return base - HG + j + 1
                    return it * per + (base + (2 * (j + 1) if b == 0 else HG + HG * b + j + 1))

                def weight(self, it, kind, first=False):
                    dve.wait_ge(w_high, self.w(it, kind, first) + 1)
                    to, src = self.weights(kind)
                    nc.vector.tensor_tensor(w.low[:, to], src, w.high[:, to], ALU.subtract).then_inc(w_split, 1)

                def hidden(self, half):
                    dve.wait_ge(h_high, half + 1)
                    nc.vector.tensor_tensor(h.low[:, :, :], m.hT[:, :, half * HALF:(half + 1) * HALF],
                                            h.high[:, :, :], ALU.subtract).then_inc(h_split, 1)

                def context(self, half, b):
                    dve.wait_ge(c_high, half * NB + b + 1)
                    cols = slice(b * SKP, (b + 1) * SKP)
                    nc.vector.tensor_tensor(c.low[:, :, cols], craw[:, b % 2, :, :], c.high[:, :, cols],
                                            ALU.subtract).then_inc(c_split, 1)

                def query(self, it, j):
                    dve.wait_ge(kq_high, self.keys_high(it, NB, j))
                    rest(q.low[:, j, :], kbank[j][:, 0:HALF], self.query_column(it, j), q.high[:, j, :]
                         ).then_inc(kq_out, 1)

                def key(self, it, b, j):
                    dve.wait_ge(kq_high, self.keys_high(it, b, j))
                    if b == 0:
                        nc.vector.tensor_tensor(kT.low[:, j, 0:1], self.column(it, "bias_k", j),
                                                kT.high[:, j, 0:1], ALU.subtract)
                    rest(kT.low[:, j, 1:SKB], kbank[j][:, 1:SKB], self.column(it, "bk", j), kT.high[:, j, 1:SKB]
                         ).then_inc(kq_out, 1)

                def value(self, it, b, n):
                    dve.wait_ge(v_high, it * (2 * NB) + (self.half * NG * 2 * NB + 2 * b + n + 1))
                    wide = (2 - n) * GW
                    rest(v.low[:, b % 2, 2 * n:2 * n + 2 - n, :],
                         vbank[n][0:KW, 0:wide].rearrange("p (t w) -> p t w", w=GW), None,
                         v.high[:, b % 2, 2 * n:2 * n + 2 - n, :]).then_inc(v_out, 1)

                def turned(self, it, b, j):
                    dve.wait_ge(t_high, self.n(it, b, j))
                    rest(pt.low[:, j, :, :], tbank[0:KW, 0:KT * SQ].rearrange("p (t q) -> p t q", q=SQ), None,
                         pt.high[:, j, :, :]).then_inc(t_out, 1)

                def attended(self, it, b):
                    dve.wait_ge(o_high, self.n(it, b, HG - 1))
                    for j in range(HG):
                        cols = slice(b * SQ, (b + 1) * SQ)
                        rest(ot.low[:, j, cols], obank[:, j * SQ:(j + 1) * SQ], self.column(it, "bv", j),
                             ot.high[:, j, cols]).then_inc(o_out, 1)

                def maximum(self, it, b, j):
                    dve.wait_ge(s_done, self.n(it, b, j))
                    nc.vector.tensor_reduce(mx[:, b % 2, j:j + 1], sbank[j][0:SQ, 0:SKB], AX.X, ALU.max
                                            ).then_inc(max_done, 1)

                def softmax(self, it, b):
                    dve.wait_ge(max_done, self.n(it, b, HG - 1))
                    nc.vector.tensor_scalar(nmx[:, b % 2, :], mx[:, b % 2, :], -scale, None, ALU.mult
                                            ).then_inc(nmx_done, 1)
                    dve.wait_ge(exp_done, self.n(it, b, HG - 1) + 1)
                    nc.vector.reciprocal(rinv[:, b % 2, :], rsum[:, b % 2, :]).then_inc(recip_done, 1)

                def output(self, it):
                    for o in (2, 3, 0, 1):
                        if o < 2:
                            dve.wait_ge(v_done, it * VO + (self.v0 + 2 * NB + o + 1))
                        else:
                            dve.wait_ge(kq_done, it * KQ + (self.kq0 + HG * NB + HG + o - 1))
                        to = m.xT[:, o, self.half * HALF:(self.half + 1) * HALF]
                        bank = (vbank if o < 2 else kbank)[o % 2]
                        nc.vector.tensor_tensor(to, to, bank[:, 0:HALF], ALU.add).then_inc(v_out if o < 2 else kq_out, 1)

            for s in (kq_out, v_out, t_out, o_out):
                dve.sem_inc(s, 1)
            for half in range(2):
                split_units(dve, half, Low(half))

        @block.gpsimd
        def _(pool):
            nc.gpsimd.memset(p[:, :, SKB:SKP], 0.0).then_inc(pads_zero, 1)
            for half in range(2):
                g0, v0, n0 = half * NG, half * NG * VO, half * NG * N2
                with pool.Fori(0, NG) as it:
                    wait_loop(pool, row_loaded, it * 16 + 16 * (g0 + 1))
                    nc.gpsimd.tensor_tensor(vrow[:, :], row[:, 0:GW], row[:, GW:2 * GW], ALU.subtract
                                            ).then_inc(row_used, 1)
                    wait_loop(pool, row_used, it + (g0 + 1))
                    nc.gpsimd.tensor_copy(vrow_split.high[:, :], vrow[:, :]).then_inc(vb_step, 1)
                    wait_loop(pool, vb_step, it * 2 + (g0 * 2 + 1))
                    nc.gpsimd.tensor_tensor(vrow_split.low[:, :], vrow[:, :], vrow_split.high[:, :], ALU.subtract
                                            ).then_inc(vb_step, 1)
                    wait_loop(pool, vb_step, it * 2 + (g0 * 2 + 2))
                    for b in range(NB):
                        wait_loop(pool, v_out, it * VO + (1 + v0 + 2 * b + 1))
                        nc.gpsimd.tensor_copy(v.high[0:1, b % 2, 0, :], vrow_split.high[:, :])
                        nc.gpsimd.tensor_copy(v.low[0:1, b % 2, 0, :], vrow_split.low[:, :]).then_inc(v_fixed, 1)
                        wait_loop(pool, recip_done, it * NB + (half * NG * NB + b + 1))
                        for j in range(HG):
                            nc.gpsimd.tensor_scalar(p[:, j, 0:SKB], p[:, j, 0:SKB], rinv[:, b % 2, j:j + 1], None,
                                                    ALU.mult).then_inc(p_normed, 1)


def phase_mlp(nc, m, ctx, tag, pack, loaded, func, b1, b2):
    sem = lambda n: ctx.enter_context(nc.semaphore(f"{n}_{tag}"))
    up_done, act_done, down_done, added, bias_added = (sem(n) for n in ("up", "gelu", "down", "add", "b2"))
    ITS = NFG // 2
    UP, DOWN = 2 * FG, 2 * C
    with ExitStack() as own:
        g = own.enter_context(nc.sbuf_tensor(f"g_{tag}", [P, 2, FG, HALF], F32))
        ps = lambda n: own.enter_context(nc.psum_tensor(f"{n}_{tag}", [P, 512], F32))
        up, down = [ps(f"up{i}") for i in range(4)], [ps(f"down{i}") for i in range(4)]
        w1 = lambda i, k, f: m.wbuf[:, i, (k * FG + f) * P:(k * FG + f + 1) * P]
        w2 = lambda i, f, c: m.wbuf[:, i, C * FG * P + f * D + c * P:C * FG * P + f * D + (c + 1) * P]
        block = own.enter_context(nc.Block())

        @block.sync
        def _(sp):
            with sp.Fori(0, ITS - 1) as it:
                for i in range(2):
                    wait_loop(sp, added, it * (2 * DOWN) + (1 + (i + 1) * DOWN))
                    sp.dma_start(m.wbuf[:, i, :], pack[bass.ds(it * 2 + (2 + i), 1), :, :].rearrange("a p w -> p (a w)")
                                 ).then_inc(loaded[i], 16)

        @block.tensor
        def _(pe):
            with pe.Fori(0, ITS) as it:
                for i in range(2):
                    pe.wait_ge(loaded[i], it * 16 + 16)
                    for s in range(2):
                        for f in range(FG):
                            n = i * UP + s * FG + f
                            pe.wait_ge(act_done, it * (2 * UP) + (1 + max(n - 3, 0)))
                            for k in range(C):
                                mm = pe.matmul(up[f][:, 0:HALF], w1(i, k, f), m.hT[:, k, s * HALF:(s + 1) * HALF],
                                               start=(k == 0), stop=(k == C - 1))
                            mm.then_inc(up_done, 1)
                    for s in range(2):
                        pe.wait_ge(act_done, it * (2 * UP) + (1 + i * UP + (s + 1) * FG))
                        for c in range(C):
                            n = i * DOWN + s * C + c
                            pe.wait_ge(added, it * (2 * DOWN) + (1 + max(n - 3, 0)))
                            for f in range(FG):
                                mm = pe.matmul(down[c][:, 0:HALF], w2(i, f, c), g[:, s, f, :],
                                               start=(f == 0), stop=(f == FG - 1))
                            mm.then_inc(down_done, 1)

        @block.scalar
        def _(act):
            act.sem_inc(act_done, 1)
            with act.Fori(0, ITS) as it:
                for i in range(2):
                    for s in range(2):
                        for f in range(FG):
                            wait_loop(act, up_done, it * (2 * UP) + (i * UP + s * FG + f + 1))
                            at = COLS[b1][0] + i * FG + f
                            nc.scalar.activation(g[:, s, f, :], up[f][:, 0:HALF], func,
                                                 bias=m.cols[:, bass.ds(it * (2 * FG) + at, 1)]).then_inc(act_done, 1)

        @block.vector
        def _(dve):
            dve.sem_inc(added, 1)
            dve.wait_ge(bias_added, C)
            with dve.Fori(0, ITS) as it:
                for i in range(2):
                    for s in range(2):
                        for c in range(C):
                            dve.wait_ge(down_done, it * (2 * DOWN) + (i * DOWN + s * C + c + 1))
                            part = m.xT[:, c, s * HALF:(s + 1) * HALF]
                            nc.vector.tensor_tensor(part, part, down[c][:, 0:HALF], ALU.add).then_inc(added, 1)

        @block.gpsimd
        def _(pool):
            for c in range(C):
                nc.gpsimd.tensor_scalar(m.xT[:, c, :], m.xT[:, c, :], col(m, b2, c), None, ALU.add
                                        ).then_inc(bias_added, 1)


def phase_dense(nc, m, ctx, tag, w, src, dst, evacuate, preload=None):
    w_loaded, product_done, stored = m.dense_marks
    with ExitStack() as own:
        wt = own.enter_context(nc.sbuf_tensor(f"w_{tag}", [P, C, D], F32))
        bank = [own.enter_context(nc.psum_tensor(f"b{i}_{tag}", [P, 512], F32)) for i in range(4)]
        block = own.enter_context(nc.Block())

        @block.sync
        def _(sp):
            sp.dma_start(wt[:, :, :], w).then_inc(w_loaded.sem, 16)
            if preload is not None:
                preload(sp)

        @block.tensor
        def _(pe):
            pe.wait_ge(w_loaded.sem, w_loaded.base + 16)
            for s in range(2):
                for c in range(C):
                    n = s * C + c
                    if n >= 4:
                        pe.wait_ge(stored.sem, stored.base + n - 3)
                    for k in range(C):
                        mm = pe.matmul(bank[n % 4][:, 0:HALF], wt[:, k, c * P:(c + 1) * P],
                                       src[:, k, s * HALF:(s + 1) * HALF], start=(k == 0), stop=(k == C - 1))
                    mm.then_inc(product_done.sem, 1)

        @block.vector
        def _(dve):
            for s in range(2):
                for c in range(C):
                    n = s * C + c
                    dve.wait_ge(product_done.sem, product_done.base + n + 1)
                    evacuate(dst[:, c, s * HALF:(s + 1) * HALF], bank[n % 4][:, 0:HALF], c,
                             slice(s * HALF, (s + 1) * HALF)).then_inc(stored.sem, 1)
    for mark, n in ((w_loaded, 16), (product_done, 2 * C), (stored, 2 * C)):
        mark.base += n


class Small:

    def __init__(self, heads, width, k_chunks, latent, scale, keep, value_stride, value_at, head):
        self.heads, self.width, self.k_chunks, self.latent, self.scale = heads, width, k_chunks, latent, scale
        self.keep = keep
        self.keys = SKP + (SQ if latent else 0)
        self.tiles = KT + (1 if latent else 0)
        self.v_width = k_chunks * P
        self.stride, self.at = value_stride, value_at
        self.head = head


class Head:

    def __init__(self, row, k_chunk, version, q_chunk, value, out_chunk, position, first=True, last=True):
        self.row, self.k_chunk, self.version, self.q_chunk = row, k_chunk, version, q_chunk
        self.value = value
        self.out_chunk, self.position = out_chunk, position
        self.first, self.last = first, last


def wide_head(n):
    return Head(32 * (n % 4), n // 4, 0, n // 4, 32 * n, n // 4, n)


def narrow_head(n):
    r, x = n % 4, n // 4
    g = 2 * r + x // 4
    return Head(32 * r, 0, x // 4, x % 4, 48 * g + (16 if x % 2 == 0 else 0), x // 2,
                (x // 2) * 8 + r * 2 + x % 2, x % 2 == 0, x % 2 == 1)


def phase_small(nc, m, ctx, tag, cfg, d, mask, bias):
    sem = lambda n: ctx.enter_context(nc.semaphore(f"{n}_{tag}"))
    w_loaded, staged = sem("w"), [sem(f"staged{i}") for i in range(2)]
    unit_done, s_done, t_done, o_done = sem("unit"), sem("s"), sem("t"), sem("o")
    unit_out, q_high, k_high, q_split = sem("uo"), sem("qh"), sem("kh"), sem("qs")
    sm_done, exp_done, o_out, divided = sem("sm"), sem("exp"), sem("oo"), sem("dv")
    t_out = [sem(f"te{i}") for i in range(2)]
    recip_done, spread_done, mask_made, setup_done, pad_done = sem("rc"), sem("sd"), sem("mk"), sem("su"), sem("pd")
    NH, NC, NTL, KEYS, VW, HW = cfg.heads, cfg.k_chunks, cfg.tiles, cfg.keys, cfg.v_width, cfg.width
    NQ, ITS = len(cfg.keep), B // 2
    heads = [cfg.head(n) for n in range(NH)]
    tiles = [(i * KW, KW) for i in range(KT)] + ([(SKP, SQ)] if cfg.latent else [])
    per_bank = 512 // VW
    v_units = [list(range(i, min(i + per_bank, NTL))) for i in range(0, NTL, per_bank)]
    units = lambda b: ([("q", b, 0)] + [("k", b, c) for c in range(min(NC, 2))] +
                       [("v", b, u) for u in range(len(v_units))] + [("k", b, c) for c in range(2, NC)])
    plan = {-1: units(0), NH - 3: units(1)}
    LAG_T, LAG_O, LAG_S, LAG_R = 2, 3, 2, 4
    STEPS = 2 * NH
    for b in range(2):
        plan[(b + 1) * NH - 1 + LAG_R] = [("r", b, 0)]
    order = [u for s in sorted(plan) for u in plan[s]]
    number = {u: n for n, u in enumerate(order)}
    NU = len(order)
    with ExitStack() as own:
        sb = lambda n, s, dt=F32: own.enter_context(nc.sbuf_tensor(f"{n}_{tag}", s, dt))
        wq, wk, wv = sb("wq", [P, C, D]), sb("wk", [P, C, NC * P]), sb("wv", [P, C, VW])
        cb = sb("cb", [P, 2, C, SKP])
        xb = sb("xb", [P, 2, C, SQ])
        qf, q = sb("qf", [P, NQ, C, SQ]), Split(sb, "q", [P, 2, NQ, C, SQ])
        kb = Split(sb, "kb", [P, 2, NC, KEYS])
        vb = sb("vb", [KW, 2, NTL, VW // cfg.width * cfg.stride])
        mraw = sb("mraw", [SQ, 2, SKP], mask["dtype"])
        mk = sb("mk", [SQ, 2, KEYS]) if mask["convert"] else mraw
        sm = sb("sm", [SQ, 3, KEYS])
        p = sb("p", [SQ, 3, KEYS])
        pt = sb("pt", [KW, 2, 4, NTL, SQ])
        nmx, rsum, rwide = sb("nmx", [SQ, 4]), sb("rsum", [SQ, 2, NH]), sb("rwide", [SQ, D])
        rinv = sb("rinv", [SQ, NH])
        rT = sb("rT", [P, C * SQ])
        qcols = sb("qcols", [P, NQ * (C + 1)])
        ps = lambda n: own.enter_context(nc.psum_tensor(f"{n}_{tag}", [P, 512], F32))
        ubank, sbank, tbank, obank = [ps("u0"), ps("u1")], [ps(f"s{i}") for i in range(3)], [ps("t0"), ps("t1")], ps("o")
        block = own.enter_context(nc.Block())
        SM, TE = 2 * NH, NH

        @block.sync
        def _(sp):
            for dst, name in ((wq, "wq"), (wk, "wk"), (wv, "wv")):
                sp.dma_start(dst[:, :, :], d[name]).then_inc(w_loaded, 16)

            def stage(b, i):
                sp.dma_start(cb[:, i, :, :], d["ctx"][bass.ds(b, 1), :, :, :].rearrange("a p c w -> p (a c) w")
                             ).then_inc(staged[i], 16)
                sp.dma_start(xb[:, i, :, :], m.xT[:, :, bass.ds(b * SQ, SQ)]).then_inc(staged[i], 16)
                sp.dma_start(mraw[:, i, :], mask["source"](b)).then_inc(staged[i], 16)

            for i in range(2):
                stage(i, i)
            with sp.Fori(0, ITS - 1) as it:
                for i in range(2):
                    wait_loop(sp, unit_out, it * NU + (1 + number["r", i, 0] + 1))
                    stage(it * 2 + (2 + i), i)

        @block.tensor
        def _(pe):
            pe.wait_ge(w_loaded, 48)
            with pe.Fori(0, ITS) as it:
                def unit(u):
                    kind, b, i = u
                    n = number[u]
                    pe.wait_ge(unit_out, it * NU + (1 + max(n - 1, 0)))
                    bank = ubank[n % 2]
                    if kind == "q":
                        pe.wait_ge(staged[b], it * 48 + 48)
                        for c in range(C):
                            for k in range(C):
                                mm = pe.matmul(bank[:, c * SQ:(c + 1) * SQ], wq[:, k, c * P:(c + 1) * P], xb[:, b, k, :],
                                               start=(k == 0), stop=(k == C - 1))
                    elif kind == "k":
                        for k in range(C):
                            mm = pe.matmul(bank[:, 0:SKP], wk[:, k, i * P:(i + 1) * P], cb[:, b, k, :],
                                           start=(k == 0), stop=(k == C - 1))
                        if cfg.latent:
                            for k in range(C):
                                mm = pe.matmul(bank[:, SKP:KEYS], wk[:, k, i * P:(i + 1) * P], xb[:, b, k, :],
                                               start=(k == 0), stop=(k == C - 1))
                    elif kind == "v":
                        for e, t in enumerate(v_units[i]):
                            lo, w = tiles[t]
                            for k in range(C):
                                lhs = cb[:, b, k, lo:lo + w] if t < KT else xb[:, b, k, :]
                                mm = pe.matmul(bank[0:w, e * VW:(e + 1) * VW], lhs, wv[:, k, :],
                                               start=(k == 0), stop=(k == C - 1))
                    else:
                        pe.wait_ge(spread_done, it * 2 + (b + 1))
                        for c in range(C):
                            mm = pe.transpose(bank[:, c * SQ:(c + 1) * SQ], rwide[:, c * P:(c + 1) * P],
                                              m.ident[0:SQ, 0:SQ])
                    mm.then_inc(unit_done, 1)

                def scores(n):
                    b, h = divmod(n, NH)
                    at = heads[h]
                    if h == 0:
                        pe.wait_ge(q_split, it * 2 + (b + 1))
                    if h % (NH // NC) == 0:
                        pe.wait_ge(unit_out, it * NU + (1 + number["k", b, at.k_chunk] + 1))
                    pe.wait_ge(sm_done, it * SM + (1 + max(n - 2, 0)))
                    rows = slice(at.row, at.row + 32)
                    products(pe, sbank[n % 3][0:SQ, 0:KEYS], q.at(rows, b, at.version, at.q_chunk),
                             kb.at(rows, b, at.k_chunk), True, True).then_inc(s_done, 1)

                def turn(n):
                    pe.wait_ge(exp_done, it * SM + (2 + n))
                    pe.wait_ge(t_out[n % 2], it * TE + (1 + n // 2))
                    for t, (lo, w) in enumerate(tiles):
                        mm = pe.transpose(tbank[n % 2][0:w, t * SQ:(t + 1) * SQ], p[:, n % 3, lo:lo + w],
                                          m.ident[0:SQ, 0:SQ])
                    mm.then_inc(t_done, 1)

                def weigh(four):
                    n = 4 * four
                    b, h = divmod(n, NH)
                    for i in range(2):
                        pe.wait_ge(t_out[i], it * TE + (2 + (n + 2) // 2))
                    if h == 0:
                        pe.wait_ge(unit_out, it * NU + (1 + number["v", b, len(v_units) - 1] + 1))
                        pe.wait_ge(o_out, it * 2 + (1 + b))
                    for t, (_, w) in enumerate(tiles):
                        for i in range(4):
                            at = heads[h + i]
                            mm = pe.matmul(obank[32 * i:32 * i + 32, at.out_chunk * SQ:(at.out_chunk + 1) * SQ],
                                           vb[0:w, b, t, at.value:at.value + 32], pt[0:w, four % 2, i, t, :],
                                           start=(at.first and t == 0), stop=(at.last and t == NTL - 1))
                    if h == NH - 4:
                        mm.then_inc(o_done, 1)

                for u in plan[-1]:
                    unit(u)
                for s in range(STEPS + LAG_R):
                    if s < STEPS:
                        scores(s)
                    if 0 <= s - LAG_T < STEPS:
                        turn(s - LAG_T)
                    for u in plan.get(s, []):
                        unit(u)
                    if LAG_O <= s < STEPS + LAG_O and (s - LAG_O) % 4 == 3:
                        weigh((s - LAG_O) // 4)

        def turned(eng, copy, it, n):
            wait_loop(eng, t_done, it * SM + (n + 1))
            src = tbank[n % 2][:, 0:NTL * SQ].rearrange("p (t q) -> p t q", q=SQ)
            to = pt[:, (n // 4) % 2, n % 4, :, :]
            i = copy(to[:, 0:KT, :], src[0:KW, 0:KT, :])
            if cfg.latent:
                i = copy(to[0:SQ, KT, :], src[0:SQ, KT, :])
            i.then_inc(t_out[n % 2], 1)

        @block.scalar
        def _(act):
            act.sem_inc(exp_done, 1)
            act.sem_inc(t_out[1], 1)
            with act.Fori(0, ITS) as it:
                def unit(u):
                    kind, b, i = u
                    if kind == "q":
                        wait_loop(act, unit_out, it * NU + (1 + number[u] + 1))
                        nc.scalar.copy(q.high[:, b, :, :, :], qf[:, :, :, :]).then_inc(q_high, 1)
                    if kind == "k":
                        wait_loop(act, unit_done, it * NU + (number[u] + 1))
                        nc.scalar.activation(kb.high[:, b, i, :], ubank[number[u] % 2][:, 0:KEYS], ACT.Identity,
                                             bias=col(m, bias["k"], i)).then_inc(k_high, 1)

                def exponential(n):
                    b, h = divmod(n, NH)
                    at = heads[h].position
                    wait_loop(act, sm_done, it * SM + (2 + n))
                    nc.scalar.activation(p[:, n % 3, :], sm[:, n % 3, :], ACT.Exp, scale=-1.0,
                                         bias=nmx[:, n % 4:n % 4 + 1],
                                         accum_out=rsum[:, b, at:at + 1]).then_inc(exp_done, 1)

                for u in plan[-1]:
                    unit(u)
                for s in range(STEPS + LAG_R):
                    if s < STEPS:
                        exponential(s)
                    if 0 <= s - LAG_T < STEPS and (s - LAG_T) % 2 == 1:
                        turned(act, nc.scalar.copy, it, s - LAG_T)
                    for u in plan.get(s, []):
                        unit(u)

        @block.vector
        def _(dve):
            for s in (unit_out, sm_done, t_out[0], o_out):
                dve.sem_inc(s, 1)
            for ver in range(NQ):
                lo = ver * (C + 1)
                keep = col(m, cfg.keep[ver])
                nc.vector.tensor_scalar(qcols[:, lo:lo + 1], keep, cfg.scale, None, ALU.mult).then_inc(setup_done, 1)
                nc.vector.tensor_scalar(qcols[:, lo + 1:lo + 1 + C], col(m, bias["q"], 0, C), keep, cfg.scale,
                                        ALU.mult, ALU.mult).then_inc(setup_done, 1)
            dve.wait_ge(setup_done, 2 * NQ)
            if cfg.latent:
                nc.vector.memset(mk[:, :, SKP:KEYS], 0.0).then_inc(pad_done, 1)
                dve.wait_ge(pad_done, 1)
            if cfg.stride > cfg.width:
                nc.vector.memset(vb[:, :, :, :], 0.0).then_inc(pad_done, 1)
                dve.wait_ge(pad_done, 1)
            with dve.Fori(0, ITS) as it:
                K_PER, k_number = 2 * NC, {u: n for n, u in enumerate(u for u in order if u[0] == "k")}

                def make_mask(b):
                    dve.wait_ge(staged[b], it * 48 + 48)
                    if mask["convert"]:
                        nc.vector.tensor_scalar(mk[:, b, 0:SKP], mraw[:, b, :], 0, MASKED, ALU.is_equal, ALU.mult
                                                ).then_inc(mask_made, 1)
                        dve.wait_ge(mask_made, it * 2 + (b + 1))

                def unit(u):
                    kind, b, i = u
                    dve.wait_ge(unit_done, it * NU + (number[u] + 1))
                    bank = ubank[number[u] % 2]
                    chunks = bank[:, 0:C * SQ].rearrange("p (c q) -> p c q", q=SQ)
                    if kind == "q":
                        for ver in range(NQ):
                            lo = ver * (C + 1)
                            shift = qcols[:, lo + 1:lo + 1 + C].unsqueeze(2).broadcast_to((P, C, SQ))
                            step = nc.vector.scalar_tensor_tensor(qf[:, ver, :, :], chunks, qcols[:, lo:lo + 1], shift,
                                                                  ALU.mult, ALU.add)
                        step.then_inc(unit_out, 1)
                    elif kind == "k":
                        dve.wait_ge(k_high, it * K_PER + (k_number[u] + 1))
                        nc.vector.scalar_tensor_tensor(kb.low[:, b, i, :], bank[:, 0:KEYS], col(m, bias["k"], i),
                                                       kb.high[:, b, i, :], ALU.add, ALU.subtract
                                                       ).then_inc(unit_out, 1)
                        if i == 0:
                            dve.wait_ge(q_high, it * 2 + (b + 1))
                            nc.vector.tensor_tensor(q.low[:, b, :, :, :], qf[:, :, :, :], q.high[:, b, :, :, :],
                                                    ALU.subtract).then_inc(q_split, 1)
                    elif kind == "v":
                        own_tiles = v_units[i]
                        n = len([t for t in own_tiles if t < KT])
                        lo = own_tiles[0]
                        if n:
                            to = vb[:, b, lo:lo + n, :].rearrange("p t (g s) -> p t g s", s=cfg.stride)
                            step = nc.vector.tensor_copy(to[:, :, :, cfg.at:cfg.at + HW],
                                                         bank[0:KW, 0:n * VW].rearrange("p (t g w) -> p t g w", t=n, w=HW))
                        if KT in own_tiles:
                            e = own_tiles.index(KT)
                            step = nc.vector.tensor_copy(vb[0:SQ, b, KT, :], bank[0:SQ, e * VW:(e + 1) * VW])
                        step.then_inc(unit_out, 1)
                    else:
                        nc.vector.tensor_copy(rT[:, :], bank[:, 0:C * SQ]).then_inc(unit_out, 1)

                def mask_max(n):
                    b = n // NH
                    wait_loop(dve, s_done, it * SM + (n + 1))
                    if n >= 3:
                        wait_loop(dve, exp_done, it * SM + (2 + n - 3))
                    nc.vector.tensor_tensor_reduce(sm[:, n % 3, :], sbank[n % 3][0:SQ, 0:KEYS], mk[:, b, :], -1.0, 3.0e38,
                                                   ALU.add, ALU.min, nmx[:, n % 4:n % 4 + 1]).then_inc(sm_done, 1)

                def spread(b):
                    dve.wait_ge(exp_done, it * SM + (1 + (b + 1) * NH))
                    nc.vector.reciprocal(rinv[:, :], rsum[:, b, :]).then_inc(recip_done, 1)
                    dve.wait_ge(recip_done, it * 2 + (b + 1))
                    nc.vector.tensor_copy(rwide[:, :].rearrange("p (h w) -> p h w", w=HW),
                                          rinv[:, :].unsqueeze(2).broadcast_to((SQ, NH, HW))).then_inc(spread_done, 1)

                def divide(b):
                    dve.wait_ge(unit_out, it * NU + (1 + number["r", b, 0] + 1))
                    dve.wait_ge(o_done, it * 2 + (b + 1))
                    view = lambda t: t.rearrange("p (c q) -> p c q", q=SQ)
                    to = m.hT[:, :, bass.ds((it * 2 + b) * SQ, SQ)]
                    nc.vector.tensor_tensor(to, view(obank[:, 0:C * SQ]), view(rT[:, :]), ALU.mult).then_inc(o_out, 1)
                    dve.wait_ge(o_out, it * 2 + (b + 2))
                    shift = col(m, bias["v"], 0, C).unsqueeze(2).broadcast_to((P, C, SQ))
                    nc.vector.tensor_tensor(to, to, shift, ALU.add).then_inc(divided, 1)

                make_mask(0)
                for u in plan[-1]:
                    unit(u)
                for s in range(STEPS + LAG_R):
                    if s == NH:
                        make_mask(1)
                    if s < STEPS:
                        mask_max(s)
                    if 0 <= s - LAG_T < STEPS and (s - LAG_T) % 2 == 0:
                        turned(dve, nc.vector.tensor_copy, it, s - LAG_T)
                    if s in (NH - 1 + LAG_S, 2 * NH - 1 + LAG_S):
                        spread(0 if s < 2 * NH else 1)
                    for u in plan.get(s, []):
                        unit(u)
                    if s in (NH - 1 + LAG_R, 2 * NH - 1 + LAG_R):
                        divide(0 if s < 2 * NH else 1)
            dve.wait_ge(divided, B)


def phase_attn3(nc, m, ctx, tag, ctx_rows):
    sem = lambda n: ctx.enter_context(nc.semaphore(f"{n}_{tag}"))
    rows_loaded, s_done, t_done, c_done, ot_done = sem("rows"), sem("s"), sem("t"), sem("c"), sem("ot")
    max_done, exp_done, t_out, recip_done, c_out, ot_out, pads = (
        sem(n) for n in ("mx", "exp", "te", "rc", "ce", "oe", "pz"))
    with ExitStack() as own:
        sb = lambda n, s: own.enter_context(nc.sbuf_tensor(f"{n}_{tag}", s, F32))
        rows = sb("rows", [KW, B, KT, D])
        p, pt, on = sb("p", [SQ, 2, SKP]), sb("pt", [KW, 2, KT, SQ]), sb("on", [SQ, 2, D])
        nmx, rsum, rinv = sb("nmx", [SQ, B]), sb("rsum", [SQ, B]), sb("rinv", [SQ, B])
        bank = lambda n: [own.enter_context(nc.psum_tensor(f"{n}{i}_{tag}", [P, 512], F32)) for i in range(2)]
        sbank, tbank, cbank, obank = bank("s"), bank("t"), bank("c"), bank("o")
        block = own.enter_context(nc.Block())

        @block.sync
        def _(sp):
            sp.dma_start(rows[:, :, :, :], ctx_rows).then_inc(rows_loaded, 16)

        @block.tensor
        def _(pe):
            def scores(b):
                if b >= 2:
                    pe.wait_ge(exp_done, b - 1)
                for c in range(C):
                    at = b * SKP + 1
                    mm = pe.matmul(sbank[b % 2][0:SQ, 0:SK], m.aT[:, c, b * SQ:(b + 1) * SQ], m.ctxT[:, c, at:at + SK],
                                   start=(c == 0), stop=(c == C - 1))
                mm.then_inc(s_done, 1)

            def turn(b):
                pe.wait_ge(exp_done, b + 1)
                if b >= 2:
                    pe.wait_ge(t_out, b - 1)
                for t in range(KT):
                    mm = pe.transpose(tbank[b % 2][0:KW, t * SQ:(t + 1) * SQ], p[:, b % 2, t * KW:(t + 1) * KW],
                                      m.ident[0:SQ, 0:SQ])
                mm.then_inc(t_done, 1)

            def weigh(b):
                pe.wait_ge(t_out, b + 1)
                if b == 0:
                    pe.wait_ge(rows_loaded, 16)
                if b >= 2:
                    pe.wait_ge(c_out, b - 1)
                for t in range(KT):
                    mm = pe.matmul(cbank[b % 2][0:SQ, :], pt[:, b % 2, t, :], rows[:, b, t, :],
                                   start=(t == 0), stop=(t == KT - 1))
                mm.then_inc(c_done, 1)

            def turn_out(b):
                pe.wait_ge(c_out, b + 1)
                if b >= 2:
                    pe.wait_ge(ot_out, b - 1)
                for c in range(C):
                    mm = pe.transpose(obank[b % 2][:, c * SQ:(c + 1) * SQ], on[:, b % 2, c * P:(c + 1) * P],
                                      m.ident[0:SQ, 0:SQ])
                mm.then_inc(ot_done, 1)

            for b in range(B + 3):
                if b < B:
                    scores(b)
                for stage, lag in ((turn, 1), (weigh, 2), (turn_out, 3)):
                    if 0 <= b - lag < B:
                        stage(b - lag)

        @block.scalar
        def _(act):
            act.wait_ge(pads, 1)
            for b in range(B + 3):
                if b < B:
                    act.wait_ge(max_done, b + 1)
                    if b >= 2:
                        act.wait_ge(t_done, b - 1)
                    nc.scalar.activation(p[:, b % 2, 1:1 + SK], sbank[b % 2][0:SQ, 0:SK], ACT.Exp,
                                         bias=nmx[:, b:b + 1], accum_out=rsum[:, b:b + 1]).then_inc(exp_done, 1)
                if b >= 3:
                    act.wait_ge(ot_done, b - 2)
                    nc.scalar.copy(m.hT[:, :, (b - 3) * SQ:(b - 2) * SQ],
                                   obank[(b - 3) % 2][:, 0:C * SQ].rearrange("p (c q) -> p c q", q=SQ)
                                   ).then_inc(ot_out, 1)

        @block.vector
        def _(dve):
            for b in range(B + 2):
                if b < B:
                    dve.wait_ge(s_done, b + 1)
                    nc.vector.tensor_reduce(nmx[:, b:b + 1], sbank[b % 2][0:SQ, 0:SK], AX.X, ALU.max, negate=True
                                            ).then_inc(max_done, 1)
                if 0 <= b - 1 < B:
                    n = b - 1
                    dve.wait_ge(t_done, n + 1)
                    dve.wait_ge(exp_done, n + 1)
                    nc.vector.tensor_copy(pt[:, n % 2, :, :], tbank[n % 2][0:KW, 0:KT * SQ].rearrange(
                        "p (t q) -> p t q", q=SQ)).then_inc(t_out, 1)
                    nc.vector.reciprocal(rinv[:, n:n + 1], rsum[:, n:n + 1]).then_inc(recip_done, 1)
                if 0 <= b - 2 < B:
                    n = b - 2
                    dve.wait_ge(c_done, n + 1)
                    dve.wait_ge(recip_done, n + 1)
                    nc.vector.tensor_scalar(on[:, n % 2, :], cbank[n % 2][0:SQ, :], rinv[:, n:n + 1], None, ALU.mult
                                            ).then_inc(c_out, 1)

        @block.gpsimd
        def _(pool):
            nc.gpsimd.memset(p[:, :, :], 0.0).then_inc(pads, 1)


def phase_store(nc, m, ctx, out):
    stored = ctx.enter_context(nc.semaphore("stored"))
    with nc.Block() as block:
        @block.sync
        def _(sp):
            sp.dma_start(out, m.xT[:, :, :]).then_inc(stored, 16)
            sp.wait_ge(stored, 16)


def program(nc, d, out, until=99):
    m = Machine()
    with ExitStack() as ctx:
        sb = lambda n, s: ctx.enter_context(nc.sbuf_tensor(n, s, F32))
        m.cols, m.ident, m.mean_of = sb("cols", [P, NCOL]), sb("ident", [P, P]), sb("mean_of", [P, P])
        m.xT, m.hT = sb("xT", [P, C, NT]), sb("hT", [P, C, NT])
        sem = lambda n: ctx.enter_context(nc.semaphore(n))
        loaded = {n: [sem(f"loaded_{n}{i}") for i in range(2)] for n in ("m0", "m1")}
        ctx_loaded = sem("ctx_loaded")
        m.norm_marks = [Mark(sem("norm_" + n)) for n in
                        ("mean", "centre", "square", "var", "deviation", "rstd", "scaled", "affine", "bias")]
        m.dense_marks = [Mark(sem("dense_" + n)) for n in ("w", "product", "stored")]

        def first_groups(name, pack):
            def load(sp):
                for i in range(2):
                    load_group(sp, m, pack, i, i, loaded[name][i])
            return load

        phase_load(nc, m, ctx, d)
        phase_norm(nc, m, ctx, "n1", m.xT, m.hT, "eps5", "ln_s1", "ln_o1", after_bias="bo1")
        if until >= 1:
            phase_attn0(nc, m, ctx, "1", d["w_a1"], d["rows1"], d["ctxB"])
        if until >= 2:
            phase_norm(nc, m, ctx, "n2", m.xT, m.hT, "eps5", "ln_s2", "ln_o2", after_bias="bo2")
            phase_attn0(nc, m, ctx, "2", d["w_a2"], d["rows2"], d["ctxB"])
        with nc.sbuf_tensor("wbuf0", [P, 2, WROW], F32) as m.wbuf:
            if until >= 3:
                phase_norm(nc, m, ctx, "nm", m.xT, m.hT, "eps5", "ln_sm", "ln_om", preload=first_groups("m0", d["w_m0"]))
                phase_mlp(nc, m, ctx, "m0", d["w_m0"], loaded["m0"], ACT.Gelu, "fc1", "fc2")
        m.aT = sb("aT", [P, C, NT])

        def with_residual(bias_name):
            def evacuate(dst, bank, c, half):
                return nc.vector.scalar_tensor_tensor(dst, bank, col(m, bias_name, c), m.xT[:, c, half], ALU.add, ALU.add)
            return evacuate

        if until >= 4:
            phase_small(nc, m, ctx, "l1", Small(16, 32, C, True, 1.0 / 32, ("one",), 32, 0, wide_head),
                        {"wq": d["l1_wq"], "wk": d["l1_wk"], "wv": d["l1_wv"], "ctx": d["ctxB"]},
                        {"dtype": I32, "convert": True,
                         "source": lambda b: d["mask1"][bass.ds(b, 1), :].broadcast_to((SQ, SKP))},
                        {"q": "l1_q", "k": "l1_k", "v": "l1_v"})
            phase_dense(nc, m, ctx, "l1o", d["l1_wo"], m.hT, m.aT, with_residual("l1_o"))
            with nc.sbuf_tensor("wbuf1", [P, 2, WROW], F32) as m.wbuf:
                phase_norm(nc, m, ctx, "l1n", m.aT, m.hT, "eps6", "l1_post", None, centred=False,
                           preload=first_groups("m1", d["w_m1"]))
                phase_mlp(nc, m, ctx, "m1", d["w_m1"], loaded["m1"], ACT.Gelu_apprx_tanh, "l1_m1", "l1_m2")
        if until >= 5:
            phase_small(nc, m, ctx, "l2", Small(32, 16, 1, False, 0.25, ("even", "odd"), 48, 16, narrow_head),
                        {"wq": d["l2_wq"], "wk": d["l2_wk"], "wv": d["l2_wv"], "ctx": d["ctxB"]},
                        {"dtype": F32, "convert": False,
                         "source": lambda b: d["mask2"][bass.ds(b, 1), :, :].rearrange("a q k -> q (a k)")},
                        {"q": "l2_q", "k": "l2_k", "v": "l2_v"})
            phase_dense(nc, m, ctx, "l2o", d["l2_wo"], m.hT, m.aT, with_residual("l2_o"))
            phase_norm(nc, m, ctx, "l2n", m.aT, m.xT, "eps6", "gamma", "beta")
        if until >= 6:
            m.ctxT = sb("ctxT3", [P, C, B * SKP])
            scale = float(D) ** -0.5
            phase_dense(nc, m, ctx, "l3q", d["l3_wq"], m.xT, m.hT,
                        lambda dst, bank, c, half: nc.vector.tensor_scalar(dst, bank, scale, None, ALU.mult),
                        preload=lambda sp: (sp.dma_start(m.ctxT[:, :, :], d["ctxT"]).then_inc(ctx_loaded, 16),
                                            sp.wait_ge(ctx_loaded, 16)))
            plain = lambda dst, bank, c, half: nc.vector.tensor_copy(dst, bank)
            phase_dense(nc, m, ctx, "l3k", d["l3_wk"], m.hT, m.aT, plain)
            phase_attn3(nc, m, ctx, "l3", d["ctxR"])
            phase_dense(nc, m, ctx, "l3v", d["l3_wv"], m.hT, m.aT, plain)
            phase_dense(nc, m, ctx, "l3o", d["l3_wo"], m.aT, m.xT,
                        lambda dst, bank, c, half: nc.vector.scalar_tensor_tensor(dst, bank, col(m, "alpha"), dst,
                                                                                  ALU.mult, ALU.add))
        phase_store(nc, m, ctx, out)


def _columns(vectors):
    import numpy as np
    return np.concatenate([np.asarray(v).reshape(-1, P).T for v in vectors], axis=1)


def _features_first(a, np):
    return np.ascontiguousarray(a.reshape(-1, P, a.shape[-1]).transpose(1, 0, 2))


def _pack_attention(wq, wk, wv, wo, np):
    per_group = lambda w: w.reshape(C, P, NG, GW).transpose(2, 1, 0, 3).reshape(NG, P, C * GW)
    out = wo.reshape(NG, HG, P, D).transpose(0, 2, 1, 3).reshape(NG, P, HG * D)
    return np.ascontiguousarray(np.concatenate([per_group(wq), per_group(wk), per_group(wv), out], axis=2))


def _pack_mlp(w1, w2, np):
    up = w1.reshape(C, P, NFG, FG * P).transpose(2, 1, 0, 3).reshape(NFG, P, C * FG * P)
    down = w2.reshape(NFG, FG, P, D).transpose(0, 2, 1, 3).reshape(NFG, P, FG * D)
    return np.ascontiguousarray(np.concatenate([up, down], axis=2))


def _layout_inputs(i):
    import numpy as np
    f = lambda n: np.asarray(i[n])
    x, ctx = f("x"), f("ctx_2048")
    a = {}
    a["x"] = _features_first(x.reshape(NT, D).T, np)
    padded = np.zeros((B, SKP, D), x.dtype)
    padded[:, 1:1 + SK] = ctx
    a["ctxT"] = _features_first(padded.reshape(B * SKP, D).T, np)
    a["ctxB"] = np.ascontiguousarray(a["ctxT"].reshape(P, C, B, SKP).transpose(2, 0, 1, 3))
    a["ctxR"] = np.ascontiguousarray(padded.reshape(B, KT, KW, D).transpose(2, 0, 1, 3))
    mask1 = np.zeros((B, SKP), f("mask_BxS2_ik0").dtype)
    mask1[:, 1:1 + SK] = f("mask_BxS2_ik0")
    a["mask1"] = mask1
    mask2 = np.full((B, SQ, SKP), MASKED, x.dtype)
    mask2[:, :, 1:1 + SK] = f("mask_Bx1xSxS2_ff0")[:, 0]
    a["mask2"] = mask2
    vectors = []
    for n in ("1", "2"):
        g = lambda k: f("L0_xattn_" + k + n)
        a["w_a" + n] = _pack_attention(g("wq"), g("wk"), g("wv"), g("wo"), np)
        a["rows" + n] = np.ascontiguousarray(
            np.concatenate([g("bias_v").reshape(NG, GW), g("bv").reshape(NG, GW)], axis=1))
        vectors += [f(f"L0_xattn_ln{n}_scale"), f(f"L0_xattn_ln{n}_offset"), g("bq"), g("bk"), g("bv"), g("bias_k"),
                    g("bo")]
    vectors += [f("L0_xattn_ln_mlp_scale"), f("L0_xattn_ln_mlp_offset"), f("L0_xattn_b_fc1"), f("L0_xattn_b_fc2")]
    a["w_m0"] = _pack_mlp(f("L0_xattn_w_fc1"), f("L0_xattn_w_fc2"), np)
    a["w_m1"] = _pack_mlp(f("L1_xattn_mlp_w1"), f("L1_xattn_mlp_w2"), np)
    kv, kvb = f("L1_xattn_kv_w").reshape(D, D, 2), f("L1_xattn_kv_b").reshape(D, 2)
    a["l1_wq"] = _features_first(f("L1_xattn_q_w"), np)
    a["l1_wk"] = _features_first(kv[:, :, 0], np)
    a["l1_wv"] = _features_first(kv[:, :, 1], np)
    a["l1_wo"] = _features_first(f("L1_xattn_out_w"), np)
    vectors += [f("L1_xattn_q_b"), kvb[:, 0], kvb[:, 1], f("L1_xattn_out_b"), f("L1_xattn_postnorm_w"),
                f("L1_xattn_mlp_b1"), f("L1_xattn_mlp_b2")]
    order = lambda w: w.reshape(-1, 8, 4, 16).transpose(0, 2, 1, 3).reshape(-1, D)
    a["l2_wq"] = _features_first(order(f("L2_xattn_Wq")), np)
    a["l2_wk"] = _features_first(f("L2_xattn_Wk"), np)
    a["l2_wv"] = _features_first(f("L2_xattn_Wv"), np)
    outputs = lambda w: np.ascontiguousarray(w.reshape(4, 4, 2, 16, -1).transpose(1, 0, 2, 3, 4).reshape(D, -1))
    a["l2_wo"] = _features_first(outputs(f("L2_xattn_Wo")), np)
    bv = outputs(np.broadcast_to(f("L2_xattn_bv").reshape(8, 1, 16), (8, 4, 16)).reshape(D)).reshape(D)
    vectors += [order(f("L2_xattn_bq").reshape(1, D)).reshape(D), f("L2_xattn_bk"), bv, f("L2_xattn_bo"),
                f("L2_xattn_gamma"), f("L2_xattn_beta")]
    a["l3_wq"] = _features_first(f("L3_xattn_w_q").T, np)
    a["l3_wk"] = _features_first(f("L3_xattn_w_k"), np)
    a["l3_wv"] = _features_first(f("L3_xattn_w_v").T, np)
    a["l3_wo"] = _features_first(f("L3_xattn_w_o").T, np)
    even = np.zeros((P,), x.dtype)
    even.reshape(4, 2, 16)[:, 0] = 1
    odd = np.zeros((P,), x.dtype)
    odd.reshape(4, 2, 16)[:, 1] = 1
    vectors += [np.full((P,), f("L3_xattn_alpha"), x.dtype), even, odd, np.ones((P,), x.dtype),
                np.full((P,), 1e-5, x.dtype), np.full((P,), 1e-6, x.dtype)]
    a["cols"] = np.ascontiguousarray(_columns(vectors))
    return a


UNTIL = 99


def kernel(**inputs):
    import concourse.bacc as _bacc
    import numpy as _np
    from concourse.bass_utils import run_bass_kernel_spmd as _run

    nc = _bacc.Bacc("TRN2", target_bir_lowering=False, num_devices=1)
    arrays = _layout_inputs(inputs)
    dram = {n: nc.dram_tensor(f"in_{n}", a.shape, mybir.dt.from_np(a.dtype), kind="ExternalInput").ap()
            for n, a in arrays.items()}
    out = nc.dram_tensor("out", (P, C, NT), F32, kind="ExternalOutput").ap()
    program(nc, dram, out, UNTIL)
    r = _run(nc, [{f"in_{n}": a for n, a in arrays.items()}], core_ids=[0])
    y = r.results[0]["out"]
    return _np.ascontiguousarray(y.transpose(1, 0, 2).reshape(D, NT).T.reshape(B, SQ, D))
```

```python
from contextlib import ExitStack

import concourse.bass as bass
from concourse import mybir

F32 = mybir.dt.float32
F32R = mybir.dt.float32r
I32 = mybir.dt.int32
ALU = mybir.AluOpType
ACT = mybir.ActivationFunctionType
AX = mybir.AxisListType

P = 128
B = 8
SQ = 112
NT = B * SQ
HALF = NT // 2
SK = 375
KT = 3
KW = 126
SKP = KT * KW
SKB = SK + 1
D = 512
C = D // P
H0 = 16
HG = 2
NG = H0 // HG
GW = HG * P
F = 2048
FG = 4
NFG = F // (FG * P)
WROW = 16 * P * HG
MASKED = -1.0e30

COLS = {}


def _layout():
    at = 0
    names = []
    for a in ("1", "2"):
        names += [("ln_s" + a, C), ("ln_o" + a, C), ("bq" + a, H0), ("bk" + a, H0), ("bv" + a, H0),
                  ("bias_k" + a, H0), ("bo" + a, C)]
    names += [("ln_sm", C), ("ln_om", C), ("fc1", F // P), ("fc2", C)]
    names += [("l1_q", C), ("l1_k", C), ("l1_v", C), ("l1_o", C), ("l1_post", C), ("l1_m1", F // P), ("l1_m2", C)]
    names += [("l2_q", C), ("l2_k", 1), ("l2_v", C), ("l2_o", C), ("gamma", C), ("beta", C)]
    names += [("alpha", 1), ("even", 1), ("odd", 1), ("one", 1), ("eps5", 1), ("eps6", 1)]
    for n, w in names:
        COLS[n] = (at, w)
        at += w
    return at


NCOL = _layout()


class Machine:
    pass


class Mark:

    def __init__(self, sem):
        self.sem, self.base = sem, 0


def col(m, name, i=0, n=1):
    at = COLS[name][0] + i
    return m.cols[:, at:at + n]


def wait_loop(eng, sem, value):
    eng.wait_ge(sem, value)
    eng.nop(nofuse=True)


def phase_load(nc, m, ctx, d):
    ident_zero = ctx.enter_context(nc.semaphore("ident_zero"))
    constants_made = ctx.enter_context(nc.semaphore("constants_made"))
    inputs_loaded = ctx.enter_context(nc.semaphore("inputs_loaded"))
    with nc.Block() as block:
        @block.sync
        def _(sp):
            sp.dma_start(m.xT[:, :, :], d["x"]).then_inc(inputs_loaded, 16)
            sp.dma_start(m.cols[:, :], d["cols"]).then_inc(inputs_loaded, 16)
            sp.wait_ge(inputs_loaded, 32)

        @block.gpsimd
        def _(pool):
            nc.gpsimd.memset(m.ident[:, :], 0.0).then_inc(ident_zero, 1)
            nc.gpsimd.memset(m.mean_of[:, :], 1.0 / D).then_inc(constants_made, 1)
            pool.wait_ge(ident_zero, 1)
            nc.gpsimd.affine_select(out=m.ident[:, :], in_=m.ident[:, :], compare_op=ALU.not_equal, fill=1.0,
                                    base=0, pattern=[[-1, P]], channel_multiplier=1).then_inc(constants_made, 1)
            pool.wait_ge(constants_made, 2)


def phase_norm(nc, m, ctx, tag, src, dst, eps, scale, offset, centred=True, after_bias=None, preload=None,
               store=None):
    mean_done, centre_done, square_done, var_done, deviation_done, rstd_done, scaled, affine_done, bias_added = (
        m.norm_marks)
    with ExitStack() as own:
        sq = own.enter_context(nc.sbuf_tensor(f"sq_{tag}", [P, 2, C, HALF], F32))
        rstd = own.enter_context(nc.sbuf_tensor(f"rstd_{tag}", [P, 2, HALF], F32))
        ps = [own.enter_context(nc.psum_tensor(f"norm{i}_{tag}", [P, 512], F32)) for i in range(4)]
        block = own.enter_context(nc.Block())
        h = lambda t, s: t[:, :, s * HALF:(s + 1) * HALF]
        spread = lambda t: t.unsqueeze(1).broadcast_to((P, C, HALF))

        @block.tensor
        def _(pe):
            for s in range(2):
                if centred:
                    for c in range(C):
                        mm = pe.matmul(ps[s][:, 0:HALF], m.mean_of[:, :], src[:, c, s * HALF:(s + 1) * HALF],
                                       start=(c == 0), stop=(c == C - 1))
                    mm.then_inc(mean_done.sem, 1)
            for s in range(2):
                pe.wait_ge(square_done.sem, square_done.base + s + 1)
                for c in range(C):
                    mm = pe.matmul(ps[2 + s][:, 0:HALF], m.mean_of[:, :], sq[:, s, c, :],
                                   start=(c == 0), stop=(c == C - 1))
                mm.then_inc(var_done.sem, 1)

        @block.scalar
        def _(act):
            for s in range(2):
                if centred:
                    act.wait_ge(centre_done.sem, centre_done.base + s + 1)
                nc.scalar.activation(sq[:, s, :, :], h(dst if centred else src, s), ACT.Square
                                     ).then_inc(square_done.sem, 1)
            for s in range(2):
                act.wait_ge(var_done.sem, var_done.base + s + 1)
                nc.scalar.activation(rstd[:, s, :], ps[2 + s][:, 0:HALF], ACT.Sqrt, bias=col(m, eps)
                                     ).then_inc(deviation_done.sem, 1)
            for s in range(2):
                act.wait_ge(scaled.sem, scaled.base + s + 1)
                for c in range(C):
                    part = dst[:, c, s * HALF:(s + 1) * HALF]
                    if offset is None:
                        i = nc.scalar.activation(part, part, ACT.Identity, scale=col(m, scale, c))
                    else:
                        i = nc.scalar.activation(part, part, ACT.Identity, bias=col(m, offset, c),
                                                 scale=col(m, scale, c))
                    i.then_inc(affine_done.sem, 1)

        @block.vector
        def _(dve):
            if centred:
                for s in range(2):
                    dve.wait_ge(mean_done.sem, mean_done.base + s + 1)
                    nc.vector.tensor_tensor(h(dst, s), h(src, s), spread(ps[s][:, 0:HALF]), ALU.subtract
                                            ).then_inc(centre_done.sem, 1)
            for s in range(2):
                dve.wait_ge(deviation_done.sem, deviation_done.base + s + 1)
                nc.vector.reciprocal(rstd[:, s, :], rstd[:, s, :]).then_inc(rstd_done.sem, 1)
                dve.wait_ge(rstd_done.sem, rstd_done.base + s + 1)
                nc.vector.tensor_tensor(h(dst, s), h(dst if centred else src, s), spread(rstd[:, s, :]), ALU.mult
                                        ).then_inc(scaled.sem, 1)

        @block.gpsimd
        def _(pool):
            if after_bias is not None:
                pool.wait_ge(centre_done.sem, centre_done.base + 2)
                for c in range(C):
                    nc.gpsimd.tensor_scalar(src[:, c, :], src[:, c, :], col(m, after_bias, c), None, ALU.add
                                            ).then_inc(bias_added.sem, 1)

        @block.sync
        def _(sp):
            if preload is not None:
                preload(sp)
    for mark in (square_done, var_done, deviation_done, rstd_done, scaled) + (
            (mean_done, centre_done) if centred else ()):
        mark.base += 2


class Split:

    def __init__(self, make, name, shape):
        self.high, self.low = make(name + "_high", shape, F32R), make(name + "_low", shape, F32R)

    def at(self, *index):
        return self.high[index], self.low[index]


def products(pe, out, stationary, moving, first, last):
    (sh, sl), (mh, ml) = stationary, moving
    pe.matmul(out, sh, mh, start=first, stop=False)
    pe.matmul(out, sh, ml, start=False, stop=False)
    return pe.matmul(out, sl, mh, start=False, stop=last)


class AttentionInputs:

    def __init__(self, nc, ctx, own, tag, pack, rows, ctx_batches):
        sem = lambda n: ctx.enter_context(nc.semaphore(f"{n}_a{tag}"))
        sb = lambda n, s: own.enter_context(nc.sbuf_tensor(f"{n}_a{tag}", s, F32))
        self.tag, self.pack, self.rows, self.ctx_batches = tag, pack, rows, ctx_batches
        self.c_loaded = [sem("craw0"), sem("craw1")]
        self.qkv_loaded, self.wo_loaded, self.row_loaded = sem("rqkv"), sem("rwo"), sem("rrow")
        self.craw, self.raw_qkv = sb("craw", [P, 2, C, SKP]), sb("raw_qkv", [P, 3 * C * GW])
        self.raw_wo, self.row = sb("raw_wo", [P, HG * D]), sb("row", [1, 2 * GW])

    def load_qkv(self, sp, g):
        sp.dma_start(self.raw_qkv[:, :], self.pack[g, :, 0:3 * C * GW].rearrange("a p w -> p (a w)")
                     ).then_inc(self.qkv_loaded, 16)

    def load_wo(self, sp, g):
        sp.dma_start(self.raw_wo[:, :], self.pack[g, :, 3 * C * GW:WROW].rearrange("a p w -> p (a w)")
                     ).then_inc(self.wo_loaded, 16)

    def load_row(self, sp, g):
        sp.dma_start(self.row[:, :], self.rows[g, :]).then_inc(self.row_loaded, 16)

    def load_context(self, sp, n):
        sp.dma_start(self.craw[:, n % 2, :, :], self.ctx_batches[n]).then_inc(self.c_loaded[n % 2], 16)

    def load_first(self, sp):
        first = bass.ds(0, 1)
        self.load_qkv(sp, first)
        for n in range(2):
            self.load_context(sp, n)
        self.load_wo(sp, first)
        self.load_row(sp, first)


def phase_attn0(nc, m, ctx, inputs):
    a = tag = inputs.tag
    sem = lambda n: ctx.enter_context(nc.semaphore(f"{n}_a{tag}"))
    c_loaded, qkv_loaded, wo_loaded = inputs.c_loaded, inputs.qkv_loaded, inputs.wo_loaded
    row_loaded, craw, raw_qkv, raw_wo, row = inputs.row_loaded, inputs.craw, inputs.raw_qkv, inputs.raw_wo, inputs.row
    qo_high, qo_split = sem("qoh"), sem("qos")
    w_high, w_split, h_high, h_split, c_high, c_split = (sem(n) for n in ("wh", "ws", "hh", "hs", "ch", "cs"))
    kq_done, v_done, s_done, t_done, o_done = (sem(n) for n in ("kq", "v", "s", "t", "o"))
    kq_high, v_high, t_high, o_high, exp_done = (sem(n) for n in ("kqh", "vh", "th", "oh", "exp"))
    kq_out, v_out, t_out, o_out = (sem(n) for n in ("kqe", "ve", "te", "oe"))
    max_done, nmx_done, recip_done = (sem(n) for n in ("mx", "nmx", "rc"))
    vb_step, row_used, v_fixed, p_normed, pads_zero = (sem(n) for n in ("vb", "ru", "vf", "pn", "pz"))
    scale = float(P) ** -0.5
    NB = B // 2
    KQ, VO, N2, OO = HG * NB + HG + 2, 2 * NB + 2, HG * NB, HG * NB
    with ExitStack() as own:
        sb = lambda n, s, dt=F32: own.enter_context(nc.sbuf_tensor(f"{n}_a{tag}", s, dt))
        c, w = Split(sb, "c", [P, C, NB * SKP]), Split(sb, "w", [P, WROW])
        h, q, ot = Split(sb, "h", [P, C, HALF]), Split(sb, "q", [P, HG, HALF]), Split(sb, "ot", [P, HG, HALF])
        kT, v, pt = Split(sb, "kT", [P, HG, SKB]), Split(sb, "v", [KW, 2, KT, GW]), Split(sb, "pt", [KW, HG, KT, SQ])
        p = sb("p", [SQ, HG, SKP])
        mx, nmx = sb("mx", [SQ, 2, HG]), sb("nmx", [SQ, 2, HG])
        rsum, rinv = sb("rsum", [SQ, 2, HG]), sb("rinv", [SQ, 2, HG])
        vrow, vrow_split = sb("vrow", [1, GW]), Split(sb, "vrs", [1, GW])
        ps = lambda n: own.enter_context(nc.psum_tensor(f"{n}_a{tag}", [P, 512], F32))
        kbank, vbank, sbank = [ps("k0"), ps("k1")], [ps("v0"), ps("v1")], [ps("s0"), ps("s1")]
        tbank, obank = ps("t"), ps("o")
        KIND = C * GW
        part = lambda lo, n=P: w.at(slice(None), slice(lo, lo + n))
        wq = lambda k, j: part(k * GW + j * P)
        wk = lambda k, j: part(KIND + k * GW + j * P)
        wv = lambda k: part(2 * KIND + k * GW, GW)
        wo = lambda j, o: part(3 * KIND + j * D + o * P)
        block = own.enter_context(nc.Block())

        @block.sync
        def _(sp):
            def load_next(g, n, wo_too=True):
                wait_loop(sp, w_split, n * 2 + 3)
                wait_loop(sp, qo_split, n * 2 + 1)
                inputs.load_qkv(sp, g)
                if wo_too:
                    wait_loop(sp, qo_split, n * 2 + 2)
                    inputs.load_wo(sp, g)
                    wait_loop(sp, row_used, n + 1)
                    inputs.load_row(sp, g)

            first = bass.ds(0, 1)
            for half in range(2):
                for b in range(NB):
                    n = half * NB + b
                    if n >= 2:
                        sp.wait_ge(c_split, n - 1)
                        inputs.load_context(sp, n)
                with sp.Fori(0, NG - 1) as it:
                    load_next(bass.ds(it + 1, 1), it + NG * half)
                load_next(first, NG * (half + 1) - 1, wo_too=(half == 0))

        @block.tensor
        def _(pe):
            for half in range(2):
                KQ0, Q0 = half * (HG + NG * KQ), HG
                kq0, v0, n0, oo0, g0 = KQ0 + Q0, half * NG * VO, half * NG * N2, half * NG * OO, half * NG

                def q_proj(j, at, unit):
                    pe.wait_ge(kq_out, at + (1 + unit - 1))
                    bank = kbank[unit % 2]
                    for k in range(C):
                        mm = products(pe, bank[:, 0:HALF], wq(k, j), h.at(slice(None), k), k == 0, k == C - 1)
                    mm.then_inc(kq_done, 1)

                pe.wait_ge(h_split, half + 1)
                if half == 0:
                    pe.wait_ge(w_split, 1)
                for j in range(HG):
                    q_proj(j, 0, KQ0 + j)
                with pe.Fori(0, NG) as it:
                    def bank_of_kq(u):
                        pe.wait_ge(kq_out, it * KQ + (1 + kq0 + u - 1))
                        return kbank[u % 2]

                    def bank_of_v(u):
                        pe.wait_ge(v_out, it * VO + (1 + v0 + u - 1))
                        return vbank[u % 2]

                    def k_proj(b, j):
                        bank = bank_of_kq(HG * b + j)
                        for k in range(C):
                            mm = products(pe, bank[:, 0:SKB], wk(k, j),
                                          c.at(slice(None), k, slice(b * SKP, b * SKP + SKB)), k == 0, k == C - 1)
                        mm.then_inc(kq_done, 1)

                    def v_proj(b, n):
                        bank = bank_of_v(2 * b + n)
                        for i, t in enumerate(([0, 1], [2])[n]):
                            for k in range(C):
                                at = b * SKP + t * KW
                                mm = products(pe, bank[0:KW, i * GW:(i + 1) * GW],
                                              c.at(slice(None), k, slice(at, at + KW)), wv(k), k == 0, k == C - 1)
                        mm.then_inc(v_done, 1)

                    def scores(b, j):
                        n = HG * b + j
                        pe.wait_ge(kq_out, it * KQ + (1 + kq0 + n + 1))
                        pe.wait_ge(exp_done, it * N2 + (1 + n0 + max(n - 1, 0)))
                        products(pe, sbank[j][0:SQ, 0:SKB], q.at(slice(None), j, slice(b * SQ, (b + 1) * SQ)),
                                 kT.at(slice(None), j), True, True).then_inc(s_done, 1)

                    def turn(b, j):
                        n = HG * b + j
                        pe.wait_ge(p_normed, it * N2 + (n0 + n + 1))
                        pe.wait_ge(t_out, it * N2 + (1 + n0 + n))
                        for t in range(KT):
                            mm = pe.transpose(tbank[0:KW, t * SQ:(t + 1) * SQ], p[:, j, t * KW:(t + 1) * KW],
                                              m.ident[0:SQ, 0:SQ])
                        mm.then_inc(t_done, 1)

                    def weigh(b, j):
                        n = HG * b + j
                        pe.wait_ge(t_out, it * N2 + (2 + n0 + n))
                        if j == 0:
                            pe.wait_ge(v_fixed, it * NB + (half * NG * NB + b + 1))
                            pe.wait_ge(v_out, it * VO + (1 + v0 + 2 * (b + 1)))
                            pe.wait_ge(o_out, it * OO + (1 + oo0 + HG * b))
                        for t in range(KT):
                            mm = products(pe, obank[:, j * SQ:(j + 1) * SQ],
                                          v.at(slice(None), b % 2, t, slice(j * P, (j + 1) * P)),
                                          pt.at(slice(None), j, t), t == 0, t == KT - 1)
                        if j == HG - 1:
                            mm.then_inc(o_done, 1)

                    def o_proj(o, lo, hi):
                        bank = (vbank if o < 2 else kbank)[o % 2]
                        if lo == 0:
                            (bank_of_v if o < 2 else bank_of_kq)(2 * NB + o if o < 2 else HG * NB + HG + o - 2)
                        pe.wait_ge(o_out, it * OO + (1 + oo0 + HG * hi))
                        cols = slice(lo * SQ, hi * SQ)
                        for j in range(HG):
                            mm = products(pe, bank[:, cols], wo(j, o), ot.at(slice(None), j, cols), j == 0, j == HG - 1)
                        if hi == NB:
                            mm.then_inc(v_done if o < 2 else kq_done, 1)

                    pe.wait_ge(w_split, it * 2 + (g0 * 2 + 3))
                    for b in range(NB):
                        pe.wait_ge(c_split, half * NB + b + 1)
                        k_proj(b, 0)
                        v_proj(b, 0)
                        if b:
                            turn(b - 1, 0)
                        k_proj(b, 1)
                        if b:
                            weigh(b - 1, 0)
                            turn(b - 1, 1)
                        v_proj(b, 1)
                        scores(b, 0)
                        if b:
                            weigh(b - 1, 1)
                        scores(b, 1)
                    last = NB - 1
                    pe.wait_ge(qo_split, it * 2 + (g0 * 2 + 3))
                    q_proj(0, it * KQ, kq0 + HG * NB)
                    q_proj(1, it * KQ, kq0 + HG * NB + 1)
                    o_proj(0, 0, last)
                    turn(last, 0)
                    o_proj(1, 0, last)
                    weigh(last, 0)
                    turn(last, 1)
                    o_proj(2, 0, last)
                    weigh(last, 1)
                    o_proj(3, 0, last)
                    for o in (2, 3, 0, 1):
                        o_proj(o, last, NB)

        def split_units(eng, half, do):
            if half == 0:
                do.weight(0, 0, True)
            do.hidden(half)
            if half == 0:
                do.weight(0, 1, True)
            do.context(half, 0)
            if half == 0:
                do.weight(0, 2, True)
            for j in range(HG):
                do.query(None, j)
            for b in range(1, NB):
                do.context(half, b)
            with eng.Fori(0, NG) as it:
                last = NB - 1
                for b in range(NB):
                    do.key(it, b, 0)
                    do.value(it, b, 0)
                    if b:
                        do.turned(it, b - 1, 0)
                    do.key(it, b, 1)
                    if b:
                        do.turned(it, b - 1, 1)
                    do.value(it, b, 1)
                    do.maximum(it, b, 0)
                    if b:
                        do.attended(it, b - 1)
                    do.maximum(it, b, 1)
                    do.softmax(it, b)
                do.weight(it, 1)
                do.query(it, 0)
                do.query(it, 1)
                do.turned(it, last, 0)
                do.turned(it, last, 1)
                do.attended(it, last)
                do.weight(it, 2)
                do.output(it)

        def weights(kind):
            if kind == 3:
                return slice(3 * KIND, WROW), raw_wo[:, :]
            return slice(kind * KIND, (kind + 1) * KIND), raw_qkv[:, kind * KIND:(kind + 1) * KIND]

        class Work:

            def __init__(self, half):
                self.half, self.g0 = half, half * NG
                self.kq0, self.v0, self.n0 = half * (HG + NG * KQ) + HG, half * NG * VO, half * NG * N2

            def kq(self, it, b, j):
                return (self.kq0 - HG + j + 1) if it is None else it * KQ + (self.kq0 + HG * b + j + 1)

            def v(self, it, b, n):
                return it * VO + (self.v0 + 2 * b + n + 1)

            def n(self, it, b, j):
                return it * N2 + (self.n0 + HG * b + j + 1)

            def o(self, it, b):
                return it * NB + (self.half * NG * NB + b + 1)

            def w(self, it, kind, first=False):
                return kind if first else it * 2 + (self.g0 * 2 + 2 + kind)

            def column(self, it, name, j):
                at = COLS[name + a][0] + j
                return m.cols[:, at:at + 1] if it is None else m.cols[:, bass.ds(it * HG + at, 1)]

            def query_column(self, it, j):
                at = COLS["bq" + a][0] + j
                return m.cols[:, at:at + 1] if it is None else m.cols[:, bass.ds(it * HG + (at + HG), 1)]


        @block.scalar
        def _(act):
            class High(Work):
                def weight(self, it, kind, first=False):
                    if kind == 0:
                        act.wait_ge(qkv_loaded, 16)
                    elif kind == 1 and not first:
                        wait_loop(act, qkv_loaded, it * 16 + (self.g0 + 2) * 16)
                    to, src = weights(kind)
                    nc.scalar.copy(w.high[:, to], src).then_inc(w_high, 1)

                def hidden(self, half):
                    nc.scalar.copy(h.high[:, :, :], m.hT[:, :, half * HALF:(half + 1) * HALF]).then_inc(h_high, 1)

                def context(self, half, b):
                    act.wait_ge(c_loaded[b % 2], 16 * (half * NB // 2 + b // 2 + 1))
                    nc.scalar.copy(c.high[:, :, b * SKP:(b + 1) * SKP], craw[:, b % 2, :, :]).then_inc(c_high, 1)

                def query(self, it, j):
                    wait_loop(act, kq_done, self.kq(it, NB, j))
                    nc.scalar.activation(q.high[:, j, :], kbank[j][:, 0:HALF], ACT.Identity,
                                         bias=self.query_column(it, j)).then_inc(kq_high, 1)

                def key(self, it, b, j):
                    wait_loop(act, kq_done, self.kq(it, b, j))
                    if b == 0:
                        nc.scalar.activation(kT.high[:, j, 0:1], self.column(it, "bias_k", j), ACT.Identity
                                             ).then_inc(kq_high, 1)
                    nc.scalar.activation(kT.high[:, j, 1:SKB], kbank[j][:, 1:SKB], ACT.Identity,
                                         bias=self.column(it, "bk", j)).then_inc(kq_high, 1)

                def value(self, it, b, n):
                    wait_loop(act, v_done, self.v(it, b, n))
                    wide = (2 - n) * GW
                    nc.scalar.copy(v.high[:, b % 2, 2 * n:2 * n + 2 - n, :],
                                   vbank[n][0:KW, 0:wide].rearrange("p (t w) -> p t w", w=GW)).then_inc(v_high, 1)

                def turned(self, it, b, j):
                    wait_loop(act, t_done, self.n(it, b, j))
                    nc.scalar.copy(pt.high[:, j, :, :], tbank[0:KW, 0:KT * SQ].rearrange("p (t q) -> p t q", q=SQ)
                                   ).then_inc(t_high, 1)

                def attended(self, it, b):
                    wait_loop(act, o_done, self.o(it, b))
                    for j in range(HG):
                        nc.scalar.activation(ot.high[:, j, b * SQ:(b + 1) * SQ], obank[:, j * SQ:(j + 1) * SQ],
                                             ACT.Identity, bias=self.column(it, "bv", j)).then_inc(o_high, 1)

                def softmax(self, it, b):
                    wait_loop(act, nmx_done, self.o(it, b))
                    for j in range(HG):
                        nc.scalar.activation(p[:, j, 0:SKB], sbank[j][0:SQ, 0:SKB], ACT.Exp, scale=scale,
                                             bias=nmx[:, b % 2, j:j + 1],
                                             accum_out=rsum[:, b % 2, j:j + 1]).then_inc(exp_done, 1)

                def maximum(self, it, b, j):
                    pass

                def output(self, it):
                    pass

            act.sem_inc(exp_done, 1)
            act.wait_ge(pads_zero, 1)
            for half in range(2):
                split_units(act, half, High(half))

        @block.vector
        def _(dve):
            def rest(out, bank, bias, high):
                if bias is None:
                    return nc.vector.tensor_tensor(out, bank, high, ALU.subtract)
                return nc.vector.scalar_tensor_tensor(out, bank, bias, high, ALU.add, ALU.subtract)

            class Low(Work):
                def keys_high(self, it, b, j):
                    per = HG * NB + HG + HG
                    base = self.half * (HG + NG * per) + HG
                    if it is None:
                        return base - HG + j + 1
                    return it * per + (base + (2 * (j + 1) if b == 0 else HG + HG * b + j + 1))

                def weight(self, it, kind, first=False):
                    dve.wait_ge(w_high, self.w(it, kind, first) + 1)
                    to, src = weights(kind)
                    nc.vector.tensor_tensor(w.low[:, to], src, w.high[:, to], ALU.subtract).then_inc(w_split, 1)

                def hidden(self, half):
                    dve.wait_ge(h_high, half + 1)
                    nc.vector.tensor_tensor(h.low[:, :, :], m.hT[:, :, half * HALF:(half + 1) * HALF],
                                            h.high[:, :, :], ALU.subtract).then_inc(h_split, 1)

                def context(self, half, b):
                    dve.wait_ge(c_high, half * NB + b + 1)
                    cols = slice(b * SKP, (b + 1) * SKP)
                    nc.vector.tensor_tensor(c.low[:, :, cols], craw[:, b % 2, :, :], c.high[:, :, cols],
                                            ALU.subtract).then_inc(c_split, 1)

                def query(self, it, j):
                    dve.wait_ge(kq_high, self.keys_high(it, NB, j))
                    rest(q.low[:, j, :], kbank[j][:, 0:HALF], self.query_column(it, j), q.high[:, j, :]
                         ).then_inc(kq_out, 1)

                def key(self, it, b, j):
                    dve.wait_ge(kq_high, self.keys_high(it, b, j))
                    if b == 0:
                        nc.vector.tensor_tensor(kT.low[:, j, 0:1], self.column(it, "bias_k", j),
                                                kT.high[:, j, 0:1], ALU.subtract)
                    rest(kT.low[:, j, 1:SKB], kbank[j][:, 1:SKB], self.column(it, "bk", j), kT.high[:, j, 1:SKB]
                         ).then_inc(kq_out, 1)

                def value(self, it, b, n):
                    dve.wait_ge(v_high, it * (2 * NB) + (self.half * NG * 2 * NB + 2 * b + n + 1))
                    wide = (2 - n) * GW
                    rest(v.low[:, b % 2, 2 * n:2 * n + 2 - n, :],
                         vbank[n][0:KW, 0:wide].rearrange("p (t w) -> p t w", w=GW), None,
                         v.high[:, b % 2, 2 * n:2 * n + 2 - n, :]).then_inc(v_out, 1)

                def turned(self, it, b, j):
                    dve.wait_ge(t_high, self.n(it, b, j))
                    rest(pt.low[:, j, :, :], tbank[0:KW, 0:KT * SQ].rearrange("p (t q) -> p t q", q=SQ), None,
                         pt.high[:, j, :, :]).then_inc(t_out, 1)

                def attended(self, it, b):
                    dve.wait_ge(o_high, self.n(it, b, HG - 1))
                    for j in range(HG):
                        cols = slice(b * SQ, (b + 1) * SQ)
                        rest(ot.low[:, j, cols], obank[:, j * SQ:(j + 1) * SQ], self.column(it, "bv", j),
                             ot.high[:, j, cols]).then_inc(o_out, 1)

                def maximum(self, it, b, j):
                    dve.wait_ge(s_done, self.n(it, b, j))
                    nc.vector.tensor_reduce(mx[:, b % 2, j:j + 1], sbank[j][0:SQ, 0:SKB], AX.X, ALU.max
                                            ).then_inc(max_done, 1)

                def softmax(self, it, b):
                    dve.wait_ge(max_done, self.n(it, b, HG - 1))
                    nc.vector.tensor_scalar(nmx[:, b % 2, :], mx[:, b % 2, :], -scale, None, ALU.mult
                                            ).then_inc(nmx_done, 1)
                    dve.wait_ge(exp_done, self.n(it, b, HG - 1) + 1)
                    nc.vector.reciprocal(rinv[:, b % 2, :], rsum[:, b % 2, :]).then_inc(recip_done, 1)

                def output(self, it):
                    for o in (2, 3, 0, 1):
                        if o < 2:
                            dve.wait_ge(v_done, it * VO + (self.v0 + 2 * NB + o + 1))
                        else:
                            dve.wait_ge(kq_done, it * KQ + (self.kq0 + HG * NB + HG + o - 1))
                        to = m.xT[:, o, self.half * HALF:(self.half + 1) * HALF]
                        bank = (vbank if o < 2 else kbank)[o % 2]
                        nc.vector.tensor_tensor(to, to, bank[:, 0:HALF], ALU.add).then_inc(v_out if o < 2 else kq_out, 1)

            for s in (kq_out, v_out, t_out, o_out):
                dve.sem_inc(s, 1)
            for half in range(2):
                split_units(dve, half, Low(half))

        @block.gpsimd
        def _(pool):
            def weight(it, g0, kind, n):
                if kind == 3:
                    wait_loop(pool, wo_loaded, it * 16 + (g0 + 1) * 16)
                else:
                    wait_loop(pool, qkv_loaded, it * 16 + (g0 + 2) * 16)
                to, src = weights(kind)
                nc.gpsimd.tensor_copy(w.high[:, to], src).then_inc(qo_high, 1)
                wait_loop(pool, qo_high, it * 2 + (g0 * 2 + n + 1))
                nc.gpsimd.tensor_tensor(w.low[:, to], src, w.high[:, to], ALU.subtract).then_inc(qo_split, 1)

            pool.sem_inc(qo_split, 1)
            nc.gpsimd.memset(p[:, :, SKB:SKP], 0.0).then_inc(pads_zero, 1)
            for half in range(2):
                g0, v0, n0 = half * NG, half * NG * VO, half * NG * N2
                with pool.Fori(0, NG) as it:
                    wait_loop(pool, row_loaded, it * 16 + 16 * (g0 + 1))
                    nc.gpsimd.tensor_tensor(vrow[:, :], row[:, 0:GW], row[:, GW:2 * GW], ALU.subtract
                                            ).then_inc(row_used, 1)
                    wait_loop(pool, row_used, it + (g0 + 1))
                    nc.gpsimd.tensor_copy(vrow_split.high[:, :], vrow[:, :]).then_inc(vb_step, 1)
                    wait_loop(pool, vb_step, it * 2 + (g0 * 2 + 1))
                    nc.gpsimd.tensor_tensor(vrow_split.low[:, :], vrow[:, :], vrow_split.high[:, :], ALU.subtract
                                            ).then_inc(vb_step, 1)
                    wait_loop(pool, vb_step, it * 2 + (g0 * 2 + 2))
                    for b in range(NB):
                        wait_loop(pool, v_out, it * VO + (1 + v0 + 2 * b + 1))
                        nc.gpsimd.tensor_copy(v.high[0:1, b % 2, 0, :], vrow_split.high[:, :])
                        nc.gpsimd.tensor_copy(v.low[0:1, b % 2, 0, :], vrow_split.low[:, :]).then_inc(v_fixed, 1)
                        wait_loop(pool, recip_done, it * NB + (half * NG * NB + b + 1))
                        for j in range(HG):
                            nc.gpsimd.tensor_scalar(p[:, j, 0:SKB], p[:, j, 0:SKB], rinv[:, b % 2, j:j + 1], None,
                                                    ALU.mult).then_inc(p_normed, 1)
                        if b == 0:
                            weight(it, g0, 3, 0)
                        if b == 1:
                            weight(it, g0, 0, 1)


def phase_mlp(nc, m, ctx, tag, pack, func, b1, b2):
    up_done, act_done, down_done, added, bias_added, loaded, w_high, w_split, g_high, g_split = m.mlp_marks
    ITS = NFG // 2
    UP, DOWN = 2 * FG, 2 * C
    MID = C * FG * P
    with ExitStack() as own:
        sb = lambda n, s, dt=F32: own.enter_context(nc.sbuf_tensor(f"{n}_{tag}", s, dt))
        w, h = Split(sb, "w", [P, 2, WROW]), Split(sb, "h", [P, C, NT])
        hidden, g = sb("hidden", [P, 2, FG, HALF]), Split(sb, "g", [P, 2, FG, HALF])
        ps = lambda n: own.enter_context(nc.psum_tensor(f"{n}_{tag}", [P, 512], F32))
        up, down = [ps(f"up{i}") for i in range(4)], [ps(f"down{i}") for i in range(4)]
        at = lambda i, lo: w.at(slice(None), i, slice(lo, lo + P))
        w1 = lambda i, k, f: at(i, (k * FG + f) * P)
        w2 = lambda i, f, c: at(i, MID + f * D + c * P)
        parts = (slice(0, MID), slice(MID, WROW))
        block = own.enter_context(nc.Block())

        @block.sync
        def _(sp):
            with sp.Fori(0, ITS - 1) as it:
                for i in range(2):
                    wait_loop(sp, w_split.sem, it * 4 + (w_split.base + 1 + 2 * (i + 1)))
                    sp.dma_start(m.wraw[:, :], pack[bass.ds(it * 2 + (i + 1), 1), :, :].rearrange("a p w -> p (a w)")
                                 ).then_inc(loaded.sem, 16)
            for n, group in ((NFG - 2, NFG - 1), (NFG - 1, 0)):
                sp.wait_ge(w_split.sem, w_split.base + 1 + 2 * (n + 1))
                sp.dma_start(m.wraw[:, :], pack[group]).then_inc(loaded.sem, 16)

        @block.tensor
        def _(pe):
            with pe.Fori(0, ITS) as it:
                for i in range(2):
                    pe.wait_ge(w_split.sem, it * 4 + (w_split.base + 1 + 2 * i + 1))
                    for s in range(2):
                        for f in range(FG):
                            n = i * UP + s * FG + f
                            pe.wait_ge(act_done.sem, it * (2 * UP) + (act_done.base + 1 + max(n - 3, 0)))
                            for k in range(C):
                                mm = products(pe, up[f][:, 0:HALF], w1(i, k, f),
                                              h.at(slice(None), k, slice(s * HALF, (s + 1) * HALF)), k == 0, k == C - 1)
                            mm.then_inc(up_done.sem, 1)
                    pe.wait_ge(w_split.sem, it * 4 + (w_split.base + 1 + 2 * i + 2))
                    for s in range(2):
                        pe.wait_ge(g_split.sem, it * (2 * UP) + (g_split.base + i * UP + (s + 1) * FG))
                        for c in range(C):
                            n = i * DOWN + s * C + c
                            pe.wait_ge(added.sem, it * (2 * DOWN) + (added.base + 1 + max(n - 3, 0)))
                            for f in range(FG):
                                mm = products(pe, down[c][:, 0:HALF], w2(i, f, c), g.at(slice(None), s, f),
                                              f == 0, f == FG - 1)
                            mm.then_inc(down_done.sem, 1)

        @block.scalar
        def _(act):
            act.sem_inc(act_done.sem, 1)
            nc.scalar.copy(h.high[:, :, :], m.hT[:, :, :]).then_inc(w_high.sem, 1)
            act.wait_ge(loaded.sem, loaded.base + 16)
            for part in parts:
                nc.scalar.copy(w.high[:, 0, part], m.wraw[:, part]).then_inc(w_high.sem, 1)
            with act.Fori(0, ITS) as it:
                for i in range(2):
                    for s in range(2):
                        for f in range(FG):
                            n = i * UP + s * FG + f
                            wait_loop(act, up_done.sem, it * (2 * UP) + (up_done.base + n + 1))
                            at_col = COLS[b1][0] + i * FG + f
                            nc.scalar.activation(hidden[:, s, f, :], up[f][:, 0:HALF], func,
                                                 bias=m.cols[:, bass.ds(it * (2 * FG) + at_col, 1)]
                                                 ).then_inc(act_done.sem, 1)
                        if s == 0:
                            wait_loop(act, loaded.sem, it * 32 + (loaded.base + 16 * (i + 2)))
                            for part in parts:
                                nc.scalar.copy(w.high[:, 1 - i, part], m.wraw[:, part]).then_inc(w_high.sem, 1)

        @block.vector
        def _(dve):
            def split_weights(i, k, value):
                dve.wait_ge(w_high.sem, value)
                nc.vector.tensor_tensor(w.low[:, i, parts[k]], m.wraw[:, parts[k]], w.high[:, i, parts[k]],
                                        ALU.subtract).then_inc(w_split.sem, 1)

            dve.sem_inc(added.sem, 1)
            dve.wait_ge(w_high.sem, w_high.base + 1)
            nc.vector.tensor_tensor(h.low[:, :, :], m.hT[:, :, :], h.high[:, :, :], ALU.subtract
                                    ).then_inc(w_split.sem, 1)
            for k in range(2):
                split_weights(0, k, w_high.base + 1 + k + 1)
            dve.wait_ge(bias_added.sem, bias_added.base + C)
            with dve.Fori(0, ITS) as it:
                for i in range(2):
                    for s in range(2):
                        for f in range(FG):
                            n = i * UP + s * FG + f
                            dve.wait_ge(act_done.sem, it * (2 * UP) + (act_done.base + 1 + n + 1))
                            nc.vector.tensor_copy(g.high[:, s, f, :], hidden[:, s, f, :]).then_inc(g_high.sem, 1)
                        if s == 0:
                            for k in range(2):
                                split_weights(1 - i, k, it * 4 + (w_high.base + 1 + 2 * (i + 1) + k + 1))
                    for s in range(2):
                        for c in range(C):
                            n = i * DOWN + s * C + c
                            dve.wait_ge(down_done.sem, it * (2 * DOWN) + (down_done.base + n + 1))
                            part = m.xT[:, c, s * HALF:(s + 1) * HALF]
                            nc.vector.tensor_tensor(part, part, down[c][:, 0:HALF], ALU.add).then_inc(added.sem, 1)

        @block.gpsimd
        def _(pool):
            for c in range(C):
                nc.gpsimd.tensor_scalar(m.xT[:, c, :], m.xT[:, c, :], col(m, b2, c), None, ALU.add
                                        ).then_inc(bias_added.sem, 1)
            with pool.Fori(0, ITS) as it:
                for i in range(2):
                    for s in range(2):
                        for f in range(FG):
                            n = i * UP + s * FG + f
                            wait_loop(pool, g_high.sem, it * (2 * UP) + (g_high.base + n + 1))
                            nc.gpsimd.tensor_tensor(g.low[:, s, f, :], hidden[:, s, f, :], g.high[:, s, f, :],
                                                    ALU.subtract).then_inc(g_split.sem, 1)
    for mark, n in ((up_done, UP * NFG), (act_done, 1 + UP * NFG), (down_done, DOWN * NFG), (added, 1 + DOWN * NFG),
                    (bias_added, C), (loaded, 16 * (NFG + 1)), (w_high, 1 + 2 * (NFG + 1)),
                    (w_split, 1 + 2 * (NFG + 1)), (g_high, UP * NFG), (g_split, UP * NFG)):
        mark.base += n


def phase_dense(nc, m, ctx, tag, src, dst, evacuate, preload=None):
    product_done, stored = m.dense_marks
    wt, w_loaded = m.dense_weights[tag]
    with ExitStack() as own:
        bank = [own.enter_context(nc.psum_tensor(f"b{i}_{tag}", [P, 512], F32)) for i in range(4)]
        block = own.enter_context(nc.Block())

        @block.sync
        def _(sp):
            if preload is not None:
                preload(sp)

        @block.tensor
        def _(pe):
            pe.wait_ge(w_loaded, 16)
            for s in range(2):
                for c in range(C):
                    n = s * C + c
                    if n >= 4:
                        pe.wait_ge(stored.sem, stored.base + n - 3)
                    for k in range(C):
                        mm = pe.matmul(bank[n % 4][:, 0:HALF], wt[:, k, c * P:(c + 1) * P],
                                       src[:, k, s * HALF:(s + 1) * HALF], start=(k == 0), stop=(k == C - 1))
                    mm.then_inc(product_done.sem, 1)

        @block.vector
        def _(dve):
            for s in range(2):
                for c in range(C):
                    n = s * C + c
                    dve.wait_ge(product_done.sem, product_done.base + n + 1)
                    evacuate(dst[:, c, s * HALF:(s + 1) * HALF], bank[n % 4][:, 0:HALF], c,
                             slice(s * HALF, (s + 1) * HALF)).then_inc(stored.sem, 1)
    for mark in (product_done, stored):
        mark.base += 2 * C


class Small:

    def __init__(self, heads, width, k_chunks, latent, scale, keep, value_stride, value_at, head):
        self.heads, self.width, self.k_chunks, self.latent, self.scale = heads, width, k_chunks, latent, scale
        self.keep = keep
        self.keys = SKP + (SQ if latent else 0)
        self.tiles = KT + (1 if latent else 0)
        self.v_width = k_chunks * P
        self.stride, self.at = value_stride, value_at
        self.head = head


class Head:

    def __init__(self, row, k_chunk, version, q_chunk, value, out_chunk, position, first=True, last=True):
        self.row, self.k_chunk, self.version, self.q_chunk = row, k_chunk, version, q_chunk
        self.value = value
        self.out_chunk, self.position = out_chunk, position
        self.first, self.last = first, last


def wide_head(n):
    return Head(32 * (n % 4), n // 4, 0, n // 4, 32 * n, n // 4, n)


def narrow_head(n):
    r, x = n % 4, n // 4
    g = 2 * r + x // 4
    return Head(32 * r, 0, x // 4, x % 4, 48 * g + (16 if x % 2 == 0 else 0), x // 2,
                (x // 2) * 8 + r * 2 + x % 2, x % 2 == 0, x % 2 == 1)


def phase_small(nc, m, ctx, tag, cfg, d, mask, bias, preload):
    sem = lambda n: ctx.enter_context(nc.semaphore(f"{n}_{tag}"))
    w_loaded, staged = sem("w"), [sem(f"staged{i}") for i in range(2)]
    unit_done, s_done, t_done, o_done = sem("unit"), sem("s"), sem("t"), sem("o")
    unit_out, q_high, k_high, q_split = sem("uo"), sem("qh"), sem("kh"), sem("qs")
    sm_done, exp_done, o_out, divided = sem("sm"), sem("exp"), sem("oo"), sem("dv")
    t_out = [sem(f"te{i}") for i in range(2)]
    recip_done, spread_done, mask_made, setup_done = sem("rc"), sem("sd"), sem("mk"), sem("su")
    NH, NC, NTL, KEYS, VW, HW = cfg.heads, cfg.k_chunks, cfg.tiles, cfg.keys, cfg.v_width, cfg.width
    NQ, ITS = len(cfg.keep), B // 2
    heads = [cfg.head(n) for n in range(NH)]
    tiles = [(i * KW, KW) for i in range(KT)] + ([(SKP, SQ)] if cfg.latent else [])
    per_bank = 512 // VW
    v_units = [list(range(i, min(i + per_bank, NTL))) for i in range(0, NTL, per_bank)]
    units = lambda b: ([("q", b, 0)] + [("k", b, c) for c in range(min(NC, 2))] +
                       [("v", b, u) for u in range(len(v_units))] + [("k", b, c) for c in range(2, NC)])
    plan = {-1: units(0), NH - 3: units(1)}
    LAG_T, LAG_O, LAG_S, LAG_R = 2, 3, 2, 4
    STEPS = 2 * NH
    for b in range(2):
        plan[(b + 1) * NH - 1 + LAG_R] = [("r", b, 0)]
    order = [u for s in sorted(plan) for u in plan[s]]
    number = {u: n for n, u in enumerate(order)}
    NU = len(order)
    with ExitStack() as own:
        sb = lambda n, s, dt=F32: own.enter_context(nc.sbuf_tensor(f"{n}_{tag}", s, dt))
        wq, wk, wv = sb("wq", [P, C, D]), sb("wk", [P, C, NC * P]), sb("wv", [P, C, VW])
        cb = sb("cb", [P, 2, C, SKP])
        xb = sb("xb", [P, 2, C, SQ])
        qf, q = sb("qf", [P, NQ, C, SQ]), Split(sb, "q", [P, 2, NQ, C, SQ])
        kb = Split(sb, "kb", [P, 2, NC, KEYS])
        vb = sb("vb", [KW, 2, NTL, VW // cfg.width * cfg.stride])
        mraw = sb("mraw", [SQ, 2, SKP], mask["dtype"])
        mk = sb("mk", [SQ, 2, KEYS]) if mask["convert"] else mraw
        sm = sb("sm", [SQ, 3, KEYS])
        p = sb("p", [SQ, 3, KEYS])
        pt = sb("pt", [KW, 2, 4, NTL, SQ])
        nmx, rsum, rwide = sb("nmx", [SQ, 4]), sb("rsum", [SQ, 2, NH]), sb("rwide", [SQ, D])
        rinv = sb("rinv", [SQ, NH])
        rT = sb("rT", [P, C * SQ])
        qcols = sb("qcols", [P, NQ * (C + 1)])
        ps = lambda n: own.enter_context(nc.psum_tensor(f"{n}_{tag}", [P, 512], F32))
        ubank, sbank, tbank, obank = [ps("u0"), ps("u1")], [ps(f"s{i}") for i in range(3)], [ps("t0"), ps("t1")], ps("o")
        block = own.enter_context(nc.Block())
        SM, TE = 2 * NH, NH

        @block.sync
        def _(sp):
            for dst, name in ((wq, "wq"), (wk, "wk"), (wv, "wv")):
                sp.dma_start(dst[:, :, :], d[name]).then_inc(w_loaded, 16)

            def stage(b, i):
                sp.dma_start(cb[:, i, :, :], d["ctx"][bass.ds(b, 1), :, :, :].rearrange("a p c w -> p (a c) w")
                             ).then_inc(staged[i], 16)
                sp.dma_start(xb[:, i, :, :], m.xT[:, :, bass.ds(b * SQ, SQ)]).then_inc(staged[i], 16)
                sp.dma_start(mraw[:, i, :], mask["source"](b)).then_inc(staged[i], 16)

            for i in range(2):
                stage(i, i)
            preload(sp)
            with sp.Fori(0, ITS - 1) as it:
                for i in range(2):
                    wait_loop(sp, unit_out, it * NU + (1 + number["r", i, 0] + 1))
                    stage(it * 2 + (2 + i), i)

        @block.tensor
        def _(pe):
            pe.wait_ge(w_loaded, 48)
            with pe.Fori(0, ITS) as it:
                def unit(u):
                    kind, b, i = u
                    n = number[u]
                    pe.wait_ge(unit_out, it * NU + (1 + max(n - 1, 0)))
                    bank = ubank[n % 2]
                    if kind == "q":
                        pe.wait_ge(staged[b], it * 48 + 48)
                        for c in range(C):
                            for k in range(C):
                                mm = pe.matmul(bank[:, c * SQ:(c + 1) * SQ], wq[:, k, c * P:(c + 1) * P], xb[:, b, k, :],
                                               start=(k == 0), stop=(k == C - 1))
                    elif kind == "k":
                        for k in range(C):
                            mm = pe.matmul(bank[:, 0:SKP], wk[:, k, i * P:(i + 1) * P], cb[:, b, k, :],
                                           start=(k == 0), stop=(k == C - 1))
                        if cfg.latent:
                            for k in range(C):
                                mm = pe.matmul(bank[:, SKP:KEYS], wk[:, k, i * P:(i + 1) * P], xb[:, b, k, :],
                                               start=(k == 0), stop=(k == C - 1))
                    elif kind == "v":
                        for e, t in enumerate(v_units[i]):
                            lo, w = tiles[t]
                            for k in range(C):
                                lhs = cb[:, b, k, lo:lo + w] if t < KT else xb[:, b, k, :]
                                mm = pe.matmul(bank[0:w, e * VW:(e + 1) * VW], lhs, wv[:, k, :],
                                               start=(k == 0), stop=(k == C - 1))
                    else:
                        pe.wait_ge(spread_done, it * 2 + (b + 1))
                        for c in range(C):
                            mm = pe.transpose(bank[:, c * SQ:(c + 1) * SQ], rwide[:, c * P:(c + 1) * P],
                                              m.ident[0:SQ, 0:SQ])
                    mm.then_inc(unit_done, 1)

                def scores(n):
                    b, h = divmod(n, NH)
                    at = heads[h]
                    if h == 0:
                        pe.wait_ge(q_split, it * 2 + (b + 1))
                    if h % (NH // NC) == 0:
                        pe.wait_ge(unit_out, it * NU + (1 + number["k", b, at.k_chunk] + 1))
                    pe.wait_ge(sm_done, it * SM + (1 + max(n - 2, 0)))
                    rows = slice(at.row, at.row + 32)
                    products(pe, sbank[n % 3][0:SQ, 0:KEYS], q.at(rows, b, at.version, at.q_chunk),
                             kb.at(rows, b, at.k_chunk), True, True).then_inc(s_done, 1)

                def turn(n):
                    pe.wait_ge(exp_done, it * SM + (2 + n))
                    pe.wait_ge(t_out[n % 2], it * TE + (1 + n // 2))
                    for t, (lo, w) in enumerate(tiles):
                        mm = pe.transpose(tbank[n % 2][0:w, t * SQ:(t + 1) * SQ], p[:, n % 3, lo:lo + w],
                                          m.ident[0:SQ, 0:SQ])
                    mm.then_inc(t_done, 1)

                def weigh(four):
                    n = 4 * four
                    b, h = divmod(n, NH)
                    for i in range(2):
                        pe.wait_ge(t_out[i], it * TE + (2 + (n + 2) // 2))
                    if h == 0:
                        pe.wait_ge(unit_out, it * NU + (1 + number["v", b, len(v_units) - 1] + 1))
                        pe.wait_ge(o_out, it * 2 + (1 + b))
                    for t, (_, w) in enumerate(tiles):
                        for i in range(4):
                            at = heads[h + i]
                            mm = pe.matmul(obank[32 * i:32 * i + 32, at.out_chunk * SQ:(at.out_chunk + 1) * SQ],
                                           vb[0:w, b, t, at.value:at.value + 32], pt[0:w, four % 2, i, t, :],
                                           start=(at.first and t == 0), stop=(at.last and t == NTL - 1))
                    if h == NH - 4:
                        mm.then_inc(o_done, 1)

                for u in plan[-1]:
                    unit(u)
                for s in range(STEPS + LAG_R):
                    if s < STEPS:
                        scores(s)
                    if 0 <= s - LAG_T < STEPS:
                        turn(s - LAG_T)
                    for u in plan.get(s, []):
                        unit(u)
                    if LAG_O <= s < STEPS + LAG_O and (s - LAG_O) % 4 == 3:
                        weigh((s - LAG_O) // 4)

        def turned(eng, copy, it, n):
            wait_loop(eng, t_done, it * SM + (n + 1))
            src = tbank[n % 2][:, 0:NTL * SQ].rearrange("p (t q) -> p t q", q=SQ)
            to = pt[:, (n // 4) % 2, n % 4, :, :]
            i = copy(to[:, 0:KT, :], src[0:KW, 0:KT, :])
            if cfg.latent:
                i = copy(to[0:SQ, KT, :], src[0:SQ, KT, :])
            i.then_inc(t_out[n % 2], 1)

        @block.scalar
        def _(act):
            act.sem_inc(exp_done, 1)
            act.sem_inc(t_out[1], 1)
            with act.Fori(0, ITS) as it:
                def unit(u):
                    kind, b, i = u
                    if kind == "q":
                        wait_loop(act, unit_out, it * NU + (1 + number[u] + 1))
                        nc.scalar.copy(q.high[:, b, :, :, :], qf[:, :, :, :]).then_inc(q_high, 1)
                    if kind == "k":
                        wait_loop(act, unit_done, it * NU + (number[u] + 1))
                        nc.scalar.activation(kb.high[:, b, i, :], ubank[number[u] % 2][:, 0:KEYS], ACT.Identity,
                                             bias=col(m, bias["k"], i)).then_inc(k_high, 1)

                def exponential(n):
                    b, h = divmod(n, NH)
                    at = heads[h].position
                    wait_loop(act, sm_done, it * SM + (2 + n))
                    nc.scalar.activation(p[:, n % 3, :], sm[:, n % 3, :], ACT.Exp, scale=-1.0,
                                         bias=nmx[:, n % 4:n % 4 + 1],
                                         accum_out=rsum[:, b, at:at + 1]).then_inc(exp_done, 1)

                for u in plan[-1]:
                    unit(u)
                for s in range(STEPS + LAG_R):
                    if s < STEPS:
                        exponential(s)
                    if 0 <= s - LAG_T < STEPS and (s - LAG_T) % 2 == 1:
                        turned(act, nc.scalar.copy, it, s - LAG_T)
                    for u in plan.get(s, []):
                        unit(u)

        @block.vector
        def _(dve):
            for s in (unit_out, sm_done, t_out[0], o_out):
                dve.sem_inc(s, 1)
            for ver in range(NQ):
                lo = ver * (C + 1)
                keep = col(m, cfg.keep[ver])
                nc.vector.tensor_scalar(qcols[:, lo:lo + 1], keep, cfg.scale, None, ALU.mult).then_inc(setup_done, 1)
                nc.vector.tensor_scalar(qcols[:, lo + 1:lo + 1 + C], col(m, bias["q"], 0, C), keep, cfg.scale,
                                        ALU.mult, ALU.mult).then_inc(setup_done, 1)
            if cfg.latent:
                nc.vector.memset(mk[:, :, SKP:KEYS], 0.0).then_inc(setup_done, 1)
            else:
                nc.vector.memset(vb[:, :, :, :], 0.0).then_inc(setup_done, 1)
            dve.wait_ge(setup_done, 2 * NQ + 1)
            with dve.Fori(0, ITS) as it:
                K_PER, k_number = 2 * NC, {u: n for n, u in enumerate(u for u in order if u[0] == "k")}

                def make_mask(b):
                    dve.wait_ge(staged[b], it * 48 + 48)
                    if mask["convert"]:
                        nc.vector.tensor_scalar(mk[:, b, 0:SKP], mraw[:, b, :], 0, MASKED, ALU.is_equal, ALU.mult
                                                ).then_inc(mask_made, 1)
                        dve.wait_ge(mask_made, it * 2 + (b + 1))

                def unit(u):
                    kind, b, i = u
                    dve.wait_ge(unit_done, it * NU + (number[u] + 1))
                    bank = ubank[number[u] % 2]
                    chunks = bank[:, 0:C * SQ].rearrange("p (c q) -> p c q", q=SQ)
                    if kind == "q":
                        for ver in range(NQ):
                            lo = ver * (C + 1)
                            shift = qcols[:, lo + 1:lo + 1 + C].unsqueeze(2).broadcast_to((P, C, SQ))
                            step = nc.vector.scalar_tensor_tensor(qf[:, ver, :, :], chunks, qcols[:, lo:lo + 1], shift,
                                                                  ALU.mult, ALU.add)
                        step.then_inc(unit_out, 1)
                    elif kind == "k":
                        dve.wait_ge(k_high, it * K_PER + (k_number[u] + 1))
                        nc.vector.scalar_tensor_tensor(kb.low[:, b, i, :], bank[:, 0:KEYS], col(m, bias["k"], i),
                                                       kb.high[:, b, i, :], ALU.add, ALU.subtract
                                                       ).then_inc(unit_out, 1)
                        if i == 0:
                            dve.wait_ge(q_high, it * 2 + (b + 1))
                            nc.vector.tensor_tensor(q.low[:, b, :, :, :], qf[:, :, :, :], q.high[:, b, :, :, :],
                                                    ALU.subtract).then_inc(q_split, 1)
                    elif kind == "v":
                        own_tiles = v_units[i]
                        n = len([t for t in own_tiles if t < KT])
                        lo = own_tiles[0]
                        if n:
                            to = vb[:, b, lo:lo + n, :].rearrange("p t (g s) -> p t g s", s=cfg.stride)
                            step = nc.vector.tensor_copy(to[:, :, :, cfg.at:cfg.at + HW],
                                                         bank[0:KW, 0:n * VW].rearrange("p (t g w) -> p t g w", t=n, w=HW))
                        if KT in own_tiles:
                            e = own_tiles.index(KT)
                            step = nc.vector.tensor_copy(vb[0:SQ, b, KT, :], bank[0:SQ, e * VW:(e + 1) * VW])
                        step.then_inc(unit_out, 1)
                    else:
                        nc.vector.tensor_copy(rT[:, :], bank[:, 0:C * SQ]).then_inc(unit_out, 1)

                def mask_max(n):
                    b = n // NH
                    wait_loop(dve, s_done, it * SM + (n + 1))
                    if n >= 3:
                        wait_loop(dve, exp_done, it * SM + (2 + n - 3))
                    nc.vector.tensor_tensor_reduce(sm[:, n % 3, :], sbank[n % 3][0:SQ, 0:KEYS], mk[:, b, :], -1.0, 3.0e38,
                                                   ALU.add, ALU.min, nmx[:, n % 4:n % 4 + 1]).then_inc(sm_done, 1)

                def spread(b):
                    dve.wait_ge(exp_done, it * SM + (1 + (b + 1) * NH))
                    nc.vector.reciprocal(rinv[:, :], rsum[:, b, :]).then_inc(recip_done, 1)
                    dve.wait_ge(recip_done, it * 2 + (b + 1))
                    nc.vector.tensor_copy(rwide[:, :].rearrange("p (h w) -> p h w", w=HW),
                                          rinv[:, :].unsqueeze(2).broadcast_to((SQ, NH, HW))).then_inc(spread_done, 1)

                def divide(b):
                    dve.wait_ge(unit_out, it * NU + (1 + number["r", b, 0] + 1))
                    dve.wait_ge(o_done, it * 2 + (b + 1))
                    view = lambda t: t.rearrange("p (c q) -> p c q", q=SQ)
                    to = m.hT[:, :, bass.ds((it * 2 + b) * SQ, SQ)]
                    nc.vector.tensor_tensor(to, view(obank[:, 0:C * SQ]), view(rT[:, :]), ALU.mult).then_inc(o_out, 1)
                    dve.wait_ge(o_out, it * 2 + (b + 2))
                    shift = col(m, bias["v"], 0, C).unsqueeze(2).broadcast_to((P, C, SQ))
                    nc.vector.tensor_tensor(to, to, shift, ALU.add).then_inc(divided, 1)

                make_mask(0)
                for u in plan[-1]:
                    unit(u)
                for s in range(STEPS + LAG_R):
                    if s == NH:
                        make_mask(1)
                    if s < STEPS:
                        mask_max(s)
                    if 0 <= s - LAG_T < STEPS and (s - LAG_T) % 2 == 0:
                        turned(dve, nc.vector.tensor_copy, it, s - LAG_T)
                    if s in (NH - 1 + LAG_S, 2 * NH - 1 + LAG_S):
                        spread(0 if s < 2 * NH else 1)
                    for u in plan.get(s, []):
                        unit(u)
                    if s in (NH - 1 + LAG_R, 2 * NH - 1 + LAG_R):
                        divide(0 if s < 2 * NH else 1)
            dve.wait_ge(divided, B)


def phase_attn3(nc, m, ctx, tag, ctx_rows, ctx_loaded):
    sem = lambda n: ctx.enter_context(nc.semaphore(f"{n}_{tag}"))
    rows_loaded, s_done, t_done, c_done, ot_done = sem("rows"), sem("s"), sem("t"), sem("c"), sem("ot")
    max_done, exp_done, t_out, recip_done, c_out, ot_out, pads = (
        sem(n) for n in ("mx", "exp", "te", "rc", "ce", "oe", "pz"))
    with ExitStack() as own:
        sb = lambda n, s: own.enter_context(nc.sbuf_tensor(f"{n}_{tag}", s, F32))
        rows = sb("rows", [KW, B, KT, D])
        p, pt, on = sb("p", [SQ, 2, SKP]), sb("pt", [KW, 2, KT, SQ]), sb("on", [SQ, 2, D])
        nmx, rsum, rinv = sb("nmx", [SQ, B]), sb("rsum", [SQ, B]), sb("rinv", [SQ, B])
        bank = lambda n: [own.enter_context(nc.psum_tensor(f"{n}{i}_{tag}", [P, 512], F32)) for i in range(2)]
        sbank, tbank, cbank, obank = bank("s"), bank("t"), bank("c"), bank("o")
        block = own.enter_context(nc.Block())

        @block.sync
        def _(sp):
            sp.dma_start(rows[:, :, :, :], ctx_rows).then_inc(rows_loaded, 16)

        @block.tensor
        def _(pe):
            def scores(b):
                if b == 0:
                    pe.wait_ge(ctx_loaded, 16)
                if b >= 2:
                    pe.wait_ge(exp_done, b - 1)
                for c in range(C):
                    at = b * SKP + 1
                    mm = pe.matmul(sbank[b % 2][0:SQ, 0:SK], m.aT[:, c, b * SQ:(b + 1) * SQ], m.ctxT[:, c, at:at + SK],
                                   start=(c == 0), stop=(c == C - 1))
                mm.then_inc(s_done, 1)

            def turn(b):
                pe.wait_ge(exp_done, b + 1)
                if b >= 2:
                    pe.wait_ge(t_out, b - 1)
                for t in range(KT):
                    mm = pe.transpose(tbank[b % 2][0:KW, t * SQ:(t + 1) * SQ], p[:, b % 2, t * KW:(t + 1) * KW],
                                      m.ident[0:SQ, 0:SQ])
                mm.then_inc(t_done, 1)

            def weigh(b):
                pe.wait_ge(t_out, b + 1)
                if b == 0:
                    pe.wait_ge(rows_loaded, 16)
                if b >= 2:
                    pe.wait_ge(c_out, b - 1)
                for t in range(KT):
                    mm = pe.matmul(cbank[b % 2][0:SQ, :], pt[:, b % 2, t, :], rows[:, b, t, :],
                                   start=(t == 0), stop=(t == KT - 1))
                mm.then_inc(c_done, 1)

            def turn_out(b):
                pe.wait_ge(c_out, b + 1)
                if b >= 2:
                    pe.wait_ge(ot_out, b - 1)
                for c in range(C):
                    mm = pe.transpose(obank[b % 2][:, c * SQ:(c + 1) * SQ], on[:, b % 2, c * P:(c + 1) * P],
                                      m.ident[0:SQ, 0:SQ])
                mm.then_inc(ot_done, 1)

            for b in range(B + 3):
                if b < B:
                    scores(b)
                for stage, lag in ((turn, 1), (weigh, 2), (turn_out, 3)):
                    if 0 <= b - lag < B:
                        stage(b - lag)

        @block.scalar
        def _(act):
            act.wait_ge(pads, 1)
            for b in range(B + 3):
                if b < B:
                    act.wait_ge(max_done, b + 1)
                    if b >= 2:
                        act.wait_ge(t_done, b - 1)
                    nc.scalar.activation(p[:, b % 2, 1:1 + SK], sbank[b % 2][0:SQ, 0:SK], ACT.Exp,
                                         bias=nmx[:, b:b + 1], accum_out=rsum[:, b:b + 1]).then_inc(exp_done, 1)
                if b >= 3:
                    act.wait_ge(ot_done, b - 2)
                    nc.scalar.copy(m.hT[:, :, (b - 3) * SQ:(b - 2) * SQ],
                                   obank[(b - 3) % 2][:, 0:C * SQ].rearrange("p (c q) -> p c q", q=SQ)
                                   ).then_inc(ot_out, 1)

        @block.vector
        def _(dve):
            for b in range(B + 2):
                if b < B:
                    dve.wait_ge(s_done, b + 1)
                    nc.vector.tensor_reduce(nmx[:, b:b + 1], sbank[b % 2][0:SQ, 0:SK], AX.X, ALU.max, negate=True
                                            ).then_inc(max_done, 1)
                if 0 <= b - 1 < B:
                    n = b - 1
                    dve.wait_ge(t_done, n + 1)
                    dve.wait_ge(exp_done, n + 1)
                    nc.vector.tensor_copy(pt[:, n % 2, :, :], tbank[n % 2][0:KW, 0:KT * SQ].rearrange(
                        "p (t q) -> p t q", q=SQ)).then_inc(t_out, 1)
                    nc.vector.reciprocal(rinv[:, n:n + 1], rsum[:, n:n + 1]).then_inc(recip_done, 1)
                if 0 <= b - 2 < B:
                    n = b - 2
                    dve.wait_ge(c_done, n + 1)
                    dve.wait_ge(recip_done, n + 1)
                    nc.vector.tensor_scalar(on[:, n % 2, :], cbank[n % 2][0:SQ, :], rinv[:, n:n + 1], None, ALU.mult
                                            ).then_inc(c_out, 1)

        @block.gpsimd
        def _(pool):
            nc.gpsimd.memset(p[:, :, :], 0.0).then_inc(pads, 1)


def phase_store(nc, m, ctx, out):
    stored = ctx.enter_context(nc.semaphore("stored"))
    with nc.Block() as block:
        @block.sync
        def _(sp):
            sp.dma_start(out, m.xT[:, :, :]).then_inc(stored, 16)
            sp.wait_ge(stored, 16)


def program(nc, d, out, until=99):
    m = Machine()
    with ExitStack() as ctx:
        sb = lambda n, s: ctx.enter_context(nc.sbuf_tensor(n, s, F32))
        m.cols, m.ident, m.mean_of = sb("cols", [P, NCOL]), sb("ident", [P, P]), sb("mean_of", [P, P])
        m.xT, m.hT = sb("xT", [P, C, NT]), sb("hT", [P, C, NT])
        sem = lambda n: ctx.enter_context(nc.semaphore(n))
        ctx_loaded = sem("ctx_loaded")
        m.norm_marks = [Mark(sem("norm_" + n)) for n in
                        ("mean", "centre", "square", "var", "deviation", "rstd", "scaled", "affine", "bias")]
        m.dense_marks = [Mark(sem("dense_" + n)) for n in ("product", "stored")]
        m.dense_weights = {}
        m.mlp_marks = [Mark(sem("mlp_" + n)) for n in
                       ("up", "act", "down", "added", "bias", "loaded", "w_high", "w_split", "g_high", "g_split")]

        def first_group(pack):
            return lambda sp: sp.dma_start(m.wraw[:, :], pack[0]).then_inc(m.mlp_marks[5].sem, 16)

        def dense_weights(*names):
            for n in names:
                m.dense_weights[n] = (sb("w_" + n, [P, C, D]), sem("loaded_" + n))

            def load(sp):
                for n in names:
                    to, ready = m.dense_weights[n]
                    sp.dma_start(to[:, :, :], d[n[:2] + "_w" + n[2:]]).then_inc(ready, 16)
            return load

        phase_load(nc, m, ctx, d)
        for a in ("1", "2"):
            with ExitStack() as raw:
                inputs = AttentionInputs(nc, ctx, raw, a, d["w_a" + a], d["rows" + a], d["ctxB"])
                phase_norm(nc, m, ctx, "n" + a, m.xT, m.hT, "eps5", "ln_s" + a, "ln_o" + a, after_bias="bo" + a,
                           preload=inputs.load_first)
                phase_attn0(nc, m, ctx, inputs)
            if until == int(a):
                break
        with nc.sbuf_tensor("wraw0", [P, WROW], F32) as m.wraw:
            if until >= 3:
                phase_norm(nc, m, ctx, "nm", m.xT, m.hT, "eps5", "ln_sm", "ln_om", preload=first_group(d["w_m0"]))
                phase_mlp(nc, m, ctx, "m0", d["w_m0"], ACT.Gelu, "fc1", "fc2")
        m.aT = sb("aT", [P, C, NT])

        def with_residual(bias_name):
            def evacuate(dst, bank, c, half):
                return nc.vector.scalar_tensor_tensor(dst, bank, col(m, bias_name, c), m.xT[:, c, half], ALU.add, ALU.add)
            return evacuate

        if until >= 4:
            phase_small(nc, m, ctx, "l1", Small(16, 32, C, True, 1.0 / 32, ("one",), 32, 0, wide_head),
                        {"wq": d["l1_wq"], "wk": d["l1_wk"], "wv": d["l1_wv"], "ctx": d["ctxB"]},
                        {"dtype": I32, "convert": True,
                         "source": lambda b: d["mask1"][bass.ds(b, 1), :].broadcast_to((SQ, SKP))},
                        {"q": "l1_q", "k": "l1_k", "v": "l1_v"}, dense_weights("l1o"))
            phase_dense(nc, m, ctx, "l1o", m.hT, m.aT, with_residual("l1_o"))
            with nc.sbuf_tensor("wraw1", [P, WROW], F32) as m.wraw:
                phase_norm(nc, m, ctx, "l1n", m.aT, m.hT, "eps6", "l1_post", None, centred=False,
                           preload=first_group(d["w_m1"]))
                phase_mlp(nc, m, ctx, "m1", d["w_m1"], ACT.Gelu_apprx_tanh, "l1_m1", "l1_m2")
        if until >= 5:
            phase_small(nc, m, ctx, "l2", Small(32, 16, 1, False, 0.25, ("even", "odd"), 48, 16, narrow_head),
                        {"wq": d["l2_wq"], "wk": d["l2_wk"], "wv": d["l2_wv"], "ctx": d["ctxB"]},
                        {"dtype": F32, "convert": False,
                         "source": lambda b: d["mask2"][bass.ds(b, 1), :, :].rearrange("a q k -> q (a k)")},
                        {"q": "l2_q", "k": "l2_k", "v": "l2_v"}, dense_weights("l2o"))
            load_l3 = dense_weights("l3q", "l3k", "l3v", "l3o")
            m.ctxT = sb("ctxT3", [P, C, B * SKP])
            phase_dense(nc, m, ctx, "l2o", m.hT, m.aT, with_residual("l2_o"),
                        preload=lambda sp: (load_l3(sp),
                                            sp.dma_start(m.ctxT[:, :, :], d["ctxT"]).then_inc(ctx_loaded, 16)))
            phase_norm(nc, m, ctx, "l2n", m.aT, m.xT, "eps6", "gamma", "beta")
        if until >= 6:
            scale = float(D) ** -0.5
            phase_dense(nc, m, ctx, "l3q", m.xT, m.hT,
                        lambda dst, bank, c, half: nc.vector.tensor_scalar(dst, bank, scale, None, ALU.mult))
            plain = lambda dst, bank, c, half: nc.vector.tensor_copy(dst, bank)
            phase_dense(nc, m, ctx, "l3k", m.hT, m.aT, plain)
            phase_attn3(nc, m, ctx, "l3", d["ctxR"], ctx_loaded)
            phase_dense(nc, m, ctx, "l3v", m.hT, m.aT, plain)
            phase_dense(nc, m, ctx, "l3o", m.aT, m.xT,
                        lambda dst, bank, c, half: nc.vector.scalar_tensor_tensor(dst, bank, col(m, "alpha"), dst,
                                                                                  ALU.mult, ALU.add))
        phase_store(nc, m, ctx, out)


def _columns(vectors):
    import numpy as np
    return np.concatenate([np.asarray(v).reshape(-1, P).T for v in vectors], axis=1)


def _features_first(a, np):
    return np.ascontiguousarray(a.reshape(-1, P, a.shape[-1]).transpose(1, 0, 2))


def _pack_attention(wq, wk, wv, wo, np):
    per_group = lambda w: w.reshape(C, P, NG, GW).transpose(2, 1, 0, 3).reshape(NG, P, C * GW)
    out = wo.reshape(NG, HG, P, D).transpose(0, 2, 1, 3).reshape(NG, P, HG * D)
    return np.ascontiguousarray(np.concatenate([per_group(wq), per_group(wk), per_group(wv), out], axis=2))


def _pack_mlp(w1, w2, np):
    up = w1.reshape(C, P, NFG, FG * P).transpose(2, 1, 0, 3).reshape(NFG, P, C * FG * P)
    down = w2.reshape(NFG, FG, P, D).transpose(0, 2, 1, 3).reshape(NFG, P, FG * D)
    return np.ascontiguousarray(np.concatenate([up, down], axis=2))


def _layout_inputs(i):
    import numpy as np
    f = lambda n: np.asarray(i[n])
    x, ctx = f("x"), f("ctx_2048")
    a = {}
    a["x"] = _features_first(x.reshape(NT, D).T, np)
    padded = np.zeros((B, SKP, D), x.dtype)
    padded[:, 1:1 + SK] = ctx
    a["ctxT"] = _features_first(padded.reshape(B * SKP, D).T, np)
    a["ctxB"] = np.ascontiguousarray(a["ctxT"].reshape(P, C, B, SKP).transpose(2, 0, 1, 3))
    a["ctxR"] = np.ascontiguousarray(padded.reshape(B, KT, KW, D).transpose(2, 0, 1, 3))
    mask1 = np.zeros((B, SKP), f("mask_BxS2_ik0").dtype)
    mask1[:, 1:1 + SK] = f("mask_BxS2_ik0")
    a["mask1"] = mask1
    mask2 = np.full((B, SQ, SKP), MASKED, x.dtype)
    mask2[:, :, 1:1 + SK] = f("mask_Bx1xSxS2_ff0")[:, 0]
    a["mask2"] = mask2
    vectors = []
    for n in ("1", "2"):
        g = lambda k: f("L0_xattn_" + k + n)
        a["w_a" + n] = _pack_attention(g("wq"), g("wk"), g("wv"), g("wo"), np)
        a["rows" + n] = np.ascontiguousarray(
            np.concatenate([g("bias_v").reshape(NG, GW), g("bv").reshape(NG, GW)], axis=1))
        vectors += [f(f"L0_xattn_ln{n}_scale"), f(f"L0_xattn_ln{n}_offset"), g("bq"), g("bk"), g("bv"), g("bias_k"),
                    g("bo")]
    vectors += [f("L0_xattn_ln_mlp_scale"), f("L0_xattn_ln_mlp_offset"), f("L0_xattn_b_fc1"), f("L0_xattn_b_fc2")]
    a["w_m0"] = _pack_mlp(f("L0_xattn_w_fc1"), f("L0_xattn_w_fc2"), np)
    a["w_m1"] = _pack_mlp(f("L1_xattn_mlp_w1"), f("L1_xattn_mlp_w2"), np)
    kv, kvb = f("L1_xattn_kv_w").reshape(D, D, 2), f("L1_xattn_kv_b").reshape(D, 2)
    a["l1_wq"] = _features_first(f("L1_xattn_q_w"), np)
    a["l1_wk"] = _features_first(kv[:, :, 0], np)
    a["l1_wv"] = _features_first(kv[:, :, 1], np)
    a["l1_wo"] = _features_first(f("L1_xattn_out_w"), np)
    vectors += [f("L1_xattn_q_b"), kvb[:, 0], kvb[:, 1], f("L1_xattn_out_b"), f("L1_xattn_postnorm_w"),
                f("L1_xattn_mlp_b1"), f("L1_xattn_mlp_b2")]
    order = lambda w: w.reshape(-1, 8, 4, 16).transpose(0, 2, 1, 3).reshape(-1, D)
    a["l2_wq"] = _features_first(order(f("L2_xattn_Wq")), np)
    a["l2_wk"] = _features_first(f("L2_xattn_Wk"), np)
    a["l2_wv"] = _features_first(f("L2_xattn_Wv"), np)
    outputs = lambda w: np.ascontiguousarray(w.reshape(4, 4, 2, 16, -1).transpose(1, 0, 2, 3, 4).reshape(D, -1))
    a["l2_wo"] = _features_first(outputs(f("L2_xattn_Wo")), np)
    bv = outputs(np.broadcast_to(f("L2_xattn_bv").reshape(8, 1, 16), (8, 4, 16)).reshape(D)).reshape(D)
    vectors += [order(f("L2_xattn_bq").reshape(1, D)).reshape(D), f("L2_xattn_bk"), bv, f("L2_xattn_bo"),
                f("L2_xattn_gamma"), f("L2_xattn_beta")]
    a["l3_wq"] = _features_first(f("L3_xattn_w_q").T, np)
    a["l3_wk"] = _features_first(f("L3_xattn_w_k"), np)
    a["l3_wv"] = _features_first(f("L3_xattn_w_v").T, np)
    a["l3_wo"] = _features_first(f("L3_xattn_w_o").T, np)
    even = np.zeros((P,), x.dtype)
    even.reshape(4, 2, 16)[:, 0] = 1
    odd = np.zeros((P,), x.dtype)
    odd.reshape(4, 2, 16)[:, 1] = 1
    vectors += [np.full((P,), f("L3_xattn_alpha"), x.dtype), even, odd, np.ones((P,), x.dtype),
                np.full((P,), 1e-5, x.dtype), np.full((P,), 1e-6, x.dtype)]
    a["cols"] = np.ascontiguousarray(_columns(vectors))
    return a


UNTIL = 99


def kernel(**inputs):
    import concourse.bacc as _bacc
    import numpy as _np
    from concourse.bass_utils import run_bass_kernel_spmd as _run

    nc = _bacc.Bacc("TRN2", target_bir_lowering=False, num_devices=1)
    arrays = _layout_inputs(inputs)
    dram = {n: nc.dram_tensor(f"in_{n}", a.shape, mybir.dt.from_np(a.dtype), kind="ExternalInput").ap()
            for n, a in arrays.items()}
    out = nc.dram_tensor("out", (P, C, NT), F32, kind="ExternalOutput").ap()
    program(nc, dram, out, UNTIL)
    r = _run(nc, [{f"in_{n}": a for n, a in arrays.items()}], core_ids=[0])
    y = r.results[0]["out"]
    return _np.ascontiguousarray(y.transpose(1, 0, 2).reshape(D, NT).T.reshape(B, SQ, D))
```
